# Optimizing a Trainium2 kernel written in Bass

```python
import numpy as np
import jax
import jax.numpy as jnp

def _softmax(x, axis=-1):
    return jax.nn.softmax(x, axis=axis)

def _gelu(x):
    return jax.nn.gelu(x, approximate=True)

def _silu(x):
    return jax.nn.silu(x)

def _sigmoid(x):
    return jax.nn.sigmoid(x)

def _layernorm(x, axis=-1, eps=1e-05):
    m = jnp.mean(x, axis=axis, keepdims=True)
    v = jnp.var(x, axis=axis, keepdims=True)
    return (x - m) / jnp.sqrt(v + eps)

def _scatter_add(tgt, idx, src, axis=0):
    return tgt.at[idx].add(src)

def _segment_sum(src, seg, n):
    return jax.ops.segment_sum(src, seg, n)
kernel_name = 'mk_gps_d1_gnn_r8_4f7cbd'

def setup_inputs(seed: int=0):
    np.random.seed(seed)
    _w = jnp.asarray

    def _rec_inputs():
        import jax
        import jax.numpy as jnp
        _gk = jax.random.key(seed)
        x = -8.776e-05 + 1 * jax.random.normal(jax.random.fold_in(_gk, 1), (6250, 256), jnp.float32)
        src = jax.random.randint(jax.random.fold_in(_gk, 2), (100000,), 0, 6250, jnp.int32)
        dst = jax.random.randint(jax.random.fold_in(_gk, 3), (100000,), 0, 6250, jnp.int32)
        _o = jnp.argsort(dst, stable=True)
        src = src[_o]
        dst = dst[_o]
        edge_type_16 = jax.random.randint(jax.random.fold_in(_gk, 12), (100000,), 0, 16, jnp.int32)
        edge_weight1 = jax.random.uniform(jax.random.fold_in(_gk, 13), (100000, 1), jnp.float32, 0.0, 0.999998)
        return (x, src, dst, edge_type_16, edge_weight1)
    x, src, dst, edge_type_16, edge_weight1 = _rec_inputs()

    def _L0_gnn_setup():
        import jax, jax.numpy as jnp
        import numpy as np
        N_NODES = 2500
        N_EDGES = 40000
        NUM_RELS = 16
        IN_FEAT = 256
        OUT_FEAT = 256
        key = jax.random.key(seed)
        k_h, k_w, k_n, k_s, k_d, k_r = jax.random.split(key, 6)
        h = jax.random.normal(k_h, (N_NODES, IN_FEAT), dtype=jnp.float32)
        weight = jax.random.normal(k_w, (NUM_RELS, IN_FEAT, OUT_FEAT), dtype=jnp.float32)
        norm = jax.random.uniform(k_n, (N_EDGES, 1), dtype=jnp.float32)
        src = jax.random.randint(k_s, (N_EDGES,), 0, N_NODES, dtype=jnp.int32)
        dst = jax.random.randint(k_d, (N_EDGES,), 0, N_NODES, dtype=jnp.int32)
        rel_type = jax.random.randint(k_r, (N_EDGES,), 0, NUM_RELS, dtype=jnp.int32)
        return {'h': h, 'weight': weight, 'norm': norm, 'src': src, 'dst': dst, 'rel_type': rel_type}
    _L0_gnn_all = _L0_gnn_setup()
    _L0_gnn_in = {k: v for k, v in _L0_gnn_all.items() if k in ('weight',)}
    del _L0_gnn_all

    def _L0_mix_setup():
        import jax, jax.numpy as jnp
        import numpy as np
        B, N, C, H = (8, 2048, 256, 8)
        D = C // H
        GH = C // 4
        key = jax.random.key(seed)
        ks = jax.random.split(key, 6)
        s = 0.02
        return {'x': jax.random.normal(ks[0], (B, N, C), dtype=jnp.float32), 'Wqkv': jax.random.normal(ks[1], (C, 3 * C), dtype=jnp.float32) * s, 'Wproj': jax.random.normal(ks[2], (C, C), dtype=jnp.float32) * s, 'bproj': jnp.zeros((C,), dtype=jnp.float32), 'ln_g': jnp.ones((C,), dtype=jnp.float32), 'ln_b': jnp.zeros((C,), dtype=jnp.float32), 'Wg1': jax.random.normal(ks[3], (C, GH), dtype=jnp.float32) * s, 'bg1': jnp.zeros((GH,), dtype=jnp.float32), 'Wg2': jax.random.normal(ks[4], (GH, C), dtype=jnp.float32) * s, 'bg2': jnp.zeros((C,), dtype=jnp.float32)}
    _L0_mix_all = _L0_mix_setup()
    _L0_mix_in = {k: v for k, v in _L0_mix_all.items() if k in ('Wqkv', 'Wproj', 'bproj', 'ln_g', 'ln_b', 'Wg1', 'bg1', 'Wg2', 'bg2')}
    del _L0_mix_all

    def _L0_ffn_setup():
        import jax, jax.numpy as jnp
        import numpy as np
        NUM_EXPERTS = 8
        TOP_K = 2
        B, S, D = (8, 1024, 256)

        def _moe(tokens, router_w, w1, b1, w2, b2):
            N = tokens.shape[0]
            E = router_w.shape[0]
            logits = tokens.astype(jnp.float32) @ router_w.astype(jnp.float32).T
            probs = jax.nn.softmax(logits, axis=-1)
            rw, re = jax.lax.top_k(probs, TOP_K)
            if TOP_K > 1:
                rw = rw / jnp.maximum(rw.sum(-1, keepdims=True), 1e-12)
            rw = rw.astype(tokens.dtype)
            combine = jnp.zeros((N, E), tokens.dtype).at[jnp.arange(N)[:, None], re].set(rw)
            out = tokens
            for e in range(E):
                h = jax.nn.gelu(tokens @ w1[e] + b1[e], approximate=False)
                y = h @ w2[e] + b2[e]
                out = out + combine[:, e:e + 1] * y
            return out
        key = jax.random.key(seed)
        ks = jax.random.split(key, 4)
        scale = 1.0 / np.sqrt(D).astype(np.float32)
        return {'input_embeddings': jax.random.normal(ks[0], (B, S, D), jnp.float32), 'router_w': jax.random.normal(ks[1], (NUM_EXPERTS, D), jnp.float32) * scale, 'w1': jax.random.normal(ks[2], (NUM_EXPERTS, D, D), jnp.float32) * scale, 'b1': jnp.zeros((NUM_EXPERTS, D), jnp.float32), 'w2': jax.random.normal(ks[3], (NUM_EXPERTS, D, D), jnp.float32) * scale, 'b2': jnp.zeros((NUM_EXPERTS, D), jnp.float32)}
    _L0_ffn_all = _L0_ffn_setup()
    _L0_ffn_in = {k: v for k, v in _L0_ffn_all.items() if k in ('router_w', 'w1', 'b1', 'w2', 'b2')}
    del _L0_ffn_all
    return {'x': x, 'src': src, 'dst': dst, 'edge_type_16': edge_type_16, 'edge_weight1': edge_weight1, 'L0_gnn_weight': _L0_gnn_in['weight'], 'L0_mix_Wqkv': _L0_mix_in['Wqkv'], 'L0_mix_Wproj': _L0_mix_in['Wproj'], 'L0_mix_bproj': _L0_mix_in['bproj'], 'L0_mix_ln_g': _L0_mix_in['ln_g'], 'L0_mix_ln_b': _L0_mix_in['ln_b'], 'L0_mix_Wg1': _L0_mix_in['Wg1'], 'L0_mix_bg1': _L0_mix_in['bg1'], 'L0_mix_Wg2': _L0_mix_in['Wg2'], 'L0_mix_bg2': _L0_mix_in['bg2'], 'L0_ffn_router_w': _L0_ffn_in['router_w'], 'L0_ffn_w1': _L0_ffn_in['w1'], 'L0_ffn_b1': _L0_ffn_in['b1'], 'L0_ffn_w2': _L0_ffn_in['w2'], 'L0_ffn_b2': _L0_ffn_in['b2']}

def reference(x, src, dst, edge_type_16, edge_weight1, L0_gnn_weight, L0_mix_Wqkv, L0_mix_Wproj, L0_mix_bproj, L0_mix_ln_g, L0_mix_ln_b, L0_mix_Wg1, L0_mix_bg1, L0_mix_Wg2, L0_mix_bg2, L0_ffn_router_w, L0_ffn_w1, L0_ffn_b1, L0_ffn_w2, L0_ffn_b2):
    import jax
    import jax.numpy as jnp

    def _L0_gnn_ref(h, weight, norm, src, dst, rel_type):
        import jax, jax.numpy as jnp
        import numpy as np
        N_NODES = 2500
        N_EDGES = 40000
        NUM_RELS = 16
        IN_FEAT = 256
        OUT_FEAT = 256
        transformed = jnp.einsum('ni,rio->rno', h, weight)
        msg = transformed[rel_type, src] * norm
        out = jax.ops.segment_sum(msg, dst, num_segments=h.shape[0])
        return out

    def _L0_mix_ref(x, Wqkv, Wproj, bproj, ln_g, ln_b, Wg1, bg1, Wg2, bg2):
        import jax, jax.numpy as jnp
        import numpy as np
        B, N, C, H = (8, 2048, 256, 8)
        D = C // H
        GH = C // 4
        b, n, c = x.shape
        h, d = (H, D)
        qkv = (x @ Wqkv).reshape(b, n, 3, h, d)
        q, k, v = (qkv[:, :, 0], qkv[:, :, 1], qkv[:, :, 2])
        k = jax.nn.softmax(k, axis=1)
        context = jnp.einsum('bnhd,bnhv->bhdv', k, v)
        out = jnp.einsum('bnhd,bhdv->bnhv', q, context).reshape(b, n, c)
        mu = jnp.mean(x, axis=-1, keepdims=True)
        var = jnp.var(x, axis=-1, keepdims=True)
        xn = (x - mu) * jax.lax.rsqrt(var + 1e-05) * ln_g + ln_b
        hgate = jax.nn.gelu(xn @ Wg1 + bg1, approximate=False)
        gate = jax.nn.sigmoid(hgate @ Wg2 + bg2)
        return out * gate @ Wproj + bproj

    def _L0_ffn_ref(input_embeddings, router_w, w1, b1, w2, b2):
        import jax, jax.numpy as jnp
        import numpy as np
        NUM_EXPERTS = 8
        TOP_K = 2
        B, S, D = (8, 1024, 256)

        def _moe(tokens, router_w, w1, b1, w2, b2):
            N = tokens.shape[0]
            E = router_w.shape[0]
            logits = tokens.astype(jnp.float32) @ router_w.astype(jnp.float32).T
            probs = jax.nn.softmax(logits, axis=-1)
            rw, re = jax.lax.top_k(probs, TOP_K)
            if TOP_K > 1:
                rw = rw / jnp.maximum(rw.sum(-1, keepdims=True), 1e-12)
            rw = rw.astype(tokens.dtype)
            combine = jnp.zeros((N, E), tokens.dtype).at[jnp.arange(N)[:, None], re].set(rw)
            out = tokens
            for e in range(E):
                h = jax.nn.gelu(tokens @ w1[e] + b1[e], approximate=False)
                y = h @ w2[e] + b2[e]
                out = out + combine[:, e:e + 1] * y
            return out
        b, s, d = input_embeddings.shape
        tokens = input_embeddings.reshape(b * s, d)
        return _moe(tokens, router_w, w1, b1, w2, b2).reshape(b, s, d)
    xn = _layernorm(x, axis=-1)
    x = x + _L0_gnn_ref(xn, L0_gnn_weight, edge_weight1, src, dst, edge_type_16) + _L0_mix_ref(xn[None], L0_mix_Wqkv, L0_mix_Wproj, L0_mix_bproj, L0_mix_ln_g, L0_mix_ln_b, L0_mix_Wg1, L0_mix_bg1, L0_mix_Wg2, L0_mix_bg2)[0]
    x = x + _L0_ffn_ref(_layernorm(x, axis=-1)[None], L0_ffn_router_w, L0_ffn_w1, L0_ffn_b1, L0_ffn_w2, L0_ffn_b2)[0]
    return x

_drawn_inputs = setup_inputs


def setup_inputs(seed=0):
    import zlib

    import numpy as np

    out = dict(_drawn_inputs(seed))
    spreads = {'L0_mix_bproj': (0.0, 0.8),
     'L0_mix_ln_g': (1.0, 0.6),
     'L0_mix_ln_b': (0.0, 0.8),
     'L0_mix_bg1': (0.0, 0.8),
     'L0_mix_bg2': (0.0, 0.8),
     'L0_ffn_b1': (0.0, 0.8),
     'L0_ffn_b2': (0.0, 2.0)}
    factors = {'L0_mix_Wqkv': 8.0,
     'L0_mix_Wproj': 8.0,
     'L0_mix_Wg1': 8.0,
     'L0_mix_Wg2': 8.0,
     'L0_ffn_router_w': 4.879,
     'L0_ffn_w1': 4.852,
     'L0_ffn_w2': 4.367}
    for name, (base, spread) in spreads.items():
        noise = np.random.default_rng([zlib.crc32(name.encode()), seed]).standard_normal(out[name].shape)
        drawn = base * np.exp(spread * noise) if base else spread * noise
        out[name] = jnp.asarray(drawn.astype(out[name].dtype))
    for name, factor in factors.items():
        out[name] = (out[name] * factor).astype(out[name].dtype)
    return out
```

```python
from contextlib import ExitStack

import concourse.bass as bass
from concourse import mybir

ALU = mybir.AluOpType
ACT = mybir.ActivationFunctionType
AX = mybir.AxisListType
F32 = mybir.dt.float32
F32R = mybir.dt.float32r
I32 = mybir.dt.int32
U32 = mybir.dt.uint32

P = 128
EPS = 1e-5
HI, LO = 0, 1
PASSES = ((HI, HI), (LO, HI), (HI, LO))


class Tally:

    def __init__(self, sem):
        self.sem, self.n = sem, 0

    def inc(self, instruction):
        instruction.then_inc(self.sem, 1)
        self.n = self.n + 1

    def link(self, eng, instruction):
        self.inc(instruction)
        eng.wait_ge(self.sem, self.n)


def gps_layer(nc, x, src, dst, rel, norm, Wr, Wqkv, Wproj, bproj, ln_g, ln_b, Wg1, bg1, Wg2, bg2,
              router_w, w1, b1, w2, b2, out):
    N, C = x.shape
    E = src.shape[0]
    R = Wr.shape[0]
    X = router_w.shape[0]
    G = Wg1.shape[1]
    NT = -(-N // P)
    TAIL = N - (NT - 1) * P
    NP = NT // 2
    CC = C // P
    HEAD = C // 8
    NB = P // HEAD
    EPT = 16
    SUP = 4
    WIN = P
    STEP = 32
    SHIFT = 2
    ET = NT * EPT
    ER = 112
    EB = ET // ER
    PAD_DST = -100000
    VW = P + 1
    KVW = C + CC * VW
    WC = 4
    AHEAD = 2 * X
    FAR = 1 << 19
    SLOTS = 7
    RING = 16
    assert N * 16 == E and NT == 2 * NP + 1 and ET == EB * ER and NT % SLOTS == 0 and CC == 2

    table = nc.dram_tensor("table", [NT * P * R, C], F32).ap()
    kv_d = nc.dram_tensor("kv_d", [NT, P, KVW], F32).ap()
    xt_d = nc.dram_tensor("xt_d", [NT, P, 2 * C], F32).ap()
    hg_d = nc.dram_tensor("hg_d", [NT, G, P], F32).ap()
    dsl_d = nc.dram_tensor("dsl_d", [P, ET], F32).ap()
    gnn_d = nc.dram_tensor("gnn_d", [NT * P, C], F32).ap()

    ctx = ExitStack()
    with ctx:
        def sb(name, shape, dt, where=ctx):
            return where.enter_context(nc.sbuf_tensor(name, shape, dt))

        def sem(name):
            return ctx.enter_context(nc.semaphore(name))

        xres = sb("xres", [P, NT, C], F32)
        wreg = sb("wreg", [P, 2, 4, CC, WC, C], F32R)
        raw = sb("raw", [P, 2, CC * WC * C], F32)
        stg = sb("stg", [P, RING, C], F32)
        wproj = sb("wproj", [P, 2, CC, C], F32R)
        wqc = sb("wqc", [P, 2, CC, C], F32R)
        gidx = sb("gidx", [P, ET], I32)
        dpr = sb("dpr", [P, ET], F32)
        nrm = sb("nrm", [P, ET], F32)
        ident = sb("ident", [P, P], F32)
        ones = sb("ones", [P, P], F32)
        dbl = sb("dbl", [P, 2 * P], F32)
        kmax = sb("kmax", [P, C], F32)
        kmb = sb("kmb", [P, C], F32)
        wg2 = sb("wg2", [G, C], F32)
        cols = sb("cols", [P, 32], F32)
        rwt = sb("rwt", [P, CC, X], F32)
        b2s = sb("b2s", [X, C], F32)
        iota8 = sb("iota8", [P, X], F32)
        small = sb("small", [P, 160], F32)
        smallu = sb("smallu", [P, 2, X], U32)
        flag = sb("flag", [1, 1], I32)
        wqt = sb("wqt", [P, CC, C], F32)

        with ExitStack() as one:
            wkv_raw = sb("wkv_raw", [P, CC, 2 * C], F32, one)
            wq_raw = sb("wq_raw", [P, CC, C], F32, one)
            wp_raw = sb("wp_raw", [P, CC, C], F32, one)
            wg1_raw = sb("wg1_raw", [P, CC, G], F32, one)
            wg1_f = sb("wg1_f", [P, CC, G], F32, one)
            wkvg = sb("wkvg", [P, 2, CC, 2 * C + G], F32R, one)
            xt = [sb(f"xt{b}", [P, 2, CC, P], F32R, one) for b in range(2)]
            xn = [sb(f"xn{b}", [P, C], F32, one) for b in range(2)]
            kvs = [sb(f"kvs{b}", [P, KVW], F32, one) for b in range(2)]
            hgn = sb("hgn", [P, 2, G], F32, one)
            hgt = [sb(f"hgt{b}", [G, P], F32, one) for b in range(2)]
            erow = sb("erow", [ER, 2, EB * P], F32, one)
            vrow = sb("vrow", [24, P], F32, one)
            rwr = sb("rwr", [X, C], F32, one)
            bpb = sb("bpb", [P, C], F32, one)
            g1b = sb("g1b", [P, G], F32, one)
            lnbb = sb("lnbb", [P, CC, P], F32, one)
        two = ctx.enter_context(ExitStack())
        ctxbd = sb("ctxbd", [P, CC, P], F32, two)
        dg = sb("dg", [P, C], F32, two)
        mh = sb("mh", [P, 8, C], F32R, two)
        ml = sb("ml", [P, 8, C], F32R, two)
        sel = sb("sel", [P, 8, P], F32R, two)
        tt = sb("tt", [P, 2, CC, 2 * P], F32R, two)
        xtp = sb("xtp", [P, 2, 2 * C], F32R, two)
        hgp = sb("hgp", [G, 2, P], F32, two)
        ht = [sb(f"ht{b}", [P, 2, CC, 2 * P], F32R, two) for b in range(2)]
        idxcur = sb("idxcur", [P, 2 * EPT], I32, two)

        bank = [ctx.enter_context(nc.psum_tensor(f"bank{b}", [P, 512], F32)) for b in range(8)]

        erow_i = stg[:].rearrange("p a c -> p (a c)")[0:ER, 0:4 * EB * P].rearrange(
            "p (a b) -> p a b", a=4)
        src_r, rel_r, dst_r = (erow_i[:, a, :].bitcast(I32) for a in range(3))
        norm_r = erow_i[:, 3, :]
        lo_i = raw[:, 1, 0:ET].bitcast(I32)
        mask = raw[:, 1, ET:2 * ET]
        dsl = raw[:, 0, 2 * P:2 * P + ET]
        stage = stg[:].rearrange("p (h j) c -> p h (j c)", h=2)
        slot = raw[:].rearrange("p a b -> p (a b)")[:, 0:SLOTS * KVW].rearrange(
            "p (s w) -> p s w", s=SLOTS)
        rs = raw[:].rearrange("p a b -> p (a b)")
        gate = rs[:, 0:512]
        ogf = rs[:, 512:1024]
        tn = rs[:, 1024:1536].rearrange("p (a c) -> p a c", a=2)
        acc = rs[:, 1536:2048].rearrange("p (a c) -> p a c", a=2)
        hf = [rs[:, 2048 + 512 * b:2560 + 512 * b] for b in range(2)]
        comb = rs[:, 3072:3072 + 2 * X].rearrange("p (a e) -> p a e", a=2)
        lg = rs[:, 3088:3088 + 2 * X].rearrange("p (a e) -> p a e", a=2)
        top = rs[:, 3104:3104 + 2 * X].rearrange("p (a e) -> p a e", a=2)
        idf = rs[:, 3120:3120 + 2 * X].rearrange("p (a e) -> p a e", a=2)
        cb2 = rs[:, 3136:3136 + 2 * X].rearrange("p (a e) -> p a e", a=2)
        ct = rs[0:X, 3200:3456]
        f_dsl, f_low, f_turn, f_same = rs[:, 0:ET], rs[:, 800:928], rs[:, 928:1056], rs[:, 1056:1184]
        f_dup = rs[:, 1184:1185]
        f_i = rs[:, 1188:1191].bitcast(I32)
        og = xtp[:].rearrange("p a b -> p (a b)").rearrange("p (h c n) -> p h c n", h=2, c=CC)
        b1c = cols[:, 0:2 * X]
        gcol, bcol, bg2c = cols[:, 16:18], cols[:, 18:20], cols[:, 20:22]
        bg2h = small[:, 0:2]
        s2 = small[:, 2:4]
        stats = small[:, 4:16].rearrange("p (a b) -> p a b", a=2)
        mv = small[:, 16:20].rearrange("p (a b) -> p a b", a=2)
        rstd = small[:, 20:22]
        kcol = small[:, 22:24]
        rden = small[:, 24:26]
        cnt = small[:, 26:27]
        dlt = small[:, 28:30]
        th = small[:, 30:32]
        wa = small[:, 32:34]
        wb = small[:, 34:36]
        ve = small[:, 36:38]
        half = small[:, 38:40]
        bg1r = small[0:1, 64:64 + G]

        eng_names = [nc.vector.engine, nc.tensor.engine, nc.gpsimd.engine]
        waited = [sem(f"waited{n}") for n in range(3)]
        consts = sem("consts")
        cleared = sem("cleared")
        edges_in = sem("edges_in")
        vec_in = sem("vec_in")
        mixw_in = sem("mixw_in")
        raw_in = [sem(f"raw_in{b}") for b in range(2)]
        x_in = sem("x_in")
        bp_in = sem("bp_in")
        setup_pe = sem("setup_pe")
        setup_act = sem("setup_act")
        dve_chain = sem("dve_chain")
        w_hi = sem("w_hi")
        w_lo = sem("w_lo")
        xn_ready = sem("xn_ready")
        bias_in = sem("bias_in")
        xt_psum = sem("xt_psum")
        xt_hi = sem("xt_hi")
        xt_lo = sem("xt_lo")
        kv_mm = sem("kv_mm")
        kv_cp = sem("kv_cp")
        kmax_up = sem("kmax_up")
        hg_mm = sem("hg_mm")
        var_ready = sem("var_ready")
        rstd_ready = sem("rstd_ready")
        s2_ready = sem("s2_ready")
        pool_chain = sem("pool_chain")
        var2_ready = sem("var2_ready")
        rstd2_ready = sem("rstd2_ready")
        hg_pre = sem("hg_pre")
        hg_act = sem("hg_act")
        hgt_psum = sem("hgt_psum")
        hgt_cp = sem("hgt_cp")
        gnn_mm = sem("gnn_mm")
        tbl_act = sem("tbl_act")
        tbl_dve = sem("tbl_dve")
        tbl_st = [sem(f"tbl_st{h}") for h in range(2)]
        kv_st = [sem(f"kv_st{b}") for b in range(2)]
        xt_st = [sem(f"xt_st{b}") for b in range(2)]
        hg_st = [sem(f"hg_st{b}") for b in range(2)]
        kv_in = [sem(f"kv_in{s}") for s in range(SLOTS)]
        k_shift = sem("k_shift")
        k_exp = sem("k_exp")
        ctx_mm = sem("ctx_mm")
        idx_cur = sem("idx_cur")
        gath = [sem(f"gath{g}") for g in range(4)]
        msg_hi = sem("msg_hi")
        msg_lo = sem("msg_lo")
        sel_done = sem("sel_done")
        edge_mm = sem("edge_mm")
        edge_add = sem("edge_add")
        xtp_in = sem("xtp_in")
        mix_pe = sem("mix_pe")
        mix_act = sem("mix_act")
        mix_dve = sem("mix_dve")
        h_mm = sem("h_mm")
        h_act = sem("h_act")
        h_hi = sem("h_hi")
        h_lo = sem("h_lo")
        y_mm = sem("y_mm")
        y_add = sem("y_add")
        out_st = sem("out_st")
        acc_free = sem("acc_free")
        dsl_st = sem("dsl_st")
        far_idx, far_dst, far_turn, far_row, far_uniq, far_in, far_msg, far_mm, far_sum, far_st, far_ld, far_x, \
            far_init = (sem("far_" + n) for n in ("idx", "dst", "turn", "row", "uniq", "in", "msg", "mm", "sum", "st",
                                                  "ld", "x", "init"))
        k_shift_diag = sem("k_shift_diag")
        kmb_mm = sem("kmb_mm")
        ctx_done = sem("ctx_done")
        wqc_done = sem("wqc_done")
        tt_lo = sem("tt_lo")

        block = ctx.enter_context(nc.Block())

        def halves(t):
            return t.bitcast(F32)

        def edge_window(q):
            first = (STEP * q - WIN // 2) % P
            return dbl[:, (P - first) % P:(P - first) % P + P]

        def window_parts(q):
            return {0: [(64, 128, -1), (0, 64, 0)], 1: [(96, 128, -1), (0, 96, 0)],
                    2: [(0, 128, 0)], 3: [(32, 64, 0), (64, 128, 0), (0, 32, 1)]}[q]

        def apart(eng):
            eng.sem_inc(waited[eng_names.index(eng.engine)], 1)

        def first_phase_over(eng):
            eng.wait_ge(gnn_mm, 8 * NT)
            eng.wait_ge(bias_in, NT)
            eng.wait_ge(kmax_up, NT)
            eng.wait_ge(hgt_cp, NT)
            eng.wait_ge(kv_cp, 2 * NT)
            for b, n in ((0, NP + 1), (1, NP)):
                eng.wait_ge(xt_st[b], 16 * n)
                eng.wait_ge(kv_st[b], 16 * n)
                eng.wait_ge(hg_st[b], 16 * n)

        ADDS = {0: 2, 1: 2, 2: 1, 3: 3}

        @block.sync
        def _(sp):
            sp.wait_ge(cleared, 1)
            for a, v in ((src_r, src), (rel_r, rel), (dst_r, dst), (norm_r, norm.rearrange("e a -> (e a)"))):
                a3 = a.rearrange("p (b e) -> p b e", b=EB)
                first = (ER - SHIFT) * P
                sp.dma_start(a3[SHIFT:ER, 0, :], v[0:first].rearrange("(p e) -> p e", e=P)).then_inc(edges_in, 16)
                mid = first + (EB - 2) * ER * P
                sp.dma_start(a3[:, 1:EB - 1, :], v[first:mid].rearrange("(b p e) -> p b e", p=ER, e=P)).then_inc(edges_in, 16)
                full = (E - mid) // P
                sp.dma_start(a3[0:full, EB - 1, :], v[mid:mid + full * P].rearrange("(p e) -> p e", e=P)).then_inc(edges_in, 16)
                sp.dma_start(a3[full:full + 1, EB - 1, 0:E - mid - full * P],
                             v[mid + full * P:E].rearrange("(a e) -> a e", a=1)).then_inc(edges_in, 16)
            sp.wait_ge(cleared, 2)
            for k, (v, n) in enumerate(((ln_g, CC), (ln_b, CC), (bg2, CC))):
                sp.dma_start(vrow[16 + 2 * k:18 + 2 * k, :], v.rearrange("(a e) -> a e", a=CC)).then_inc(vec_in, 16)
            sp.dma_start(vrow[0:2 * X, :], b1.rearrange("x (a e) -> (x a) e", a=CC)).then_inc(vec_in, 16)
            sp.dma_start(bg1r, bg1.rearrange("(a e) -> a e", a=1)).then_inc(vec_in, 16)
            sp.dma_start(rwr[:], router_w).then_inc(vec_in, 16)
            sp.dma_start(b2s[:], b2).then_inc(vec_in, 16)
            sp.dma_start(wg2[:], Wg2).then_inc(vec_in, 16)
            wqkv_r = Wqkv.rearrange("(c p) n -> p c n", p=P)
            sp.dma_start(wkv_raw[:], wqkv_r[:, :, C:3 * C]).then_inc(mixw_in, 16)
            sp.dma_start(wg1_raw[:], Wg1.rearrange("(c p) n -> p c n", p=P)).then_inc(mixw_in, 16)
            sp.dma_start(wq_raw[:], wqkv_r[:, :, 0:C]).then_inc(mixw_in, 16)
            sp.dma_start(wp_raw[:], Wproj.rearrange("(c p) n -> p c n", p=P)).then_inc(mixw_in, 16)

            def stores(k, i, b):
                sp.wait_ge(xt_lo, k + 1)
                sp.dma_start(xt_d[bass.ds(k, 1)].rearrange("a p f -> (a p) f"),
                             halves(xt[b][:].rearrange("p h c n -> p (h c n)"))).then_inc(xt_st[b], 16)
                sp.wait_ge(kv_cp, 2 * k + 2)
                sp.dma_start(kv_d[bass.ds(k, 1)].rearrange("a p f -> (a p) f"), kvs[b][:]).then_inc(kv_st[b], 16)
                for h in range(2):
                    sp.wait_ge(tbl_act, 4 * k + 2 * h + 2)
                    sp.wait_ge(tbl_dve, 4 * k + 2 * h + 2)
                    sp.dma_start(table_rows[:, bass.ds(k, 1), h * R // 2 * C:(h + 1) * R // 2 * C].rearrange(
                        "p a f -> p (a f)"), stage[:, h, :]).then_inc(tbl_st[h], 16)
                    if h == 0:
                        sp.wait_ge(hgt_cp, k + 1)
                        sp.dma_start(hg_d[bass.ds(k, 1)].rearrange("a p f -> (a p) f"), hgt[b][:]).then_inc(hg_st[b], 16)

            table_rows = table.rearrange("(k p r) c -> p k (r c)", p=P, r=R)
            with sp.Fori(0, NP) as i:
                stores(2 * i, i, 0)
                stores(2 * i + 1, i, 1)
            stores(NT - 1, NP, 0)

            sp.wait_ge(kv_st[0], 16 * (NP + 1))
            sp.wait_ge(kv_st[1], 16 * NP)
            sp.wait_ge(w_lo, 8)

            def load_slots(i):
                for s in range(SLOTS):
                    if not isinstance(i, int) or i > 0:
                        sp.wait_ge(ctx_mm, SLOTS * (i - 1) + s + 1)
                    sp.dma_start(slot[:, s, :], kv_d[bass.ds(SLOTS * i + s, 1)].rearrange("a p f -> (a p) f")
                                 ).then_inc(kv_in[s], 16)

            load_slots(0)
            with sp.Fori(1, NT // SLOTS) as i:
                load_slots(i)

            first_phase_over(sp)

            def load_pair(p, nt):
                if not isinstance(p, int) or p > 0:
                    sp.wait_ge(mix_pe, 7 * p - 4)
                sp.dma_start(halves(xtp[:, 0:nt, :]), xt_d[bass.ds(2 * p, nt)].rearrange("a p f -> p a f")).then_inc(xtp_in, 16)
                sp.dma_start(hgp[:, 0:nt, :], hg_d[bass.ds(2 * p, nt)].rearrange("a p f -> p a f")).then_inc(xtp_in, 16)

            def store_pair(p, nt):
                sp.wait_ge(y_add, 2 * X * p + X * nt + AHEAD)
                if nt == 2:
                    sp.dma_start(out[0:NP * 2 * P].rearrange("(a p) c -> p a c", p=P)[:, bass.ds(2 * p, 2), :],
                                 acc).then_inc(out_st, 16)
                else:
                    sp.dma_start(out[(NT - 1) * P:N, :], acc[0:TAIL, 0, :]).then_inc(out_st, 16)

            load_pair(0, 2)
            sp.sem_inc(acc_free, 1)
            with sp.Fori(1, NP) as p:
                load_pair(p, 2)
                store_pair(p - 1, 2)
                sp.wait_ge(out_st, 16 * p)
                sp.sem_inc(acc_free, 1)
            load_pair(NP, 1)
            store_pair(NP - 1, 2)
            sp.wait_ge(out_st, 16 * NP)
            sp.sem_inc(acc_free, 1)
            store_pair(NP, 1)
            sp.wait_ge(out_st, 16 * (NP + 1))

        @block.gpsimd
        def _(pool):
            pool.memset(ident[:], 0.0).then_inc(consts, 1)
            pool.memset(ones[:], 1.0).then_inc(consts, 1)
            pool.wait_ge(consts, 2)
            pool.affine_select(out=ident[:], in_=ident[:], compare_op=ALU.not_equal, fill=1.0, base=0,
                               pattern=[[-1, P]], channel_multiplier=1).then_inc(consts, 1)
            pool.iota(smallu[:, 0, :].bitcast(I32), pattern=[[1, X]], base=0, channel_multiplier=0).then_inc(consts, 1)
            pool.iota(raw[:, 0, 0:2 * P].bitcast(I32), pattern=[[0, 2], [1, P]], base=0,
                      channel_multiplier=0).then_inc(consts, 1)
            pool.iota(lo_i, pattern=[[STEP, ET // SUP], [0, SUP]], base=-WIN // 2,
                      channel_multiplier=0).then_inc(consts, 1)
            pool.wait_ge(consts, 6)
            pool.tensor_copy(iota8[:], smallu[:, 0, :].bitcast(I32)).then_inc(consts, 1)
            pool.tensor_copy(dbl[:], raw[:, 0, 0:2 * P].bitcast(I32)).then_inc(consts, 1)
            pool.dma_start(bpb[:], bproj.rearrange("(a c) -> a c", a=1).to_broadcast([P, C])).then_inc(bp_in, 16)
            pool.memset(half, -0.5).then_inc(consts, 1)
            pool.wait_ge(consts, 9)
            pool.wait_ge(cleared, 2)
            pool.wait_ge(bp_in, 16)
            pc = Tally(pool_chain)

            def load_x(i):
                pool.dma_start(xres[:, bass.ds(2 * i, 2), :],
                               x[0:NP * 2 * P].rearrange("(a p) c -> p a c", p=P)[:, bass.ds(2 * i, 2), :]
                               ).then_inc(x_in, 16)

            def load_tail():
                pool.dma_start(xres[0:TAIL, NT - 1, :], x[(NT - 1) * P:N, :]).then_inc(x_in, 16)

            def roots(k, i, b):
                pool.wait_ge(var_ready, k + 1)
                if not isinstance(i, int) or i > 0:
                    pool.wait_ge(hg_pre, k - 1)
                apart(pool)
                pc.link(pool, pool.tensor_scalar(ve[:, 0:1], mv[:, b, 1:2], EPS, None, ALU.add))
                pool.tensor_tensor(rstd[:, b:b + 1], ve[:, 0:1], half[:, 0:1], ALU.pow).then_inc(rstd_ready, 1)
                pool.wait_ge(rstd_ready, k + 1)
                apart(pool)
                pc.link(pool, pool.tensor_scalar(ve[:, 1:2], mv[:, b, 1:2], rstd[:, b:b + 1], rstd[:, b:b + 1],
                                                 ALU.mult, ALU.mult))
                apart(pool)
                pc.link(pool, pool.tensor_scalar(ve[:, 1:2], ve[:, 1:2], EPS, None, ALU.add))
                pool.tensor_tensor(s2[:, b:b + 1], ve[:, 1:2], half[:, 0:1], ALU.pow).then_inc(s2_ready, 1)
                pool.wait_ge(xn_ready, k + 1)
                pool.tensor_tensor(xres[:, bass.ds(k, 1), :].rearrange("p a c -> p (a c)"),
                                   xres[:, bass.ds(k, 1), :].rearrange("p a c -> p (a c)"), bpb[:],
                                   ALU.add).then_inc(bias_in, 1)

            load_x(0)
            pool.wait_ge(x_in, 16)
            load_x(1)
            pool.wait_ge(x_in, 32)
            load_x(2)
            roots(0, 0, 0)
            roots(1, 0, 1)
            with pool.Fori(1, NP - 2) as i:
                pc.n = 6 * i
                pool.wait_ge(x_in, 16 * i + 32)
                load_x(i + 2)
                roots(2 * i, i, 0)
                roots(2 * i + 1, i, 1)
            for i in range(NP - 2, NP):
                pc.n = 6 * i
                if i == NP - 2:
                    pool.wait_ge(x_in, 16 * i + 32)
                    load_tail()
                roots(2 * i, i, 0)
                roots(2 * i + 1, i, 1)
            roots(NT - 1, NP, 0)
            first_phase_over(pool)
            pool.wait_ge(tbl_st[0], 16 * NT)
            pool.wait_ge(tbl_st[1], 16 * NT)
            pool.wait_ge(dve_chain, EDGE_PREP)

            pool.wait_ge(dve_chain, FLAG_READY)
            far = pool.value_load(flag[0:1, 0:1], min_val=0, max_val=NT * P * R)
            with pool.If(far > 0):
                pool.wait_ge(wqc_done, 1)
                pool.memset(stg[:, 0:3, :], 0.0).then_inc(far_init, 1)
                pool.memset(f_low, 1.0).then_inc(far_init, 1)
                pool.wait_ge(far_init, 2)
                pool.affine_select(out=f_low, in_=f_low, compare_op=ALU.is_gt, fill=0.0, base=0,
                                   pattern=[[-1, P]], channel_multiplier=1).then_inc(far_init, 1)
                pool.dma_start(f_dsl, dsl_d).then_inc(far_ld, 16)
                with pool.Fori(0, NT) as k:
                    pool.dma_start(gnn_d.rearrange("(k p) c -> p k c", p=P)[:, bass.ds(k, 1), :],
                                   stg[:, 0:1, :]).then_inc(far_ld, 16)
                pool.wait_ge(far_ld, 16 * (NT + 1))
                with pool.Fori(0, ET) as t:
                    pool.tensor_copy(f_i[:, 0:1], gidx[:, bass.ds(t, 1)]).then_inc(far_idx, 1)
                    pool.wait_ge(far_idx, t + 1)
                    apart(pool)
                    pool.indirect_dma_start(stg[:, 0, :], None, table,
                                            bass.IndirectOffsetOnAxis(ap=f_i[:, 0:1], axis=0),
                                            bounds_check=NT * P * R - 1, oob_is_err=False).then_inc(far_in, 16)
                    pool.wait_ge(far_dst, t + 1)
                    apart(pool)
                    pool.indirect_dma_start(stg[:, 1, :], None, gnn_d,
                                            bass.IndirectOffsetOnAxis(ap=f_i[:, 1:2], axis=0),
                                            bounds_check=NT * P - 1, oob_is_err=False).then_inc(far_in, 16)
                    pool.wait_ge(far_sum, t + 1)
                    apart(pool)
                    pool.indirect_dma_start(gnn_d, bass.IndirectOffsetOnAxis(ap=f_i[:, 2:3], axis=0),
                                            stg[:, 2, :], None,
                                            bounds_check=NT * P - 1, oob_is_err=False).then_inc(far_st, 16)
                    pool.wait_ge(far_st, 16 * t + 16)
                with pool.Fori(0, NT) as k:
                    pool.dma_start(stg[:, 3:4, :], gnn_d.rearrange("(k p) c -> p k c", p=P)[:, bass.ds(k, 1), :]
                                   ).then_inc(far_ld, 16)
                    pool.wait_ge(far_x, k + 1)

            def gathers(i, groups):
                for s in range(groups):
                    if s % 4 == 0:
                        for g in range(4):
                            if not isinstance(i, int) or i > 0:
                                pool.wait_ge(gath[g], 64 * (2 * i - 1 + s // 4))
                        pool.tensor_copy(idxcur[:, s * SUP:(s + 4) * SUP],
                                         gidx[:, bass.ds((8 * i + s) * SUP, 4 * SUP)]).then_inc(idx_cur, 1)
                        pool.wait_ge(idx_cur, 2 * i + s // 4 + 1)
                    if s >= 4 or not isinstance(i, int) or i > 0:
                        pool.wait_ge(msg_lo, SUP * (8 * i + s - 3))
                        apart(pool)
                    for j in range(SUP):
                        pool.indirect_dma_start(
                            stg[:, (s % 4) * SUP + j, :], None, table,
                            bass.IndirectOffsetOnAxis(ap=idxcur[:, s * SUP + j:s * SUP + j + 1], axis=0),
                            bounds_check=NT * P * R - 1, oob_is_err=False).then_inc(gath[s % 4], 16)
                    if (i if isinstance(i, int) else 1) > 0 and s == min(6, groups - 1):
                        roots2(i - 1, 2)

            def roots2(p, nt):
                pool.wait_ge(var2_ready, 2 * p + nt)
                apart(pool)
                pc.link(pool, pool.tensor_scalar(ve[:, 0:nt], mv[:, 0:nt, 1], EPS, None, ALU.add))
                pool.tensor_tensor(rstd[:, 0:nt], ve[:, 0:nt], half[:, 0:nt], ALU.pow).then_inc(rstd2_ready, 1)

            gathers(0, 8)
            base = pc.n
            with pool.Fori(1, NP) as i:
                pc.n = base + i - 1
                gathers(i, 8)
            pc.n = base + NP - 1
            gathers(NP, 4)
            roots2(NP, 1)

        @block.scalar
        def _(act):
            chunks = [Wr[WC * n:WC * n + WC] for n in range(4)] + \
                     [w[WC * n:WC * n + WC] for w in (w1, w2) for n in range(2)]

            def load_chunk(n):
                for c in range(CC):
                    act.dma_start(raw[:, n % 2, :].rearrange("p (c r o) -> p c r o", c=CC, r=WC)[:, c],
                                  chunks[n].rearrange("r (c p) o -> p c r o", p=P)[:, c]).then_inc(raw_in[n % 2], 16)

            def split_hi(n):
                act.wait_ge(raw_in[n % 2], 32 * (n // 2 + 1))
                act.copy(wreg[:, HI, n % 4].rearrange("p c r o -> p (c r o)"), raw[:, n % 2, :]).then_inc(w_hi, 1)

            act.wait_ge(dve_chain, EDGE_PREP)
            act.dma_start(dsl_d, dsl).then_inc(dsl_st, 16)
            load_chunk(1)
            act.wait_ge(dsl_st, 16)
            load_chunk(0)
            act.wait_ge(setup_pe, 3)
            act.copy(nrm[:, 0:4 * ER], bank[4][:, 0:4 * ER]).then_inc(setup_act, 1)
            act.copy(nrm[:, 4 * ER:ET], bank[5][:, 0:ET - 4 * ER]).then_inc(setup_act, 1)
            act.wait_ge(mixw_in, 64)
            act.copy(wkvg[:, HI, :, 0:2 * C], wkv_raw[:]).then_inc(setup_act, 1)
            act.copy(wproj[:, HI], wp_raw[:]).then_inc(setup_act, 1)
            act.wait_ge(dve_chain, WG1_READY)
            act.copy(wkvg[:, HI, :, 2 * C:2 * C + G], wg1_f[:]).then_inc(setup_act, 1)
            act.wait_ge(setup_pe, 4)
            act.copy(wqt[:].rearrange("p c n -> p (c n)"), bank[6][:]).then_inc(setup_act, 1)
            for n in range(4):
                split_hi(n)
                act.wait_ge(w_lo, n + 1)
                load_chunk(n + 2)

            def table_out(k, j):
                if j % 4 == 0:
                    if not isinstance(k, int) or k > 0:
                        act.wait_ge(tbl_st[j // 4], 16 * k)
                act.wait_ge(gnn_mm, 8 * k + j + 1)
                act.copy(stage[:, j // 4, (j % 4) * 512:(j % 4 + 1) * 512], bank[3 + j % 4][:]).then_inc(tbl_act, 1)

            def xt_high(k, i, b):
                act.wait_ge(xt_psum, k + 1)
                if not isinstance(i, int) or i > 0:
                    act.wait_ge(gnn_mm, 8 * k - 8)
                    act.wait_ge(xt_st[b], 16 * i)
                act.copy(xt[b][:, HI].rearrange("p c n -> p (c n)"), bank[0][:, 0:C]).then_inc(xt_hi, 1)

            def tile_act(k, i, b, more, nxt):
                act.wait_ge(kv_mm, k + 1)
                if not isinstance(i, int) or i > 0:
                    act.wait_ge(kv_st[b], 16 * i)
                    act.wait_ge(kmax_up, k - 1)
                act.copy(kvs[b][:, 0:C], bank[1][:, 0:C]).then_inc(kv_cp, 1)
                act.copy(kvs[b][:, C:].rearrange("p (c w) -> p c w", c=CC)[:, :, 0:P],
                         bank[1][:, C:2 * C].rearrange("p (c w) -> p c w", c=CC)).then_inc(kv_cp, 1)
                act.wait_ge(hg_pre, k + 1)
                act.activation(hgn[:, 1, :], hgn[:, 0, :], ACT.Gelu).then_inc(hg_act, 1)
                table_out(k, 0)
                table_out(k, 2)
                if more:
                    xt_high(*nxt)
                act.wait_ge(hgt_psum, k + 1)
                if not isinstance(i, int) or i > 0:
                    act.wait_ge(hg_st[b], 16 * i)
                act.copy(hgt[b][:], bank[7][0:G, 0:P]).then_inc(hgt_cp, 1)
                table_out(k, 4)
                table_out(k, 6)

            xt_high(0, 0, 0)
            tile_act(0, 0, 0, True, (1, 0, 1))
            tile_act(1, 0, 1, True, (2, 1, 0))
            with act.Fori(1, NP) as i:
                tile_act(2 * i, i, 0, True, (2 * i + 1, i, 1))
                tile_act(2 * i + 1, i, 1, True, (2 * i + 2, i + 1, 0))
            tile_act(NT - 1, NP, 0, False, None)

            for n in range(4, 8):
                if n == 4:
                    act.wait_ge(gnn_mm, 8 * NT)
                split_hi(n)
                if n < 6:
                    act.wait_ge(w_lo, n + 1)
                    load_chunk(n + 2)

            def exps(i):
                for s in range(SLOTS):
                    act.wait_ge(k_shift, SLOTS * i + s + 1)
                    act.activation(slot[:, s, 0:C], slot[:, s, 0:C], ACT.Exp).then_inc(k_exp, 1)

            with act.Fori(0, NT // SLOTS) as i:
                exps(i)
            act.wait_ge(setup_pe, 8)
            act.mul(wqc[:, HI].rearrange("p c n -> p (c n)"), bank[4][:], 0.5).then_inc(setup_act, 1)

            first_phase_over(act)

            def msgs(i, s, first):
                S = 8 * i + s
                act.wait_ge(gath[s % 4], 64 * (2 * i + s // 4 + 1))
                if s >= 2 or not first:
                    act.wait_ge(edge_mm, S - 1)
                for j in range(SUP):
                    act.activation(mh[:, (s % 2) * SUP + j, :], stg[:, (s % 4) * SUP + j, :], ACT.Copy,
                                   scale=nrm[:, bass.ds(SUP * S + j, 1)]).then_inc(msg_hi, 1)

            def mix(p, nt):
                n = nt * P
                act.wait_ge(mix_pe, 7 * p + 2)
                for c in range(CC):
                    act.activation(gate[:, c * 256:c * 256 + n], bank[5][:, c * 256:c * 256 + n], ACT.Tanh,
                                   bias=bg2h[:, c:c + 1], scale=0.5).then_inc(mix_act, 1)
                act.wait_ge(mix_dve, 5 * p + 1)
                act.copy(og[:, HI, :, 0:n], ogf.rearrange("p (c n) -> p c n", c=CC)[:, :, 0:n]).then_inc(mix_act, 1)

            def prep(p, nt):
                n = nt * P
                act.wait_ge(mix_pe, 7 * p + 4)
                act.copy(tt[:, HI, :, 0:n], bank[5][:].rearrange("p (c n) -> p c n", c=CC)[:, :, 0:n]).then_inc(mix_act, 1)

            def route(p, nt):
                act.wait_ge(mix_dve, 5 * p + 4)
                act.activation(th[:, 0:nt], dlt[:, 0:nt], ACT.Tanh, scale=0.5).then_inc(mix_act, 1)
                act.wait_ge(mix_pe, 7 * p + 6)
                act.copy(ct[:, 0:nt * P], bank[5][0:X, 0:nt * P]).then_inc(mix_act, 1)

            def gelus(p, e, nt):
                n = nt * P
                T = X * p + e
                act.wait_ge(h_mm, T + 1)
                if e == 0:
                    act.wait_ge(y_add, 2 * X * p + AHEAD)
                if e >= 2:
                    act.wait_ge(h_lo, T - 1)
                for c in range(CC):
                    act.activation(hf[e % 2][:, c * 256:c * 256 + n], bank[2 + e % 2][:, c * 256:c * 256 + n],
                                   ACT.Gelu, bias=b1c[:, 2 * e + c:2 * e + c + 1]).then_inc(h_act, 1)
                act.wait_ge(h_act, 2 * T + 2)
                if e >= 2:
                    act.wait_ge(y_mm, T - 1)
                act.copy(ht[e % 2][:, HI, :, 0:n],
                         hf[e % 2].rearrange("p (c n) -> p c n", c=CC)[:, :, 0:n]).then_inc(h_hi, 1)

            def body(i, groups, first):
                for s in range(groups):
                    msgs(i, s, first)
                    if not first:
                        interleaved(s, i - 1, 2, groups, mix, prep, route, gelus)

            body(0, 8, True)
            with act.Fori(1, NP) as i:
                body(i, 8, False)
            body(NP, 4, False)
            mix(NP, 1)
            prep(NP, 1)
            route(NP, 1)
            for e in range(X):
                gelus(NP, e, 1)

        @block.vector
        def _(dve):
            ch = Tally(dve_chain)
            dve.sem_inc(y_add, AHEAD)
            dve.memset(src_r, 0)
            dve.memset(rel_r, 0)
            dve.memset(dst_r, PAD_DST)
            dve.memset(norm_r, 0.0).then_inc(cleared, 1)
            dve.memset(vrow[:], 0.0)
            dve.memset(xres[96:P, NT - 1, :], 0.0)
            for b in range(2):
                for c in range(CC):
                    dve.memset(kvs[b][:, C + c * VW + P:C + c * VW + VW], 1.0)
            dve.memset(kmax[:], -3.0e38).then_inc(cleared, 1)
            dve.wait_ge(cleared, 2)

            dve.wait_ge(edges_in, 16 * 16)
            ch.inc(dve.scalar_tensor_tensor(out=erow[:, 0, :], in0=src_r, scalar=float(R), in1=rel_r,
                                            op0=ALU.mult, op1=ALU.add))
            ch.inc(dve.tensor_copy(erow[:, 1, :], dst_r))
            dve.wait_ge(setup_pe, 1)
            ch.inc(dve.tensor_copy(gidx[:, 0:4 * ER], bank[0][:, 0:4 * ER]))
            ch.inc(dve.tensor_copy(gidx[:, 4 * ER:ET], bank[1][:, 0:ET - 4 * ER]))
            dve.wait_ge(consts, 8)
            dve.wait_ge(setup_pe, 2)
            ch.inc(dve.tensor_tensor(dpr[:, 0:4 * ER], bank[2][:, 0:4 * ER], lo_i[:, 0:4 * ER], ALU.subtract))
            ch.link(dve, dve.tensor_tensor(dpr[:, 4 * ER:ET], bank[3][:, 0:ET - 4 * ER], lo_i[:, 4 * ER:ET], ALU.subtract))
            ch.link(dve, dve.tensor_scalar(mask, dpr[:], 0.0, None, ALU.is_lt))
            ch.link(dve, dve.scalar_tensor_tensor(out=mask, in0=dpr[:], scalar=PAD_DST / 2.0, in1=mask,
                                                  op0=ALU.is_gt, op1=ALU.mult))
            ch.link(dve, dve.scalar_tensor_tensor(out=mask, in0=dpr[:], scalar=WIN - 1.0, in1=mask,
                                                  op0=ALU.is_gt, op1=ALU.add))
            ch.link(dve, dve.tensor_reduce(cnt, mask, AX.X, ALU.add))
            ch.link(dve, dve.tensor_tensor(dsl, dpr[:], lo_i, ALU.add))
            ch.link(dve, dve.scalar_tensor_tensor(out=dsl, in0=dsl, scalar=-float(FAR), in1=mask, op0=ALU.add,
                                                  op1=ALU.mult))
            ch.link(dve, dve.tensor_scalar(dsl, dsl, float(FAR), None, ALU.add))
            assert ch.n == EDGE_PREP
            dve.wait_ge(setup_pe, 5)
            ch.inc(dve.tensor_copy(cols[:, 0:22], bank[7][:, 0:22]))
            ch.link(dve, dve.tensor_copy(rwt[:].rearrange("p c x -> p (c x)"), bank[7][:, 32:32 + CC * X]))
            dve.wait_ge(mixw_in, 64)
            dve.wait_ge(vec_in, 8 * 16)
            ch.inc(dve.tensor_scalar(bg2h, bg2c, 0.5, None, ALU.mult))
            for c in range(CC):
                ch.inc(dve.tensor_scalar(wg1_f[:, c, :], wg1_raw[:, c, :], gcol[:, c:c + 1], None, ALU.mult))
                ch.inc(dve.tensor_scalar(lnbb[:, c, :], ones[:], bcol[:, c:c + 1], None, ALU.mult))
            dve.wait_ge(dve_chain, ch.n)
            assert ch.n == WG1_READY
            dve.wait_ge(setup_pe, 6)
            ch.inc(dve.tensor_copy(g1b[:], bank[5][:, 0:G]))
            ch.inc(dve.tensor_copy(flag[:], bank[5][0:1, G:G + 1]))
            assert ch.n == FLAG_READY
            dve.wait_ge(setup_act, 5)
            ch.inc(dve.tensor_tensor(wkvg[:, LO, :, 0:2 * C], wkv_raw[:], halves(wkvg[:, HI, :, 0:2 * C]), ALU.subtract))
            ch.inc(dve.tensor_tensor(wkvg[:, LO, :, 2 * C:2 * C + G], wg1_f[:],
                                     halves(wkvg[:, HI, :, 2 * C:2 * C + G]), ALU.subtract))
            ch.inc(dve.tensor_tensor(wproj[:, LO], wp_raw[:], halves(wproj[:, HI]), ALU.subtract))
            assert ch.n == MIXW_READY

            def split_lo(n):
                dve.wait_ge(w_hi, n + 1)
                dve.tensor_tensor(wreg[:, LO, n % 4].rearrange("p c r o -> p (c r o)"), raw[:, n % 2, :],
                                  halves(wreg[:, HI, n % 4].rearrange("p c r o -> p (c r o)")),
                                  ALU.subtract).then_inc(w_lo, 1)

            for n in range(4):
                split_lo(n)

            def layer_norm(k, i, b):
                dve.wait_ge(x_in, 16 * i + 16)
                if not isinstance(i, int) or i > 0:
                    dve.wait_ge(xt_psum, k - 1)
                xk = xres[:, bass.ds(k, 1), :].rearrange("p a c -> p (a c)")
                apart(dve)
                ch.link(dve, dve.bn_stats(stats[:, b, :], xk))
                if not isinstance(i, int) or i > 0:
                    dve.wait_ge(s2_ready, k - 1)
                apart(dve)
                dve.bn_aggr(mv[:, b, :], stats[:, b, :]).then_inc(var_ready, 1)
                dve.wait_ge(rstd_ready, k + 1)
                dve.tensor_scalar(xn[b][:], xk, mv[:, b, 0:1], rstd[:, b:b + 1], ALU.subtract,
                                  ALU.mult).then_inc(xn_ready, 1)

            def table_out(k, j):
                if j % 4 == 1:
                    if not isinstance(k, int) or k > 0:
                        dve.wait_ge(tbl_st[j // 4], 16 * k)
                dve.wait_ge(gnn_mm, 8 * k + j + 1)
                dve.tensor_copy(stage[:, j // 4, (j % 4) * 512:(j % 4 + 1) * 512], bank[3 + j % 4][:]).then_inc(tbl_dve, 1)

            def xt_low(k, b):
                dve.wait_ge(xt_hi, k + 1)
                dve.tensor_tensor(xt[b][:, LO].rearrange("p c n -> p (c n)"), bank[0][:, 0:C],
                                  halves(xt[b][:, HI].rearrange("p c n -> p (c n)")), ALU.subtract).then_inc(xt_lo, 1)

            def tile_dve(k, i, b, rows, nxt):
                dve.wait_ge(hg_mm, k + 1)
                dve.wait_ge(s2_ready, k + 1)
                if not isinstance(k, int) or k > 0:
                    dve.wait_ge(hg_act, k)
                dve.scalar_tensor_tensor(out=hgn[:, 0, :], in0=bank[2][:, 0:G], scalar=s2[:, b:b + 1], in1=g1b[:],
                                         op0=ALU.mult, op1=ALU.add).then_inc(hg_pre, 1)
                if nxt:
                    layer_norm(*nxt)
                table_out(k, 1)
                table_out(k, 3)
                if nxt:
                    xt_low(nxt[0], nxt[2])
                dve.wait_ge(kv_cp, 2 * k + 2)
                if not isinstance(k, int) or k > 0:
                    dve.wait_ge(kmax_up, k)
                dve.tensor_tensor(kmax[0:rows], kmax[0:rows], kvs[b][0:rows, 0:C], ALU.max).then_inc(kmax_up, 1)
                table_out(k, 5)
                table_out(k, 7)

            layer_norm(0, 0, 0)
            xt_low(0, 0)
            tile_dve(0, 0, 0, P, (1, 0, 1))
            tile_dve(1, 0, 1, P, (2, 1, 0))
            base = ch.n
            with dve.Fori(1, NP) as i:
                ch.n = base + 2 * (i - 1)
                tile_dve(2 * i, i, 0, P, (2 * i + 1, i, 1))
                tile_dve(2 * i + 1, i, 1, P, (2 * i + 2, i + 1, 0))
            ch.n = base + 2 * (NP - 1)
            tile_dve(NT - 1, NP, 0, TAIL, None)

            first_phase_over(dve)
            dve.wait_ge(setup_pe, 7)
            ch.link(dve, dve.tensor_reduce(kcol, bank[0][:, 0:C].rearrange("p (c n) -> p c n", c=CC), AX.X, ALU.max))
            for c in range(CC):
                ins = dve.tensor_scalar(dg[:, c * P:(c + 1) * P], ident[:], kcol[:, c:c + 1], None, ALU.mult)
                ins.then_inc(k_shift_diag, 1)
            dve.wait_ge(kmb_mm, 1)
            ch.link(dve, dve.tensor_copy(kmb[:], bank[1][:, 0:C]))
            for n in range(4, 8):
                split_lo(n)

            def shifts(i):
                for s in range(SLOTS):
                    dve.wait_ge(kv_in[s], 16 * i + 16)
                    dve.tensor_tensor(slot[:, s, 0:C], slot[:, s, 0:C], kmb[:], ALU.subtract).then_inc(k_shift, 1)

            with dve.Fori(0, NT // SLOTS) as i:
                shifts(i)

            ch.link(dve, dve.memset(ctxbd[:], 0.0))
            dve.wait_ge(ctx_mm, NT)
            for c in range(CC):
                ch.inc(dve.reciprocal(rden[:, c:c + 1], bank[2 + c][:, P:P + 1]))
            dve.wait_ge(dve_chain, ch.n)
            for c in range(CC):
                for h in range(NB):
                    d = slice(h * HEAD, (h + 1) * HEAD)
                    dve.tensor_scalar(ctxbd[d, c, d], bank[2 + c][d, d], rden[d, c:c + 1], None,
                                      ALU.mult).then_inc(ctx_done, 1)
            dve.wait_ge(setup_act, 7)
            dve.scalar_tensor_tensor(out=wqc[:, LO].rearrange("p c n -> p (c n)"), in0=bank[4][:], scalar=0.5,
                                     in1=halves(wqc[:, HI].rearrange("p c n -> p (c n)")), op0=ALU.mult,
                                     op1=ALU.subtract).then_inc(wqc_done, 1)
            dve.wait_ge(dve_chain, FLAG_READY)
            far = dve.value_load(flag[0:1, 0:1], min_val=0, max_val=NT * P * R)
            with dve.If(far > 0):
                dve.wait_ge(far_init, 3)
                dve.wait_ge(far_ld, 16 * (NT + 1))
                fch = Tally(dve_chain)
                with dve.Fori(0, ET) as t:
                    fch.n = ch.n + 3 * t
                    dcol = f_dsl[:, bass.ds(t, 1)]
                    dve.wait_ge(far_idx, t + 1)
                    dve.tensor_copy(f_i[:, 1:2], dcol).then_inc(far_dst, 1)
                    dve.tensor_scalar(f_turn, ones[:], dcol, None, ALU.mult).then_inc(far_turn, 1)
                    dve.wait_ge(far_row, t + 1)
                    fch.link(dve, dve.tensor_scalar(f_same, bank[6][:, 0:P], dcol, None, ALU.is_equal))
                    fch.link(dve, dve.tensor_tensor(f_turn, f_same, f_low, ALU.mult))
                    fch.link(dve, dve.tensor_reduce(f_dup, f_turn, AX.X, ALU.add))
                    dve.scalar_tensor_tensor(out=f_i[:, 2:3], in0=f_dup, scalar=float(FAR), in1=dcol,
                                             op0=ALU.mult, op1=ALU.add).then_inc(far_uniq, 1)
                    dve.wait_ge(far_in, 32 * t + 32)
                    dve.tensor_scalar(stg[:, 3, :], stg[:, 0, :], nrm[:, bass.ds(t, 1)], None,
                                      ALU.mult).then_inc(far_msg, 1)
                    dve.wait_ge(far_mm, t + 1)
                    dve.wait_ge(far_uniq, t + 1)
                    dve.tensor_tensor(stg[:, 2, :], bank[7][:, 0:C], stg[:, 1, :], ALU.add).then_inc(far_sum, 1)
                with dve.Fori(0, NT) as k:
                    dve.wait_ge(far_ld, 16 * k + 16 * (NT + 2))
                    xk = xres[:, bass.ds(k, 1), :]
                    dve.tensor_tensor(xk, xk, stg[:, 3:4, :], ALU.add).then_inc(far_x, 1)
            with dve.Else():
                dve.sem_inc(dve_chain, 3 * ET)
            ch.n = ch.n + 3 * ET

            def adds_before(S8, s):
                return 16 * S8 + 8 * (s // 4) + sum(ADDS[q] for q in range(s % 4)) - SKIPPED

            def msgs(i, s, first):
                S = 8 * i + s
                if s >= 2 or not first:
                    dve.wait_ge(edge_mm, S - 1)
                for j in range(SUP):
                    dve.tensor_scalar(sel[:, (s % 2) * SUP + j, :], edge_window(s % 4), dpr[:, bass.ds(SUP * S + j, 1)],
                                      None, ALU.is_equal).then_inc(sel_done, 1)
                for j in range(SUP):
                    m = (s % 2) * SUP + j
                    dve.wait_ge(msg_hi, SUP * S + j + 1)
                    dve.scalar_tensor_tensor(out=ml[:, m, :], in0=stg[:, (s % 4) * SUP + j, :],
                                             scalar=nrm[:, bass.ds(SUP * S + j, 1)], in1=halves(mh[:, m, :]),
                                             op0=ALU.mult, op1=ALU.subtract).then_inc(msg_lo, 1)

            def adds(i, s):
                dve.wait_ge(edge_mm, 8 * i + s + 1)
                if not (isinstance(i, int) and i == 0 and s == 0):
                    dve.wait_ge(edge_add, adds_before(i, s))
                for a, b, t in window_parts(s % 4):
                    if isinstance(i, int) and not 0 <= 2 * i + s // 4 + t < NT:
                        continue
                    k = 2 * i + s // 4 + t
                    xk = xres[a:b, bass.ds(k, 1), :].rearrange("p a c -> p (a c)")
                    dve.tensor_tensor(xk, bank[s % 2][a:b, 0:C], xk, ALU.add).then_inc(edge_add, 1)

            def mix(p, nt):
                n = nt * P
                dve.wait_ge(mix_act, 6 * p + 2)
                dve.scalar_tensor_tensor(out=ogf.rearrange("p (c n) -> p c n", c=CC)[:, :, 0:n],
                                         in0=gate.rearrange("p (c n) -> p c n", c=CC)[:, :, 0:n], scalar=1.0,
                                         in1=bank[4][:].rearrange("p (c n) -> p c n", c=CC)[:, :, 0:n],
                                         op0=ALU.add, op1=ALU.mult).then_inc(mix_dve, 1)
                dve.wait_ge(mix_act, 6 * p + 3)
                dve.tensor_tensor(og[:, LO, :, 0:n], ogf.rearrange("p (c n) -> p c n", c=CC)[:, :, 0:n],
                                  halves(og[:, HI, :, 0:n]), ALU.subtract).then_inc(mix_dve, 1)

            def prep(p, nt):
                n = nt * P
                xp = xres[:, bass.ds(2 * p, nt), :]
                dve.wait_ge(mix_pe, 7 * p + 3)
                ch.link(dve, dve.tensor_tensor(xp, bank[4][:].rearrange("p (a c) -> p a c", a=2)[:, 0:nt], xp, ALU.add))
                apart(dve)
                for a in range(nt):
                    ch.inc(dve.bn_stats(stats[:, a, :], xres[:, bass.ds(2 * p + a, 1), :].rearrange("p a c -> p (a c)")))
                dve.wait_ge(dve_chain, ch.n)
                apart(dve)
                for a in range(nt):
                    dve.bn_aggr(mv[:, a, :], stats[:, a, :]).then_inc(var2_ready, 1)
                dve.wait_ge(rstd2_ready, p + 1)
                for a in range(nt):
                    ins = dve.tensor_scalar(tn[:, a, :], xres[:, bass.ds(2 * p + a, 1), :].rearrange("p a c -> p (a c)"),
                                            mv[:, a, 0:1], rstd[:, a:a + 1], ALU.subtract, ALU.mult)
                    ch.inc(ins)
                dve.wait_ge(dve_chain, ch.n)
                dve.wait_ge(acc_free, p + 1)
                dve.tensor_tensor(acc[:, 0:nt], xp, tn[:, 0:nt], ALU.add).then_inc(mix_dve, 1)
                dve.wait_ge(mix_act, 6 * p + 4)
                dve.tensor_tensor(tt[:, LO, :, 0:n], bank[5][:].rearrange("p (c n) -> p c n", c=CC)[:, :, 0:n],
                                  halves(tt[:, HI, :, 0:n]), ALU.subtract).then_inc(tt_lo, 1)

            def route(p, nt):
                dve.wait_ge(mix_pe, 7 * p + 5)
                ch.link(dve, dve.tensor_copy(lg[:, 0:nt], bank[4][:, 0:nt * X].rearrange("p (a e) -> p a e", a=nt)))
                apart(dve)
                for a in range(nt):
                    ch.inc(dve.max(top[:, a, :], lg[:, a, :]))
                dve.wait_ge(dve_chain, ch.n)
                apart(dve)
                for a in range(nt):
                    ch.inc(dve.max_index(smallu[:, a, :], top[:, a, :], lg[:, a, :]))
                ch.inc(dve.tensor_tensor(dlt[:, 0:nt], top[:, 0:nt, 0], top[:, 0:nt, 1], ALU.subtract))
                dve.wait_ge(dve_chain, ch.n)
                dve.tensor_copy(idf[:, 0:nt], smallu[:, 0:nt]).then_inc(mix_dve, 1)
                dve.wait_ge(mix_act, 6 * p + 5)
                dve.wait_ge(mix_dve, 5 * p + 4)
                ch.inc(dve.tensor_scalar(wa[:, 0:nt], th[:, 0:nt], 0.5, 0.5, ALU.mult, ALU.add))
                ch.inc(dve.tensor_scalar(wb[:, 0:nt], th[:, 0:nt], -0.5, 0.5, ALU.mult, ALU.add))
                dve.wait_ge(dve_chain, ch.n)
                for a in range(nt):
                    ch.inc(dve.tensor_scalar(cb2[:, a, :], iota8[:], idf[:, a, 0:1], wa[:, a:a + 1], ALU.is_equal, ALU.mult))
                    ch.inc(dve.tensor_scalar(lg[:, a, :], iota8[:], idf[:, a, 1:2], wb[:, a:a + 1], ALU.is_equal, ALU.mult))
                dve.wait_ge(dve_chain, ch.n)
                dve.tensor_tensor(comb[:, 0:nt], cb2[:, 0:nt], lg[:, 0:nt], ALU.add).then_inc(mix_dve, 1)
                dve.wait_ge(mix_pe, 7 * p + 7)
                ch.link(dve, dve.tensor_tensor(acc[:, 0:nt], bank[4][:].rearrange("p (a c) -> p a c", a=2)[:, 0:nt],
                                               acc[:, 0:nt], ALU.add))

            def h_low(p, e, nt):
                n = nt * P
                dve.wait_ge(h_hi, X * p + e + 1)
                dve.tensor_tensor(ht[e % 2][:, LO, :, 0:n],
                                  hf[e % 2].rearrange("p (c n) -> p c n", c=CC)[:, :, 0:n],
                                  halves(ht[e % 2][:, HI, :, 0:n]), ALU.subtract).then_inc(h_lo, 1)

            def y_in(p, e, nt):
                dve.wait_ge(y_mm, X * p + e + 1)
                if e > 0:
                    dve.wait_ge(y_add, 2 * X * p + nt * e + AHEAD)
                for a in range(nt):
                    dve.scalar_tensor_tensor(out=acc[:, a, :], in0=bank[6 + e % 2][:, a * C:(a + 1) * C],
                                             scalar=comb[:, a, e:e + 1], in1=acc[:, a, :], op0=ALU.mult,
                                             op1=ALU.add).then_inc(y_add, 1)

            def expert(p, e, nt):
                h_low(p, e, nt)
                if e > 0:
                    y_in(p, e - 1, nt)
                if e == X - 1:
                    y_in(p, e, nt)

            def body(i, groups, first):
                for s in range(groups):
                    msgs(i, s, first)
                    adds(i, s)
                    if not first:
                        interleaved(s, i - 1, 2, groups, mix, prep, route, expert)

            body(0, 8, True)
            base = ch.n
            with dve.Fori(1, NP) as i:
                ch.n = base + CHAIN2 * (i - 1)
                body(i, 8, False)
            ch.n = base + CHAIN2 * (NP - 1)
            body(NP, 4, False)
            mix(NP, 1)
            prep(NP, 1)
            route(NP, 1)
            for e in range(X):
                expert(NP, e, 1)

        @block.tensor
        def _(pe):
            pe.wait_ge(consts, 8)
            for a, (rows, at, need) in enumerate(((erow[:, 0, :], 0, 1), (erow[:, 1, :], 2, 2), (norm_r, 4, 2))):
                pe.wait_ge(dve_chain, need)
                for j in range(EB):
                    mm = pe.transpose(bank[at + j // 4][:, (j % 4) * ER:(j % 4 + 1) * ER],
                                      rows[:, j * P:(j + 1) * P], ident[0:ER, 0:ER])
                mm.then_inc(setup_pe, 1)
            pe.wait_ge(mixw_in, 64)
            for c in range(CC):
                for d in range(CC):
                    mm = pe.transpose(bank[6][:, c * C + d * P:c * C + (d + 1) * P],
                                      wq_raw[:, d, c * P:(c + 1) * P], ident[:])
            mm.then_inc(setup_pe, 1)
            pe.wait_ge(vec_in, 8 * 16)
            pe.transpose(bank[7][:, 0:22], vrow[0:22, :], ident[0:22, 0:22])
            for c in range(CC):
                mm = pe.transpose(bank[7][:, 32 + c * X:32 + (c + 1) * X], rwr[:, c * P:(c + 1) * P], ident[0:X, 0:X])
            mm.then_inc(setup_pe, 1)
            pe.wait_ge(dve_chain, WG1_READY)
            pe.wait_ge(setup_act, 2)
            for c in range(CC):
                pe.matmul(bank[5][:, 0:G], lnbb[:, c, :], wg1_raw[:, c, :], start=(c == 0), stop=False)
            pe.matmul(bank[5][:, 0:G], ones[0:1, :], bg1r, start=False, stop=True)
            pe.matmul(bank[5][0:1, G:G + 1], cnt, ones[:, 0:1], start=True, stop=True).then_inc(setup_pe, 1)

            def three(dst, stat, mov, k0=0, chunks=CC):
                n = 0
                for c in range(chunks):
                    for a, b in PASSES:
                        mm = pe.matmul(dst, stat(a, c), mov(b, c), start=(n == 0), stop=(n == 3 * chunks - 1))
                        n += 1
                return mm

            def turn(k, b):
                pe.wait_ge(xn_ready, k + 1)
                if not isinstance(k, int) or k > 0:
                    pe.wait_ge(xt_lo, k)
                for c in range(CC):
                    mm = pe.transpose(bank[0][:, c * P:(c + 1) * P], xn[b][:, c * P:(c + 1) * P], ident[:])
                mm.then_inc(xt_psum, 1)

            def relations(k, b, j):
                if j % 2 == 0:
                    if j >= 4 or not isinstance(k, int) or k > 0:
                        pe.wait_ge(tbl_act, 4 * k + j // 2 - 1)
                else:
                    if j >= 4 or not isinstance(k, int) or k > 0:
                        pe.wait_ge(tbl_dve, 4 * k + (j - 3) // 2)
                w = 2 * (j % 2)
                three(bank[3 + j % 4][:], lambda a, c: xt[b][:, a, c, :],
                      lambda h, c: wreg[:, h, j // 2, c, w:w + 2, :].rearrange("p r o -> p (r o)")).then_inc(gnn_mm, 1)

            def tile_pe(k, i, b, nxt):
                pe.wait_ge(xt_lo, k + 1)
                if not isinstance(k, int) or k > 0:
                    pe.wait_ge(kv_cp, 2 * k)
                three(bank[1][:], lambda a, c: xt[b][:, a, c, :], lambda h, c: wkvg[:, h, c, 0:2 * C]).then_inc(kv_mm, 1)
                if not isinstance(k, int) or k > 0:
                    pe.wait_ge(hg_pre, k)
                three(bank[2][:, 0:G], lambda a, c: xt[b][:, a, c, :],
                      lambda h, c: wkvg[:, h, c, 2 * C:2 * C + G]).then_inc(hg_mm, 1)
                for j in range(4):
                    relations(k, b, j)
                if nxt:
                    turn(*nxt)
                pe.wait_ge(hg_act, k + 1)
                if not isinstance(k, int) or k > 0:
                    pe.wait_ge(hgt_cp, k)
                apart(pe)
                pe.transpose(bank[7][0:G, 0:P], hgn[:, 1, :], ident[:]).then_inc(hgt_psum, 1)
                for j in range(4, 8):
                    relations(k, b, j)

            pe.wait_ge(w_lo, 4)
            pe.wait_ge(dve_chain, MIXW_READY)
            turn(0, 0)
            tile_pe(0, 0, 0, (1, 1))
            tile_pe(1, 0, 1, (2, 0))
            with pe.Fori(1, NP) as i:
                tile_pe(2 * i, i, 0, (2 * i + 1, 1))
                tile_pe(2 * i + 1, i, 1, (2 * i + 2, 0))
            tile_pe(NT - 1, NP, 0, None)

            pe.wait_ge(kmax_up, NT)
            for c in range(CC):
                mm = pe.transpose(bank[0][:, c * P:(c + 1) * P], kmax[:, c * P:(c + 1) * P], ident[:])
            mm.then_inc(setup_pe, 1)
            pe.wait_ge(k_shift_diag, 2)
            pe.matmul(bank[1][:, 0:C], ones[:], dg[:], start=True, stop=True).then_inc(kmb_mm, 1)

            def contexts(i, first, last):
                for s in range(SLOTS):
                    pe.wait_ge(k_exp, SLOTS * i + s + 1)
                    rows = TAIL if last and s == SLOTS - 1 else P
                    for c in range(CC):
                        mm = pe.matmul(bank[2 + c][:, 0:VW], slot[0:rows, s, c * P:(c + 1) * P],
                                       slot[0:rows, s, C + c * VW:C + (c + 1) * VW],
                                       start=(first and s == 0), stop=(last and s == SLOTS - 1))
                    mm.then_inc(ctx_mm, 1)

            contexts(0, True, False)
            with pe.Fori(1, NT // SLOTS - 1) as i:
                contexts(i, False, False)
            contexts(NT // SLOTS - 1, False, True)
            pe.wait_ge(ctx_done, CC * NB)
            for d in range(CC):
                for c in range(CC):
                    mm = pe.matmul(bank[4][:, d * C + c * P:d * C + (c + 1) * P], wqt[:, c, d * P:(d + 1) * P],
                                   ctxbd[:, c, :], start=True, stop=True)
            mm.then_inc(setup_pe, 1)

            def adds_before(S8, s):
                return 16 * S8 + 8 * (s // 4) + sum(ADDS[q] for q in range(s % 4)) - SKIPPED

            def edges(i, s, first):
                S = 8 * i + s
                if s >= 2 or not first:
                    pe.wait_ge(edge_add, adds_before(i, s - 1) if s >= 1 else adds_before(i - 1, 7))
                pe.wait_ge(sel_done, SUP * S + SUP)
                for j in range(SUP):
                    m = (s % 2) * SUP + j
                    pe.wait_ge(msg_lo, SUP * S + j + 1)
                    pe.matmul(bank[s % 2][:, 0:C], sel[:, m, :], mh[:, m, :], start=(j == 0), stop=False)
                    mm = pe.matmul(bank[s % 2][:, 0:C], sel[:, m, :], ml[:, m, :], start=False, stop=(j == SUP - 1))
                mm.then_inc(edge_mm, 1)

            def mix(p, nt):
                n = nt * P
                pe.wait_ge(xtp_in, 32 * p + 32)
                pe.wait_ge(y_add, 2 * X * p + AHEAD)
                for v in range(CC):
                    mm = three(bank[4][:, v * 256:v * 256 + n], lambda a, c: wqc[:, a, c, v * P:(v + 1) * P],
                               lambda h, c: xtp[:, 0:nt, h * C + c * P:h * C + (c + 1) * P])
                mm.then_inc(mix_pe, 1)
                for v in range(CC):
                    mm = pe.matmul(bank[5][:, v * 256:v * 256 + n], wg2[:, v * P:(v + 1) * P],
                                   hgp[:, 0:nt, :].rearrange("p a n -> p (a n)"), start=True, stop=True)
                mm.then_inc(mix_pe, 1)
                pe.wait_ge(mix_dve, 5 * p + 2)
                for a in range(nt):
                    mm = three(bank[4][:, a * C:(a + 1) * C], lambda h, c: og[:, h, c, a * P:(a + 1) * P],
                               lambda h, c: wproj[:, h, c, :])
                mm.then_inc(mix_pe, 1)

            def prep(p, nt):
                pe.wait_ge(mix_dve, 5 * p + 3)
                for a in range(nt):
                    for c in range(CC):
                        mm = pe.transpose(bank[5][:, c * 256 + a * P:c * 256 + (a + 1) * P],
                                          tn[:, a, c * P:(c + 1) * P], ident[:])
                mm.then_inc(mix_pe, 1)

            def route(p, nt):
                pe.wait_ge(tt_lo, p + 1)
                for a in range(nt):
                    for m in range(2 * CC):
                        h, c = m // CC, m % CC
                        mm = pe.matmul(bank[4][:, a * X:(a + 1) * X], halves(tt[:, h, c, a * P:(a + 1) * P]),
                                       rwt[:, c, :], start=(m == 0), stop=(m == 2 * CC - 1))
                mm.then_inc(mix_pe, 1)
                pe.wait_ge(mix_dve, 5 * p + 5)
                for a in range(nt):
                    mm = pe.transpose(bank[5][0:X, a * P:(a + 1) * P], comb[:, a, :], ident[:])
                mm.then_inc(mix_pe, 1)
                pe.wait_ge(mix_act, 6 * p + 6)
                for a in range(nt):
                    mm = pe.matmul(bank[4][:, a * C:(a + 1) * C], ct[:, a * P:(a + 1) * P], b2s[:],
                                   start=True, stop=True)
                mm.then_inc(mix_pe, 1)

            def layer1(p, e, nt):
                n = nt * P
                T = X * p + e
                if e >= 2:
                    pe.wait_ge(h_act, 2 * T - 2)
                for v in range(CC):
                    mm = three(bank[2 + e % 2][:, v * 256:v * 256 + n],
                               lambda a, c: wreg[:, a, e // WC, c, e % WC, v * P:(v + 1) * P],
                               lambda h, c: tt[:, h, c, 0:n])
                mm.then_inc(h_mm, 1)

            def layer2(p, e, nt):
                T = X * p + e
                pe.wait_ge(h_lo, T + 1)
                if e >= 2:
                    pe.wait_ge(y_add, 2 * X * p + nt * (e - 1) + AHEAD)
                for a in range(nt):
                    mm = three(bank[6 + e % 2][:, a * C:(a + 1) * C], lambda h, c: ht[e % 2][:, h, c, a * P:(a + 1) * P],
                               lambda h, c: wreg[:, h, 2 + e // WC, c, e % WC, :])
                mm.then_inc(y_mm, 1)

            def expert(p, e, nt):
                layer1(p, e, nt)
                if e > 0:
                    layer2(p, e - 1, nt)
                if e == X - 1:
                    layer2(p, e, nt)

            def body(i, groups, first):
                for s in range(groups):
                    edges(i, s, first)
                    if not first:
                        interleaved(s, i - 1, 2, groups, mix, prep, route, expert)

            pe.wait_ge(dve_chain, FLAG_READY)
            far = pe.value_load(flag[0:1, 0:1], min_val=0, max_val=NT * P * R)
            with pe.If(far > 0):
                with pe.Fori(0, ET) as t:
                    pe.wait_ge(far_turn, t + 1)
                    pe.transpose(bank[6][:, 0:P], f_turn, ident[:]).then_inc(far_row, 1)
                    pe.wait_ge(far_msg, t + 1)
                    pe.matmul(bank[7][:, 0:C], f_same, stg[:, 3, :], start=True, stop=True).then_inc(far_mm, 1)

            pe.wait_ge(wqc_done, 1)
            body(0, 8, True)
            with pe.Fori(1, NP) as i:
                body(i, 8, False)
            body(NP, 4, False)
            mix(NP, 1)
            prep(NP, 1)
            route(NP, 1)
            for e in range(X):
                expert(NP, e, 1)


EDGE_PREP = 13
WG1_READY = EDGE_PREP + 7
FLAG_READY = WG1_READY + 2
MIXW_READY = FLAG_READY + 3
CHAIN2 = 18
SKIPPED = 2


def interleaved(s, p, nt, groups, mix, prep, route, expert):
    if s == 1:
        mix(p, nt)
    if s == 2:
        prep(p, nt)
        route(p, nt)
    if groups == 8:
        for e in {3: (0, 1), 4: (2,), 5: (3, 4), 6: (5,), 7: (6, 7)}.get(s, ()):
            expert(p, e, nt)
    elif s == 3:
        for e in range(8):
            expert(p, e, nt)


_INS = ['x', 'src', 'dst', 'edge_type_16', 'edge_weight1', 'L0_gnn_weight', 'L0_mix_Wqkv', 'L0_mix_Wproj',
        'L0_mix_bproj', 'L0_mix_ln_g', 'L0_mix_ln_b', 'L0_mix_Wg1', 'L0_mix_bg1', 'L0_mix_Wg2', 'L0_mix_bg2',
        'L0_ffn_router_w', 'L0_ffn_w1', 'L0_ffn_b1', 'L0_ffn_w2', 'L0_ffn_b2']


def kernel(**inputs):
    import numpy as _np
    import concourse.bacc as _bacc
    from concourse import mybir as _mybir
    from concourse.bass_utils import run_bass_kernel_spmd as _run

    nc = _bacc.Bacc("TRN2", target_bir_lowering=False, num_devices=1, dynamic_dma_scratch_size=8192)
    arrays, args = {}, []
    for name in _INS:
        a = _np.ascontiguousarray(inputs[name])
        arrays[f"in_{name}"] = a
        args.append(nc.dram_tensor(f"in_{name}", a.shape, _mybir.dt.from_np(a.dtype), kind="ExternalInput").ap())
    args.append(nc.dram_tensor("out_x", inputs["x"].shape, _mybir.dt.float32, kind="ExternalOutput").ap())
    gps_layer(nc, *args)
    r = _run(nc, [arrays], core_ids=[0])
    return r.results[0]["out_x"]
```

```python
from contextlib import ExitStack

import concourse.bass as bass
from concourse import mybir

ALU = mybir.AluOpType
ACT = mybir.ActivationFunctionType
AX = mybir.AxisListType
F32 = mybir.dt.float32
F32R = mybir.dt.float32r
I32 = mybir.dt.int32
U32 = mybir.dt.uint32

P = 128
EPS = 1e-5
HI, LO = 0, 1
PASSES = ((HI, HI), (LO, HI), (HI, LO))


class Tally:

    def __init__(self, sem):
        self.sem, self.n = sem, 0

    def inc(self, instruction):
        instruction.then_inc(self.sem, 1)
        self.n = self.n + 1

    def link(self, eng, instruction):
        self.inc(instruction)
        eng.wait_ge(self.sem, self.n)


def gps_layer(nc, x, src, dst, rel, norm, Wr, Wqkv, Wproj, bproj, ln_g, ln_b, Wg1, bg1, Wg2, bg2,
              router_w, w1, b1, w2, b2, out):
    N, C = x.shape
    E = src.shape[0]
    R = Wr.shape[0]
    X = router_w.shape[0]
    G = Wg1.shape[1]
    NT = -(-N // P)
    TAIL = N - (NT - 1) * P
    NP = NT // 2
    CC = C // P
    HEAD = C // 8
    NB = P // HEAD
    EPT = 16
    SUP = 4
    WIN = P
    STEP = 32
    SHIFT = 2
    ET = NT * EPT
    ER = 112
    EB = ET // ER
    PAD_DST = -100000
    VW = P + 1
    KVW = C + CC * VW
    WC = 4
    AHEAD = 2 * X
    FAR = 1 << 19
    SLOTS = 7
    RING = 16
    assert N * 16 == E and NT == 2 * NP + 1 and ET == EB * ER and NT % SLOTS == 0 and CC == 2

    table = nc.dram_tensor("table", [NT * P * R, C], F32).ap()
    kv_d = nc.dram_tensor("kv_d", [NT, P, KVW], F32).ap()
    xt_d = nc.dram_tensor("xt_d", [NT, P, 2 * C], F32).ap()
    hg_d = nc.dram_tensor("hg_d", [NT, G, P], F32).ap()
    dsl_d = nc.dram_tensor("dsl_d", [P, ET], F32).ap()
    gnn_d = nc.dram_tensor("gnn_d", [NT * P, C], F32).ap()

    ctx = ExitStack()
    with ctx:
        def sb(name, shape, dt, where=ctx):
            return where.enter_context(nc.sbuf_tensor(name, shape, dt))

        def sem(name):
            return ctx.enter_context(nc.semaphore(name))

        xres = sb("xres", [P, NT, C], F32)
        wreg = sb("wreg", [P, 2, 4, CC, WC, C], F32R)
        raw = sb("raw", [P, 2, CC * WC * C], F32)
        stg = sb("stg", [P, RING, C], F32)
        wproj = sb("wproj", [P, 2, CC, C], F32R)
        wqc = sb("wqc", [P, 2, CC, C], F32R)
        gidx = sb("gidx", [P, ET], I32)
        dpr = sb("dpr", [P, ET], F32)
        nrm = sb("nrm", [P, ET], F32)
        ident = sb("ident", [P, P], F32)
        ones = sb("ones", [P, P], F32)
        dbl = sb("dbl", [P, 2 * P], F32)
        kmax = sb("kmax", [P, C], F32)
        kmb = sb("kmb", [P, C], F32)
        wg2 = sb("wg2", [G, C], F32)
        cols = sb("cols", [P, 32], F32)
        rwt = sb("rwt", [P, CC, X], F32)
        b2s = sb("b2s", [X, C], F32)
        iota8 = sb("iota8", [P, X], F32)
        small = sb("small", [P, 160], F32)
        smallu = sb("smallu", [P, 2, X], U32)
        flag = sb("flag", [1, 1], I32)
        wqt = sb("wqt", [P, CC, C], F32)

        with ExitStack() as one:
            wkv_raw = sb("wkv_raw", [P, CC, 2 * C], F32, one)
            wq_raw = sb("wq_raw", [P, CC, C], F32, one)
            wp_raw = sb("wp_raw", [P, CC, C], F32, one)
            wg1_raw = sb("wg1_raw", [P, CC, G], F32, one)
            wg1_f = sb("wg1_f", [P, CC, G], F32, one)
            wkvg = sb("wkvg", [P, 2, CC, 2 * C + G], F32R, one)
            xt = [sb(f"xt{b}", [P, 2, CC, P], F32R, one) for b in range(2)]
            xn = [sb(f"xn{b}", [P, C], F32, one) for b in range(2)]
            kvs = [sb(f"kvs{b}", [P, KVW], F32, one) for b in range(2)]
            hgn = sb("hgn", [P, 2, G], F32, one)
            hgt = [sb(f"hgt{b}", [G, P], F32, one) for b in range(2)]
            erow = sb("erow", [ER, 2, EB * P], F32, one)
            vrow = sb("vrow", [24, P], F32, one)
            rwr = sb("rwr", [X, C], F32, one)
            bpb = sb("bpb", [P, C], F32, one)
            g1b = sb("g1b", [P, G], F32, one)
            lnbb = sb("lnbb", [P, CC, P], F32, one)
        two = ctx.enter_context(ExitStack())
        ctxbd = sb("ctxbd", [P, CC, P], F32, two)
        dg = sb("dg", [P, C], F32, two)
        mh = sb("mh", [P, 8, C], F32R, two)
        ml = sb("ml", [P, 8, C], F32R, two)
        sel = sb("sel", [P, 8, P], F32R, two)
        tt = sb("tt", [P, 2, CC, 2 * P], F32R, two)
        xtp = sb("xtp", [P, 2, 2 * C], F32R, two)
        hgp = sb("hgp", [G, 2, P], F32, two)
        ht = [sb(f"ht{b}", [P, 2, CC, 2 * P], F32R, two) for b in range(2)]
        idxcur = sb("idxcur", [P, 2 * EPT], I32, two)

        bank = [ctx.enter_context(nc.psum_tensor(f"bank{b}", [P, 512], F32)) for b in range(8)]

        erow_i = stg[:].rearrange("p a c -> p (a c)")[0:ER, 0:4 * EB * P].rearrange(
            "p (a b) -> p a b", a=4)
        src_r, rel_r, dst_r = (erow_i[:, a, :].bitcast(I32) for a in range(3))
        norm_r = erow_i[:, 3, :]
        lo_i = raw[:, 1, 0:ET].bitcast(I32)
        mask = raw[:, 1, ET:2 * ET]
        dsl = raw[:, 0, 2 * P:2 * P + ET]
        stage = stg[:].rearrange("p (h j) c -> p h (j c)", h=2)
        slot = raw[:].rearrange("p a b -> p (a b)")[:, 0:SLOTS * KVW].rearrange(
            "p (s w) -> p s w", s=SLOTS)
        rs = raw[:].rearrange("p a b -> p (a b)")
        gate = rs[:, 0:512]
        ogf = rs[:, 512:1024]
        tn = rs[:, 1024:1536].rearrange("p (a c) -> p a c", a=2)
        hf = [rs[:, 2048 + 512 * b:2560 + 512 * b] for b in range(2)]
        comb = rs[:, 3072:3072 + 2 * X].rearrange("p (a e) -> p a e", a=2)
        lg = rs[:, 3088:3088 + 2 * X].rearrange("p (a e) -> p a e", a=2)
        top = rs[:, 3104:3104 + 2 * X].rearrange("p (a e) -> p a e", a=2)
        idf = rs[:, 3120:3120 + 2 * X].rearrange("p (a e) -> p a e", a=2)
        cb2 = rs[:, 3136:3136 + 2 * X].rearrange("p (a e) -> p a e", a=2)
        ct = rs[0:X, 3200:3456]
        f_dsl, f_low, f_turn, f_same = rs[:, 0:ET], rs[:, 800:928], rs[:, 928:1056], rs[:, 1056:1184]
        f_dup = rs[:, 1184:1185]
        f_i = rs[:, 1188:1191].bitcast(I32)
        og = xtp[:].rearrange("p a b -> p (a b)").rearrange("p (h c n) -> p h c n", h=2, c=CC)
        b1c = cols[:, 0:2 * X]
        gcol, bcol, bg2c = cols[:, 16:18], cols[:, 18:20], cols[:, 20:22]
        bg2h = small[:, 0:2]
        s2 = small[:, 2:4]
        stats = small[:, 4:16].rearrange("p (a b) -> p a b", a=2)
        mv = small[:, 16:20].rearrange("p (a b) -> p a b", a=2)
        rstd = small[:, 20:22]
        kcol = small[:, 22:24]
        rden = small[:, 24:26]
        cnt = small[:, 26:27]
        dlt = small[:, 28:30]
        th = small[:, 30:32]
        wa = small[:, 32:34]
        wb = small[:, 34:36]
        ve = small[:, 36:38]
        half = small[:, 38:40]
        bg1r = small[0:1, 64:64 + G]

        eng_names = [nc.vector.engine, nc.tensor.engine, nc.gpsimd.engine]
        waited = [sem(f"waited{n}") for n in range(3)]
        consts = sem("consts")
        cleared = sem("cleared")
        edges_in = sem("edges_in")
        vec_in = sem("vec_in")
        mixw_in = sem("mixw_in")
        raw_in = [sem(f"raw_in{b}") for b in range(2)]
        x_in = sem("x_in")
        bp_in = sem("bp_in")
        setup_pe = sem("setup_pe")
        setup_act = sem("setup_act")
        dve_chain = sem("dve_chain")
        w_hi = sem("w_hi")
        w_lo = sem("w_lo")
        xn_ready = sem("xn_ready")
        bias_in = sem("bias_in")
        xt_psum = sem("xt_psum")
        xt_hi = sem("xt_hi")
        xt_lo = sem("xt_lo")
        kv_mm = sem("kv_mm")
        kv_cp = sem("kv_cp")
        kmax_up = sem("kmax_up")
        hg_mm = sem("hg_mm")
        var_ready = sem("var_ready")
        rstd_ready = sem("rstd_ready")
        s2_ready = sem("s2_ready")
        pool_chain = sem("pool_chain")
        var2_ready = sem("var2_ready")
        rstd2_ready = sem("rstd2_ready")
        hg_pre = sem("hg_pre")
        hg_act = sem("hg_act")
        hgt_psum = sem("hgt_psum")
        hgt_cp = sem("hgt_cp")
        gnn_mm = sem("gnn_mm")
        tbl_act = sem("tbl_act")
        tbl_dve = sem("tbl_dve")
        tbl_st = [sem(f"tbl_st{h}") for h in range(2)]
        kv_st = [sem(f"kv_st{b}") for b in range(2)]
        xt_st = [sem(f"xt_st{b}") for b in range(2)]
        hg_st = [sem(f"hg_st{b}") for b in range(2)]
        kv_in = [sem(f"kv_in{s}") for s in range(SLOTS)]
        k_shift = sem("k_shift")
        k_exp = sem("k_exp")
        ctx_mm = sem("ctx_mm")
        idx_cur = sem("idx_cur")
        gath = [sem(f"gath{g}") for g in range(4)]
        msg_hi = sem("msg_hi")
        msg_lo = sem("msg_lo")
        sel_done = sem("sel_done")
        edge_mm = sem("edge_mm")
        edge_add = sem("edge_add")
        xtp_in = sem("xtp_in")
        out_mm, gate_mm, gate_act, og_dve, og_hi, og_lo, proj_mm, tn_dve, tt_mm, tt_hi, tt_lo, logit_mm, gap_dve, \
            gap_act, comb_dve, acc_dve, ct_mm, ct_act, b2_mm, b2_add = (sem(n) for n in (
                "out_mm", "gate_mm", "gate_act", "og_dve", "og_hi", "og_lo", "proj_mm", "tn_dve", "tt_mm", "tt_hi",
                "tt_lo", "logit_mm", "gap_dve", "gap_act", "comb_dve", "acc_dve", "ct_mm", "ct_act", "b2_mm",
                "b2_add"))
        h_mm = sem("h_mm")
        h_act = sem("h_act")
        h_hi = sem("h_hi")
        h_lo = sem("h_lo")
        y_mm = sem("y_mm")
        y_add = sem("y_add")
        out_st = sem("out_st")
        dsl_st = sem("dsl_st")
        far_idx, far_dst, far_turn, far_row, far_uniq, far_in, far_msg, far_mm, far_sum, far_st, far_ld, far_x, \
            far_init = (sem("far_" + n) for n in ("idx", "dst", "turn", "row", "uniq", "in", "msg", "mm", "sum", "st",
                                                  "ld", "x", "init"))
        k_shift_diag = sem("k_shift_diag")
        kmb_mm = sem("kmb_mm")
        ctx_done = sem("ctx_done")
        wqc_done = sem("wqc_done")

        block = ctx.enter_context(nc.Block())

        def halves(t):
            return t.bitcast(F32)

        def edge_window(q):
            first = (STEP * q - WIN // 2) % P
            return dbl[:, (P - first) % P:(P - first) % P + P]

        def window_parts(q):
            return {0: [(64, 128, -1), (0, 64, 0)], 1: [(96, 128, -1), (0, 96, 0)],
                    2: [(0, 128, 0)], 3: [(32, 64, 0), (64, 128, 0), (0, 32, 1)]}[q]

        def apart(eng):
            eng.sem_inc(waited[eng_names.index(eng.engine)], 1)

        def first_phase_over(eng):
            eng.wait_ge(gnn_mm, 8 * NT)
            eng.wait_ge(bias_in, NT)
            eng.wait_ge(kmax_up, NT)
            eng.wait_ge(hgt_cp, NT)
            eng.wait_ge(kv_cp, 2 * NT)
            for b, n in ((0, NP + 1), (1, NP)):
                eng.wait_ge(xt_st[b], 16 * n)
                eng.wait_ge(kv_st[b], 16 * n)
                eng.wait_ge(hg_st[b], 16 * n)

        def adds_before(i, s):
            parts = sum(len(window_parts(q % 4)) for q in range(s))
            if isinstance(i, int) and i == 0 and s < 2:
                return s
            return 16 * i + parts - 2

        @block.sync
        def _(sp):
            sp.wait_ge(cleared, 1)
            for a, v in ((src_r, src), (rel_r, rel), (dst_r, dst), (norm_r, norm.rearrange("e a -> (e a)"))):
                a3 = a.rearrange("p (b e) -> p b e", b=EB)
                first = (ER - SHIFT) * P
                sp.dma_start(a3[SHIFT:ER, 0, :], v[0:first].rearrange("(p e) -> p e", e=P)).then_inc(edges_in, 16)
                mid = first + (EB - 2) * ER * P
                sp.dma_start(a3[:, 1:EB - 1, :], v[first:mid].rearrange("(b p e) -> p b e", p=ER, e=P)).then_inc(edges_in, 16)
                full = (E - mid) // P
                sp.dma_start(a3[0:full, EB - 1, :], v[mid:mid + full * P].rearrange("(p e) -> p e", e=P)).then_inc(edges_in, 16)
                sp.dma_start(a3[full:full + 1, EB - 1, 0:E - mid - full * P],
                             v[mid + full * P:E].rearrange("(a e) -> a e", a=1)).then_inc(edges_in, 16)
            sp.wait_ge(cleared, 2)
            for k, (v, n) in enumerate(((ln_g, CC), (ln_b, CC), (bg2, CC))):
                sp.dma_start(vrow[16 + 2 * k:18 + 2 * k, :], v.rearrange("(a e) -> a e", a=CC)).then_inc(vec_in, 16)
            sp.dma_start(vrow[0:2 * X, :], b1.rearrange("x (a e) -> (x a) e", a=CC)).then_inc(vec_in, 16)
            sp.dma_start(bg1r, bg1.rearrange("(a e) -> a e", a=1)).then_inc(vec_in, 16)
            sp.dma_start(rwr[:], router_w).then_inc(vec_in, 16)
            sp.dma_start(b2s[:], b2).then_inc(vec_in, 16)
            sp.dma_start(wg2[:], Wg2).then_inc(vec_in, 16)
            wqkv_r = Wqkv.rearrange("(c p) n -> p c n", p=P)
            sp.dma_start(wkv_raw[:], wqkv_r[:, :, C:3 * C]).then_inc(mixw_in, 16)
            sp.dma_start(wg1_raw[:], Wg1.rearrange("(c p) n -> p c n", p=P)).then_inc(mixw_in, 16)
            sp.dma_start(wq_raw[:], wqkv_r[:, :, 0:C]).then_inc(mixw_in, 16)
            sp.dma_start(wp_raw[:], Wproj.rearrange("(c p) n -> p c n", p=P)).then_inc(mixw_in, 16)

            def stores(k, i, b):
                sp.wait_ge(xt_lo, k + 1)
                sp.dma_start(xt_d[bass.ds(k, 1)].rearrange("a p f -> (a p) f"),
                             halves(xt[b][:].rearrange("p h c n -> p (h c n)"))).then_inc(xt_st[b], 16)
                sp.wait_ge(kv_cp, 2 * k + 2)
                sp.dma_start(kv_d[bass.ds(k, 1)].rearrange("a p f -> (a p) f"), kvs[b][:]).then_inc(kv_st[b], 16)
                for h in range(2):
                    sp.wait_ge(tbl_act, 4 * k + 2 * h + 2)
                    sp.wait_ge(tbl_dve, 4 * k + 2 * h + 2)
                    sp.dma_start(table_rows[:, bass.ds(k, 1), h * R // 2 * C:(h + 1) * R // 2 * C].rearrange(
                        "p a f -> p (a f)"), stage[:, h, :]).then_inc(tbl_st[h], 16)
                    if h == 0:
                        sp.wait_ge(hgt_cp, k + 1)
                        sp.dma_start(hg_d[bass.ds(k, 1)].rearrange("a p f -> (a p) f"), hgt[b][:]).then_inc(hg_st[b], 16)

            table_rows = table.rearrange("(k p r) c -> p k (r c)", p=P, r=R)
            with sp.Fori(0, NP) as i:
                stores(2 * i, i, 0)
                stores(2 * i + 1, i, 1)
            stores(NT - 1, NP, 0)

            sp.wait_ge(kv_st[0], 16 * (NP + 1))
            sp.wait_ge(kv_st[1], 16 * NP)
            sp.wait_ge(w_lo, 8)

            def load_slots(i):
                for s in range(SLOTS):
                    if not isinstance(i, int) or i > 0:
                        sp.wait_ge(ctx_mm, SLOTS * (i - 1) + s + 1)
                    sp.dma_start(slot[:, s, :], kv_d[bass.ds(SLOTS * i + s, 1)].rearrange("a p f -> (a p) f")
                                 ).then_inc(kv_in[s], 16)

            load_slots(0)
            with sp.Fori(1, NT // SLOTS) as i:
                load_slots(i)

            first_phase_over(sp)

            def load_pair(p, nt):
                if not isinstance(p, int) or p > 0:
                    sp.wait_ge(proj_mm, p)
                sp.dma_start(halves(xtp[:, 0:nt, :]), xt_d[bass.ds(2 * p, nt)].rearrange("a p f -> p a f")).then_inc(xtp_in, 16)
                sp.dma_start(hgp[:, 0:nt, :], hg_d[bass.ds(2 * p, nt)].rearrange("a p f -> p a f")).then_inc(xtp_in, 16)

            def store_pair(p, nt):
                sp.wait_ge(y_add, 2 * X * p + X * nt + AHEAD)
                if nt == 2:
                    sp.dma_start(out[0:NP * 2 * P].rearrange("(a p) c -> p a c", p=P)[:, bass.ds(2 * p, 2), :],
                                 xres[:, bass.ds(2 * p, 2), :]).then_inc(out_st, 16)
                else:
                    sp.dma_start(out[(NT - 1) * P:N, :], xres[0:TAIL, NT - 1, :]).then_inc(out_st, 16)

            load_pair(0, 2)
            load_pair(1, 2)
            with sp.Fori(2, NP) as p:
                load_pair(p, 2)
                store_pair(p - 2, 2)
            load_pair(NP, 1)
            store_pair(NP - 2, 2)
            store_pair(NP - 1, 2)
            store_pair(NP, 1)
            sp.wait_ge(out_st, 16 * (NP + 1))

        @block.gpsimd
        def _(pool):
            pool.memset(ident[:], 0.0).then_inc(consts, 1)
            pool.memset(ones[:], 1.0).then_inc(consts, 1)
            pool.wait_ge(consts, 2)
            pool.affine_select(out=ident[:], in_=ident[:], compare_op=ALU.not_equal, fill=1.0, base=0,
                               pattern=[[-1, P]], channel_multiplier=1).then_inc(consts, 1)
            pool.iota(smallu[:, 0, :].bitcast(I32), pattern=[[1, X]], base=0, channel_multiplier=0).then_inc(consts, 1)
            pool.iota(raw[:, 0, 0:2 * P].bitcast(I32), pattern=[[0, 2], [1, P]], base=0,
                      channel_multiplier=0).then_inc(consts, 1)
            pool.iota(lo_i, pattern=[[STEP, ET // SUP], [0, SUP]], base=-WIN // 2,
                      channel_multiplier=0).then_inc(consts, 1)
            pool.wait_ge(consts, 6)
            pool.tensor_copy(iota8[:], smallu[:, 0, :].bitcast(I32)).then_inc(consts, 1)
            pool.tensor_copy(dbl[:], raw[:, 0, 0:2 * P].bitcast(I32)).then_inc(consts, 1)
            pool.dma_start(bpb[:], bproj.rearrange("(a c) -> a c", a=1).to_broadcast([P, C])).then_inc(bp_in, 16)
            pool.memset(half, -0.5).then_inc(consts, 1)
            pool.wait_ge(consts, 9)
            pool.wait_ge(cleared, 2)
            pool.wait_ge(bp_in, 16)
            pc = Tally(pool_chain)

            def load_x(i):
                pool.dma_start(xres[:, bass.ds(2 * i, 2), :],
                               x[0:NP * 2 * P].rearrange("(a p) c -> p a c", p=P)[:, bass.ds(2 * i, 2), :]
                               ).then_inc(x_in, 16)

            def load_tail():
                pool.dma_start(xres[0:TAIL, NT - 1, :], x[(NT - 1) * P:N, :]).then_inc(x_in, 16)

            def roots(k, i, b):
                pool.wait_ge(var_ready, k + 1)
                if not isinstance(i, int) or i > 0:
                    pool.wait_ge(hg_pre, k - 1)
                apart(pool)
                pc.link(pool, pool.tensor_scalar(ve[:, 0:1], mv[:, b, 1:2], EPS, None, ALU.add))
                pool.tensor_tensor(rstd[:, b:b + 1], ve[:, 0:1], half[:, 0:1], ALU.pow).then_inc(rstd_ready, 1)
                pool.wait_ge(rstd_ready, k + 1)
                apart(pool)
                pc.link(pool, pool.tensor_scalar(ve[:, 1:2], mv[:, b, 1:2], rstd[:, b:b + 1], rstd[:, b:b + 1],
                                                 ALU.mult, ALU.mult))
                apart(pool)
                pc.link(pool, pool.tensor_scalar(ve[:, 1:2], ve[:, 1:2], EPS, None, ALU.add))
                pool.tensor_tensor(s2[:, b:b + 1], ve[:, 1:2], half[:, 0:1], ALU.pow).then_inc(s2_ready, 1)
                pool.wait_ge(xn_ready, k + 1)
                pool.tensor_tensor(xres[:, bass.ds(k, 1), :].rearrange("p a c -> p (a c)"),
                                   xres[:, bass.ds(k, 1), :].rearrange("p a c -> p (a c)"), bpb[:],
                                   ALU.add).then_inc(bias_in, 1)

            load_x(0)
            pool.wait_ge(x_in, 16)
            load_x(1)
            pool.wait_ge(x_in, 32)
            load_x(2)
            roots(0, 0, 0)
            roots(1, 0, 1)
            with pool.Fori(1, NP - 2) as i:
                pc.n = 6 * i
                pool.wait_ge(x_in, 16 * i + 32)
                load_x(i + 2)
                roots(2 * i, i, 0)
                roots(2 * i + 1, i, 1)
            for i in range(NP - 2, NP):
                pc.n = 6 * i
                if i == NP - 2:
                    pool.wait_ge(x_in, 16 * i + 32)
                    load_tail()
                roots(2 * i, i, 0)
                roots(2 * i + 1, i, 1)
            roots(NT - 1, NP, 0)
            first_phase_over(pool)
            pool.wait_ge(tbl_st[0], 16 * NT)
            pool.wait_ge(tbl_st[1], 16 * NT)
            pool.wait_ge(dve_chain, EDGE_PREP)

            pool.wait_ge(dve_chain, FLAG_READY)
            far = pool.value_load(flag[0:1, 0:1], min_val=0, max_val=NT * P * R)
            with pool.If(far > 0):
                pool.wait_ge(wqc_done, 1)
                pool.memset(stg[:, 0:3, :], 0.0).then_inc(far_init, 1)
                pool.memset(f_low, 1.0).then_inc(far_init, 1)
                pool.wait_ge(far_init, 2)
                pool.affine_select(out=f_low, in_=f_low, compare_op=ALU.is_gt, fill=0.0, base=0,
                                   pattern=[[-1, P]], channel_multiplier=1).then_inc(far_init, 1)
                pool.dma_start(f_dsl, dsl_d).then_inc(far_ld, 16)
                with pool.Fori(0, NT) as k:
                    pool.dma_start(gnn_d.rearrange("(k p) c -> p k c", p=P)[:, bass.ds(k, 1), :],
                                   stg[:, 0:1, :]).then_inc(far_ld, 16)
                pool.wait_ge(far_ld, 16 * (NT + 1))
                with pool.Fori(0, ET) as t:
                    pool.tensor_copy(f_i[:, 0:1], gidx[:, bass.ds(t, 1)]).then_inc(far_idx, 1)
                    pool.wait_ge(far_idx, t + 1)
                    apart(pool)
                    pool.indirect_dma_start(stg[:, 0, :], None, table,
                                            bass.IndirectOffsetOnAxis(ap=f_i[:, 0:1], axis=0),
                                            bounds_check=NT * P * R - 1, oob_is_err=False).then_inc(far_in, 16)
                    pool.wait_ge(far_dst, t + 1)
                    apart(pool)
                    pool.indirect_dma_start(stg[:, 1, :], None, gnn_d,
                                            bass.IndirectOffsetOnAxis(ap=f_i[:, 1:2], axis=0),
                                            bounds_check=NT * P - 1, oob_is_err=False).then_inc(far_in, 16)
                    pool.wait_ge(far_sum, t + 1)
                    apart(pool)
                    pool.indirect_dma_start(gnn_d, bass.IndirectOffsetOnAxis(ap=f_i[:, 2:3], axis=0),
                                            stg[:, 2, :], None,
                                            bounds_check=NT * P - 1, oob_is_err=False).then_inc(far_st, 16)
                    pool.wait_ge(far_st, 16 * t + 16)
                with pool.Fori(0, NT) as k:
                    pool.dma_start(stg[:, 3:4, :], gnn_d.rearrange("(k p) c -> p k c", p=P)[:, bass.ds(k, 1), :]
                                   ).then_inc(far_ld, 16)
                    pool.wait_ge(far_x, k + 1)

            def gathers(i, groups):
                for s in range(groups):
                    if s % 4 == 0:
                        for g in range(4):
                            if not isinstance(i, int) or i > 0:
                                pool.wait_ge(gath[g], 64 * (2 * i - 1 + s // 4))
                        pool.tensor_copy(idxcur[:, s * SUP:(s + 4) * SUP],
                                         gidx[:, bass.ds((8 * i + s) * SUP, 4 * SUP)]).then_inc(idx_cur, 1)
                        pool.wait_ge(idx_cur, 2 * i + s // 4 + 1)
                    if s >= 4 or not isinstance(i, int) or i > 0:
                        pool.wait_ge(msg_lo, SUP * (8 * i + s - 3))
                        apart(pool)
                    for j in range(SUP):
                        pool.indirect_dma_start(
                            stg[:, (s % 4) * SUP + j, :], None, table,
                            bass.IndirectOffsetOnAxis(ap=idxcur[:, s * SUP + j:s * SUP + j + 1], axis=0),
                            bounds_check=NT * P * R - 1, oob_is_err=False).then_inc(gath[s % 4], 16)
                    if s == 0 and not (isinstance(i, int) and i < 2):
                        roots2(i - 2, 2)

            def roots2(p, nt):
                pool.wait_ge(var2_ready, 2 * p + nt)
                apart(pool)
                pc.link(pool, pool.tensor_scalar(ve[:, 0:nt], mv[:, 0:nt, 1], EPS, None, ALU.add))
                pool.tensor_tensor(rstd[:, 0:nt], ve[:, 0:nt], half[:, 0:nt], ALU.pow).then_inc(rstd2_ready, 1)

            gathers(0, 8)
            base = pc.n
            gathers(1, 8)
            with pool.Fori(2, NP) as i:
                pc.n = base + i - 2
                gathers(i, 8)
            pc.n = base + NP - 2
            gathers(NP, 4)
            roots2(NP - 1, 2)
            roots2(NP, 1)

        @block.scalar
        def _(act):
            chunks = [Wr[WC * n:WC * n + WC] for n in range(4)] + \
                     [w[WC * n:WC * n + WC] for w in (w1, w2) for n in range(2)]

            def load_chunk(n):
                for c in range(CC):
                    act.dma_start(raw[:, n % 2, :].rearrange("p (c r o) -> p c r o", c=CC, r=WC)[:, c],
                                  chunks[n].rearrange("r (c p) o -> p c r o", p=P)[:, c]).then_inc(raw_in[n % 2], 16)

            def split_hi(n):
                act.wait_ge(raw_in[n % 2], 32 * (n // 2 + 1))
                act.copy(wreg[:, HI, n % 4].rearrange("p c r o -> p (c r o)"), raw[:, n % 2, :]).then_inc(w_hi, 1)

            act.wait_ge(dve_chain, EDGE_PREP)
            act.dma_start(dsl_d, dsl).then_inc(dsl_st, 16)
            load_chunk(1)
            act.wait_ge(dsl_st, 16)
            load_chunk(0)
            act.wait_ge(setup_pe, 3)
            act.copy(nrm[:, 0:4 * ER], bank[4][:, 0:4 * ER]).then_inc(setup_act, 1)
            act.copy(nrm[:, 4 * ER:ET], bank[5][:, 0:ET - 4 * ER]).then_inc(setup_act, 1)
            act.wait_ge(mixw_in, 64)
            act.copy(wkvg[:, HI, :, 0:2 * C], wkv_raw[:]).then_inc(setup_act, 1)
            act.copy(wproj[:, HI], wp_raw[:]).then_inc(setup_act, 1)
            act.wait_ge(dve_chain, WG1_READY)
            act.copy(wkvg[:, HI, :, 2 * C:2 * C + G], wg1_f[:]).then_inc(setup_act, 1)
            act.wait_ge(setup_pe, 4)
            act.copy(wqt[:].rearrange("p c n -> p (c n)"), bank[6][:]).then_inc(setup_act, 1)
            for n in range(4):
                split_hi(n)
                act.wait_ge(w_lo, n + 1)
                load_chunk(n + 2)

            def table_out(k, j):
                if j % 4 == 0:
                    if not isinstance(k, int) or k > 0:
                        act.wait_ge(tbl_st[j // 4], 16 * k)
                act.wait_ge(gnn_mm, 8 * k + j + 1)
                act.copy(stage[:, j // 4, (j % 4) * 512:(j % 4 + 1) * 512], bank[3 + j % 4][:]).then_inc(tbl_act, 1)

            def xt_high(k, i, b):
                act.wait_ge(xt_psum, k + 1)
                if not isinstance(i, int) or i > 0:
                    act.wait_ge(gnn_mm, 8 * k - 8)
                    act.wait_ge(xt_st[b], 16 * i)
                act.copy(xt[b][:, HI].rearrange("p c n -> p (c n)"), bank[0][:, 0:C]).then_inc(xt_hi, 1)

            def tile_act(k, i, b, more, nxt):
                act.wait_ge(kv_mm, k + 1)
                if not isinstance(i, int) or i > 0:
                    act.wait_ge(kv_st[b], 16 * i)
                    act.wait_ge(kmax_up, k - 1)
                act.copy(kvs[b][:, 0:C], bank[1][:, 0:C]).then_inc(kv_cp, 1)
                act.copy(kvs[b][:, C:].rearrange("p (c w) -> p c w", c=CC)[:, :, 0:P],
                         bank[1][:, C:2 * C].rearrange("p (c w) -> p c w", c=CC)).then_inc(kv_cp, 1)
                act.wait_ge(hg_pre, k + 1)
                act.activation(hgn[:, 1, :], hgn[:, 0, :], ACT.Gelu).then_inc(hg_act, 1)
                table_out(k, 0)
                table_out(k, 2)
                if more:
                    xt_high(*nxt)
                act.wait_ge(hgt_psum, k + 1)
                if not isinstance(i, int) or i > 0:
                    act.wait_ge(hg_st[b], 16 * i)
                act.copy(hgt[b][:], bank[7][0:G, 0:P]).then_inc(hgt_cp, 1)
                table_out(k, 4)
                table_out(k, 6)

            xt_high(0, 0, 0)
            tile_act(0, 0, 0, True, (1, 0, 1))
            tile_act(1, 0, 1, True, (2, 1, 0))
            with act.Fori(1, NP) as i:
                tile_act(2 * i, i, 0, True, (2 * i + 1, i, 1))
                tile_act(2 * i + 1, i, 1, True, (2 * i + 2, i + 1, 0))
            tile_act(NT - 1, NP, 0, False, None)

            for n in range(4, 8):
                if n == 4:
                    act.wait_ge(gnn_mm, 8 * NT)
                split_hi(n)
                if n < 6:
                    act.wait_ge(w_lo, n + 1)
                    load_chunk(n + 2)

            def exps(i):
                for s in range(SLOTS):
                    act.wait_ge(k_shift, SLOTS * i + s + 1)
                    act.activation(slot[:, s, 0:C], slot[:, s, 0:C], ACT.Exp).then_inc(k_exp, 1)

            with act.Fori(0, NT // SLOTS) as i:
                exps(i)
            act.wait_ge(setup_pe, 8)
            act.mul(wqc[:, HI].rearrange("p c n -> p (c n)"), bank[4][:], 0.5).then_inc(setup_act, 1)

            first_phase_over(act)

            def msgs(i, s, first):
                S = 8 * i + s
                act.wait_ge(gath[s % 4], 64 * (2 * i + s // 4 + 1))
                if s >= 2 or not first:
                    act.wait_ge(edge_mm, S - 1)
                for j in range(SUP):
                    act.activation(mh[:, (s % 2) * SUP + j, :], stg[:, (s % 4) * SUP + j, :], ACT.Copy,
                                   scale=nrm[:, bass.ds(SUP * S + j, 1)]).then_inc(msg_hi, 1)

            def cols2(t, n):
                return t.rearrange("p (c n) -> p c n", c=CC)[:, :, 0:n]

            def GATE(p, nt):
                act.wait_ge(gate_mm, p + 1)
                for c in range(CC):
                    act.activation(gate[:, c * 256:c * 256 + nt * P], bank[5][:, c * 256:c * 256 + nt * P], ACT.Tanh,
                                   bias=bg2h[:, c:c + 1], scale=0.5).then_inc(gate_act, 1)
                act.wait_ge(og_dve, p + 1)
                act.copy(og[:, HI, :, 0:nt * P], cols2(ogf, nt * P)).then_inc(og_hi, 1)

            def TURN(p, nt):
                act.wait_ge(tt_mm, p + 1)
                act.copy(tt[:, HI, :, 0:nt * P], cols2(bank[5][:], nt * P)).then_inc(tt_hi, 1)

            def LOGIT(p, nt):
                act.wait_ge(gap_dve, p + 1)
                act.activation(th[:, 0:nt], dlt[:, 0:nt], ACT.Tanh, scale=0.5).then_inc(gap_act, 1)

            def COMBT(p, nt):
                act.wait_ge(ct_mm, p + 1)
                act.copy(ct[:, 0:nt * P], bank[6][0:X, 0:nt * P]).then_inc(ct_act, 1)

            def LAYER1(p, nt, e):
                T = X * p + e
                act.wait_ge(h_mm, T + 1)
                if e == 0:
                    act.wait_ge(y_add, 2 * X * p + AHEAD)
                if e >= 2:
                    act.wait_ge(h_lo, T - 1)
                for c in range(CC):
                    act.activation(hf[e % 2][:, c * 256:c * 256 + nt * P], bank[2 + e % 2][:, c * 256:c * 256 + nt * P],
                                   ACT.Gelu, bias=b1c[:, 2 * e + c:2 * e + c + 1]).then_inc(h_act, 1)
                act.wait_ge(h_act, 2 * T + 2)
                if e >= 2:
                    act.wait_ge(y_mm, T - 1)
                act.copy(ht[e % 2][:, HI, :, 0:nt * P], cols2(hf[e % 2], nt * P)).then_inc(h_hi, 1)

            def slot_of(i, s, groups, p1, n1, p2, n2):
                if s < groups:
                    msgs(i, s, isinstance(i, int) and i == 0)
                in_slot(s, p1, n1, p2, n2, GATE=GATE, TURN=TURN, LOGIT=LOGIT, COMBT=COMBT, LAYER1=LAYER1)

            run(act, slot_of, NP)

        @block.vector
        def _(dve):
            ch = Tally(dve_chain)
            dve.sem_inc(y_add, AHEAD)
            dve.memset(src_r, 0)
            dve.memset(rel_r, 0)
            dve.memset(dst_r, PAD_DST)
            dve.memset(norm_r, 0.0).then_inc(cleared, 1)
            dve.memset(vrow[:], 0.0)
            dve.memset(xres[96:P, NT - 1, :], 0.0)
            for b in range(2):
                for c in range(CC):
                    dve.memset(kvs[b][:, C + c * VW + P:C + c * VW + VW], 1.0)
            dve.memset(kmax[:], -3.0e38).then_inc(cleared, 1)
            dve.wait_ge(cleared, 2)

            dve.wait_ge(edges_in, 16 * 16)
            ch.inc(dve.scalar_tensor_tensor(out=erow[:, 0, :], in0=src_r, scalar=float(R), in1=rel_r,
                                            op0=ALU.mult, op1=ALU.add))
            ch.inc(dve.tensor_copy(erow[:, 1, :], dst_r))
            dve.wait_ge(setup_pe, 1)
            ch.inc(dve.tensor_copy(gidx[:, 0:4 * ER], bank[0][:, 0:4 * ER]))
            ch.inc(dve.tensor_copy(gidx[:, 4 * ER:ET], bank[1][:, 0:ET - 4 * ER]))
            dve.wait_ge(consts, 8)
            dve.wait_ge(setup_pe, 2)
            ch.inc(dve.tensor_tensor(dpr[:, 0:4 * ER], bank[2][:, 0:4 * ER], lo_i[:, 0:4 * ER], ALU.subtract))
            ch.link(dve, dve.tensor_tensor(dpr[:, 4 * ER:ET], bank[3][:, 0:ET - 4 * ER], lo_i[:, 4 * ER:ET], ALU.subtract))
            ch.link(dve, dve.tensor_scalar(mask, dpr[:], 0.0, None, ALU.is_lt))
            ch.link(dve, dve.scalar_tensor_tensor(out=mask, in0=dpr[:], scalar=PAD_DST / 2.0, in1=mask,
                                                  op0=ALU.is_gt, op1=ALU.mult))
            ch.link(dve, dve.scalar_tensor_tensor(out=mask, in0=dpr[:], scalar=WIN - 1.0, in1=mask,
                                                  op0=ALU.is_gt, op1=ALU.add))
            ch.link(dve, dve.tensor_reduce(cnt, mask, AX.X, ALU.add))
            ch.link(dve, dve.tensor_tensor(dsl, dpr[:], lo_i, ALU.add))
            ch.link(dve, dve.scalar_tensor_tensor(out=dsl, in0=dsl, scalar=-float(FAR), in1=mask, op0=ALU.add,
                                                  op1=ALU.mult))
            ch.link(dve, dve.tensor_scalar(dsl, dsl, float(FAR), None, ALU.add))
            assert ch.n == EDGE_PREP
            dve.wait_ge(setup_pe, 5)
            ch.inc(dve.tensor_copy(cols[:, 0:22], bank[7][:, 0:22]))
            ch.link(dve, dve.tensor_copy(rwt[:].rearrange("p c x -> p (c x)"), bank[7][:, 32:32 + CC * X]))
            dve.wait_ge(mixw_in, 64)
            dve.wait_ge(vec_in, 8 * 16)
            ch.inc(dve.tensor_scalar(bg2h, bg2c, 0.5, None, ALU.mult))
            for c in range(CC):
                ch.inc(dve.tensor_scalar(wg1_f[:, c, :], wg1_raw[:, c, :], gcol[:, c:c + 1], None, ALU.mult))
                ch.inc(dve.tensor_scalar(lnbb[:, c, :], ones[:], bcol[:, c:c + 1], None, ALU.mult))
            dve.wait_ge(dve_chain, ch.n)
            assert ch.n == WG1_READY
            dve.wait_ge(setup_pe, 6)
            ch.inc(dve.tensor_copy(g1b[:], bank[5][:, 0:G]))
            ch.inc(dve.tensor_copy(flag[:], bank[5][0:1, G:G + 1]))
            assert ch.n == FLAG_READY
            dve.wait_ge(setup_act, 5)
            ch.inc(dve.tensor_tensor(wkvg[:, LO, :, 0:2 * C], wkv_raw[:], halves(wkvg[:, HI, :, 0:2 * C]), ALU.subtract))
            ch.inc(dve.tensor_tensor(wkvg[:, LO, :, 2 * C:2 * C + G], wg1_f[:],
                                     halves(wkvg[:, HI, :, 2 * C:2 * C + G]), ALU.subtract))
            ch.inc(dve.tensor_tensor(wproj[:, LO], wp_raw[:], halves(wproj[:, HI]), ALU.subtract))
            assert ch.n == MIXW_READY

            def split_lo(n):
                dve.wait_ge(w_hi, n + 1)
                dve.tensor_tensor(wreg[:, LO, n % 4].rearrange("p c r o -> p (c r o)"), raw[:, n % 2, :],
                                  halves(wreg[:, HI, n % 4].rearrange("p c r o -> p (c r o)")),
                                  ALU.subtract).then_inc(w_lo, 1)

            for n in range(4):
                split_lo(n)

            def layer_norm(k, i, b):
                dve.wait_ge(x_in, 16 * i + 16)
                if not isinstance(i, int) or i > 0:
                    dve.wait_ge(xt_psum, k - 1)
                xk = xres[:, bass.ds(k, 1), :].rearrange("p a c -> p (a c)")
                apart(dve)
                ch.link(dve, dve.bn_stats(stats[:, b, :], xk))
                if not isinstance(i, int) or i > 0:
                    dve.wait_ge(s2_ready, k - 1)
                apart(dve)
                dve.bn_aggr(mv[:, b, :], stats[:, b, :]).then_inc(var_ready, 1)
                dve.wait_ge(rstd_ready, k + 1)
                dve.tensor_scalar(xn[b][:], xk, mv[:, b, 0:1], rstd[:, b:b + 1], ALU.subtract,
                                  ALU.mult).then_inc(xn_ready, 1)

            def table_out(k, j):
                if j % 4 == 1:
                    if not isinstance(k, int) or k > 0:
                        dve.wait_ge(tbl_st[j // 4], 16 * k)
                dve.wait_ge(gnn_mm, 8 * k + j + 1)
                dve.tensor_copy(stage[:, j // 4, (j % 4) * 512:(j % 4 + 1) * 512], bank[3 + j % 4][:]).then_inc(tbl_dve, 1)

            def xt_low(k, b):
                dve.wait_ge(xt_hi, k + 1)
                dve.tensor_tensor(xt[b][:, LO].rearrange("p c n -> p (c n)"), bank[0][:, 0:C],
                                  halves(xt[b][:, HI].rearrange("p c n -> p (c n)")), ALU.subtract).then_inc(xt_lo, 1)

            def tile_dve(k, i, b, rows, nxt):
                dve.wait_ge(hg_mm, k + 1)
                dve.wait_ge(s2_ready, k + 1)
                if not isinstance(k, int) or k > 0:
                    dve.wait_ge(hg_act, k)
                dve.scalar_tensor_tensor(out=hgn[:, 0, :], in0=bank[2][:, 0:G], scalar=s2[:, b:b + 1], in1=g1b[:],
                                         op0=ALU.mult, op1=ALU.add).then_inc(hg_pre, 1)
                if nxt:
                    layer_norm(*nxt)
                table_out(k, 1)
                table_out(k, 3)
                if nxt:
                    xt_low(nxt[0], nxt[2])
                dve.wait_ge(kv_cp, 2 * k + 2)
                if not isinstance(k, int) or k > 0:
                    dve.wait_ge(kmax_up, k)
                dve.tensor_tensor(kmax[0:rows], kmax[0:rows], kvs[b][0:rows, 0:C], ALU.max).then_inc(kmax_up, 1)
                table_out(k, 5)
                table_out(k, 7)

            layer_norm(0, 0, 0)
            xt_low(0, 0)
            tile_dve(0, 0, 0, P, (1, 0, 1))
            tile_dve(1, 0, 1, P, (2, 1, 0))
            base = ch.n
            with dve.Fori(1, NP) as i:
                ch.n = base + 2 * (i - 1)
                tile_dve(2 * i, i, 0, P, (2 * i + 1, i, 1))
                tile_dve(2 * i + 1, i, 1, P, (2 * i + 2, i + 1, 0))
            ch.n = base + 2 * (NP - 1)
            tile_dve(NT - 1, NP, 0, TAIL, None)

            first_phase_over(dve)
            dve.wait_ge(setup_pe, 7)
            ch.link(dve, dve.tensor_reduce(kcol, bank[0][:, 0:C].rearrange("p (c n) -> p c n", c=CC), AX.X, ALU.max))
            for c in range(CC):
                ins = dve.tensor_scalar(dg[:, c * P:(c + 1) * P], ident[:], kcol[:, c:c + 1], None, ALU.mult)
                ins.then_inc(k_shift_diag, 1)
            dve.wait_ge(kmb_mm, 1)
            ch.link(dve, dve.tensor_copy(kmb[:], bank[1][:, 0:C]))
            for n in range(4, 8):
                split_lo(n)

            def shifts(i):
                for s in range(SLOTS):
                    dve.wait_ge(kv_in[s], 16 * i + 16)
                    dve.tensor_tensor(slot[:, s, 0:C], slot[:, s, 0:C], kmb[:], ALU.subtract).then_inc(k_shift, 1)

            with dve.Fori(0, NT // SLOTS) as i:
                shifts(i)

            ch.link(dve, dve.memset(ctxbd[:], 0.0))
            dve.wait_ge(ctx_mm, NT)
            for c in range(CC):
                ch.inc(dve.reciprocal(rden[:, c:c + 1], bank[2 + c][:, P:P + 1]))
            dve.wait_ge(dve_chain, ch.n)
            for c in range(CC):
                for h in range(NB):
                    d = slice(h * HEAD, (h + 1) * HEAD)
                    dve.tensor_scalar(ctxbd[d, c, d], bank[2 + c][d, d], rden[d, c:c + 1], None,
                                      ALU.mult).then_inc(ctx_done, 1)
            dve.wait_ge(setup_act, 7)
            dve.scalar_tensor_tensor(out=wqc[:, LO].rearrange("p c n -> p (c n)"), in0=bank[4][:], scalar=0.5,
                                     in1=halves(wqc[:, HI].rearrange("p c n -> p (c n)")), op0=ALU.mult,
                                     op1=ALU.subtract).then_inc(wqc_done, 1)
            dve.wait_ge(dve_chain, FLAG_READY)
            far = dve.value_load(flag[0:1, 0:1], min_val=0, max_val=NT * P * R)
            with dve.If(far > 0):
                dve.wait_ge(far_init, 3)
                dve.wait_ge(far_ld, 16 * (NT + 1))
                fch = Tally(dve_chain)
                with dve.Fori(0, ET) as t:
                    fch.n = ch.n + 3 * t
                    dcol = f_dsl[:, bass.ds(t, 1)]
                    dve.wait_ge(far_idx, t + 1)
                    dve.tensor_copy(f_i[:, 1:2], dcol).then_inc(far_dst, 1)
                    dve.tensor_scalar(f_turn, ones[:], dcol, None, ALU.mult).then_inc(far_turn, 1)
                    dve.wait_ge(far_row, t + 1)
                    fch.link(dve, dve.tensor_scalar(f_same, bank[6][:, 0:P], dcol, None, ALU.is_equal))
                    fch.link(dve, dve.tensor_tensor(f_turn, f_same, f_low, ALU.mult))
                    fch.link(dve, dve.tensor_reduce(f_dup, f_turn, AX.X, ALU.add))
                    dve.scalar_tensor_tensor(out=f_i[:, 2:3], in0=f_dup, scalar=float(FAR), in1=dcol,
                                             op0=ALU.mult, op1=ALU.add).then_inc(far_uniq, 1)
                    dve.wait_ge(far_in, 32 * t + 32)
                    dve.tensor_scalar(stg[:, 3, :], stg[:, 0, :], nrm[:, bass.ds(t, 1)], None,
                                      ALU.mult).then_inc(far_msg, 1)
                    dve.wait_ge(far_mm, t + 1)
                    dve.wait_ge(far_uniq, t + 1)
                    dve.tensor_tensor(stg[:, 2, :], bank[7][:, 0:C], stg[:, 1, :], ALU.add).then_inc(far_sum, 1)
                with dve.Fori(0, NT) as k:
                    dve.wait_ge(far_ld, 16 * k + 16 * (NT + 2))
                    xk = xres[:, bass.ds(k, 1), :]
                    dve.tensor_tensor(xk, xk, stg[:, 3:4, :], ALU.add).then_inc(far_x, 1)
            with dve.Else():
                dve.sem_inc(dve_chain, 3 * ET)
            ch.n = ch.n + 3 * ET

            def msgs(i, s, first):
                S = 8 * i + s
                if s >= 2 or not first:
                    dve.wait_ge(edge_mm, S - 1)
                for j in range(SUP):
                    dve.tensor_scalar(sel[:, (s % 2) * SUP + j, :], edge_window(s % 4), dpr[:, bass.ds(SUP * S + j, 1)],
                                      None, ALU.is_equal).then_inc(sel_done, 1)
                for j in range(SUP):
                    m = (s % 2) * SUP + j
                    dve.wait_ge(msg_hi, SUP * S + j + 1)
                    dve.scalar_tensor_tensor(out=ml[:, m, :], in0=stg[:, (s % 4) * SUP + j, :],
                                             scalar=nrm[:, bass.ds(SUP * S + j, 1)], in1=halves(mh[:, m, :]),
                                             op0=ALU.mult, op1=ALU.subtract).then_inc(msg_lo, 1)

            def adds(i, s):
                dve.wait_ge(edge_mm, 8 * i + s + 1)
                if not (isinstance(i, int) and i == 0 and s == 0):
                    dve.wait_ge(edge_add, adds_before(i, s))
                for a, b, t in window_parts(s % 4):
                    if isinstance(i, int) and not 0 <= 2 * i + s // 4 + t < NT:
                        continue
                    k = 2 * i + s // 4 + t
                    xk = xres[a:b, bass.ds(k, 1), :].rearrange("p a c -> p (a c)")
                    dve.tensor_tensor(xk, bank[s % 2][a:b, 0:C], xk, ALU.add).then_inc(edge_add, 1)

            def cols2(t, n):
                return t.rearrange("p (c n) -> p c n", c=CC)[:, :, 0:n]

            def GATE(p, nt):
                n = nt * P
                dve.wait_ge(gate_act, 2 * p + 2)
                dve.wait_ge(out_mm, p + 1)
                dve.scalar_tensor_tensor(out=cols2(ogf, n), in0=cols2(gate, n), scalar=1.0,
                                         in1=cols2(bank[4][:], n), op0=ALU.add, op1=ALU.mult).then_inc(og_dve, 1)

            def GATE_LOW(p, nt):
                dve.wait_ge(og_hi, p + 1)
                dve.tensor_tensor(og[:, LO, :, 0:nt * P], cols2(ogf, nt * P),
                                  halves(og[:, HI, :, 0:nt * P]), ALU.subtract).then_inc(og_lo, 1)

            def STATS(p, nt):
                xp = xres[:, bass.ds(2 * p, nt), :]
                dve.wait_ge(proj_mm, p + 1)
                ch.link(dve, dve.tensor_tensor(xp, bank[4][:].rearrange("p (a c) -> p a c", a=2)[:, 0:nt], xp, ALU.add))
                apart(dve)
                for a in range(nt):
                    ch.inc(dve.bn_stats(stats[:, a, :], xres[:, bass.ds(2 * p + a, 1), :].rearrange("p a c -> p (a c)")))
                dve.wait_ge(dve_chain, ch.n)
                apart(dve)
                for a in range(nt):
                    dve.bn_aggr(mv[:, a, :], stats[:, a, :]).then_inc(var2_ready, 1)

            def NORM(p, nt):
                dve.wait_ge(rstd2_ready, p + 1)
                for a in range(nt):
                    dve.tensor_scalar(tn[:, a, :], xres[:, bass.ds(2 * p + a, 1), :].rearrange("p a c -> p (a c)"),
                                      mv[:, a, 0:1], rstd[:, a:a + 1], ALU.subtract, ALU.mult).then_inc(tn_dve, 1)

            def TURN_LOW(p, nt):
                dve.wait_ge(tt_hi, p + 1)
                dve.tensor_tensor(tt[:, LO, :, 0:nt * P], cols2(bank[5][:], nt * P),
                                  halves(tt[:, HI, :, 0:nt * P]), ALU.subtract).then_inc(tt_lo, 1)

            def LOGIT(p, nt):
                dve.wait_ge(logit_mm, p + 1)
                ch.link(dve, dve.tensor_copy(lg[:, 0:nt], bank[4][:, 0:nt * X].rearrange("p (a e) -> p a e", a=nt)))
                apart(dve)
                for a in range(nt):
                    ch.inc(dve.max(top[:, a, :], lg[:, a, :]))
                dve.wait_ge(dve_chain, ch.n)
                apart(dve)
                dve.tensor_tensor(dlt[:, 0:nt], top[:, 0:nt, 0], top[:, 0:nt, 1], ALU.subtract).then_inc(gap_dve, 1)
                for a in range(nt):
                    ch.inc(dve.max_index(smallu[:, a, :], top[:, a, :], lg[:, a, :]))

            def COMB(p, nt):
                dve.wait_ge(dve_chain, ch.n)
                ch.inc(dve.tensor_copy(idf[:, 0:nt], smallu[:, 0:nt]))
                dve.wait_ge(gap_act, p + 1)
                ch.inc(dve.tensor_scalar(wa[:, 0:nt], th[:, 0:nt], 0.5, 0.5, ALU.mult, ALU.add))
                ch.inc(dve.tensor_scalar(wb[:, 0:nt], th[:, 0:nt], -0.5, 0.5, ALU.mult, ALU.add))
                dve.wait_ge(dve_chain, ch.n)
                for a in range(nt):
                    ch.inc(dve.tensor_scalar(cb2[:, a, :], iota8[:], idf[:, a, 0:1], wa[:, a:a + 1], ALU.is_equal, ALU.mult))
                    ch.inc(dve.tensor_scalar(lg[:, a, :], iota8[:], idf[:, a, 1:2], wb[:, a:a + 1], ALU.is_equal, ALU.mult))
                dve.wait_ge(dve_chain, ch.n)
                dve.wait_ge(y_add, 2 * X * p + AHEAD)
                dve.tensor_tensor(comb[:, 0:nt], cb2[:, 0:nt], lg[:, 0:nt], ALU.add).then_inc(comb_dve, 1)
                xp = xres[:, bass.ds(2 * p, nt), :]
                dve.tensor_tensor(xp, xp, tn[:, 0:nt], ALU.add).then_inc(acc_dve, 1)

            def BIAS2(p, nt):
                dve.wait_ge(b2_mm, p + 1)
                dve.wait_ge(acc_dve, p + 1)
                xp = xres[:, bass.ds(2 * p, nt), :]
                dve.tensor_tensor(xp, bank[7][:].rearrange("p (a c) -> p a c", a=2)[:, 0:nt], xp,
                                  ALU.add).then_inc(b2_add, 1)

            def LOW(p, nt, e):
                n = nt * P
                dve.wait_ge(h_hi, X * p + e + 1)
                dve.tensor_tensor(ht[e % 2][:, LO, :, 0:n], cols2(hf[e % 2], n),
                                  halves(ht[e % 2][:, HI, :, 0:n]), ALU.subtract).then_inc(h_lo, 1)

            def ADD(p, nt, e):
                dve.wait_ge(y_mm, X * p + e + 1)
                if e == 0:
                    dve.wait_ge(b2_add, p + 1)
                else:
                    dve.wait_ge(y_add, 2 * X * p + nt * e + AHEAD)
                for a in range(nt):
                    xk = xres[:, bass.ds(2 * p + a, 1), :].rearrange("p a c -> p (a c)")
                    dve.scalar_tensor_tensor(out=xk, in0=bank[6 + e % 2][:, a * C:(a + 1) * C],
                                             scalar=comb[:, a, e:e + 1], in1=xk, op0=ALU.mult,
                                             op1=ALU.add).then_inc(y_add, 1)

            def slot_of(i, s, groups, p1, n1, p2, n2):
                if not isinstance(i, int) and s == 0:
                    ch.n = ch.base + CHAIN2 * (i - 2)
                if s < groups:
                    msgs(i, s, isinstance(i, int) and i == 0)
                if s == 0 and not (isinstance(i, int) and i == 0):
                    if groups:
                        adds(i - 1, 7)
                elif 0 < s <= groups:
                    adds(i, s - 1)
                in_slot(s, p1, n1, p2, n2, GATE=GATE, GATE_LOW=GATE_LOW, STATS=STATS, NORM=NORM, TURN_LOW=TURN_LOW,
                        LOGIT=LOGIT, COMB=COMB, BIAS2=BIAS2, LOW=LOW, ADD=ADD)

            def before_loop():
                ch.base = ch.n

            def after_loop():
                ch.n = ch.base + CHAIN2 * (NP - 2)

            run(dve, slot_of, NP, before_loop, after_loop)

        @block.tensor
        def _(pe):
            pe.wait_ge(consts, 8)
            for a, (rows, at, need) in enumerate(((erow[:, 0, :], 0, 1), (erow[:, 1, :], 2, 2), (norm_r, 4, 2))):
                pe.wait_ge(dve_chain, need)
                for j in range(EB):
                    mm = pe.transpose(bank[at + j // 4][:, (j % 4) * ER:(j % 4 + 1) * ER],
                                      rows[:, j * P:(j + 1) * P], ident[0:ER, 0:ER])
                mm.then_inc(setup_pe, 1)
            pe.wait_ge(mixw_in, 64)
            for c in range(CC):
                for d in range(CC):
                    mm = pe.transpose(bank[6][:, c * C + d * P:c * C + (d + 1) * P],
                                      wq_raw[:, d, c * P:(c + 1) * P], ident[:])
            mm.then_inc(setup_pe, 1)
            pe.wait_ge(vec_in, 8 * 16)
            pe.transpose(bank[7][:, 0:22], vrow[0:22, :], ident[0:22, 0:22])
            for c in range(CC):
                mm = pe.transpose(bank[7][:, 32 + c * X:32 + (c + 1) * X], rwr[:, c * P:(c + 1) * P], ident[0:X, 0:X])
            mm.then_inc(setup_pe, 1)
            pe.wait_ge(dve_chain, WG1_READY)
            pe.wait_ge(setup_act, 2)
            for c in range(CC):
                pe.matmul(bank[5][:, 0:G], lnbb[:, c, :], wg1_raw[:, c, :], start=(c == 0), stop=False)
            pe.matmul(bank[5][:, 0:G], ones[0:1, :], bg1r, start=False, stop=True)
            pe.matmul(bank[5][0:1, G:G + 1], cnt, ones[:, 0:1], start=True, stop=True).then_inc(setup_pe, 1)

            def three(dst, stat, mov, k0=0, chunks=CC):
                n = 0
                for c in range(chunks):
                    for a, b in PASSES:
                        mm = pe.matmul(dst, stat(a, c), mov(b, c), start=(n == 0), stop=(n == 3 * chunks - 1))
                        n += 1
                return mm

            def turn(k, b):
                pe.wait_ge(xn_ready, k + 1)
                if not isinstance(k, int) or k > 0:
                    pe.wait_ge(xt_lo, k)
                for c in range(CC):
                    mm = pe.transpose(bank[0][:, c * P:(c + 1) * P], xn[b][:, c * P:(c + 1) * P], ident[:])
                mm.then_inc(xt_psum, 1)

            def relations(k, b, j):
                if j % 2 == 0:
                    if j >= 4 or not isinstance(k, int) or k > 0:
                        pe.wait_ge(tbl_act, 4 * k + j // 2 - 1)
                else:
                    if j >= 4 or not isinstance(k, int) or k > 0:
                        pe.wait_ge(tbl_dve, 4 * k + (j - 3) // 2)
                w = 2 * (j % 2)
                three(bank[3 + j % 4][:], lambda a, c: xt[b][:, a, c, :],
                      lambda h, c: wreg[:, h, j // 2, c, w:w + 2, :].rearrange("p r o -> p (r o)")).then_inc(gnn_mm, 1)

            def tile_pe(k, i, b, nxt):
                pe.wait_ge(xt_lo, k + 1)
                if not isinstance(k, int) or k > 0:
                    pe.wait_ge(kv_cp, 2 * k)
                three(bank[1][:], lambda a, c: xt[b][:, a, c, :], lambda h, c: wkvg[:, h, c, 0:2 * C]).then_inc(kv_mm, 1)
                if not isinstance(k, int) or k > 0:
                    pe.wait_ge(hg_pre, k)
                three(bank[2][:, 0:G], lambda a, c: xt[b][:, a, c, :],
                      lambda h, c: wkvg[:, h, c, 2 * C:2 * C + G]).then_inc(hg_mm, 1)
                for j in range(4):
                    relations(k, b, j)
                if nxt:
                    turn(*nxt)
                pe.wait_ge(hg_act, k + 1)
                if not isinstance(k, int) or k > 0:
                    pe.wait_ge(hgt_cp, k)
                apart(pe)
                pe.transpose(bank[7][0:G, 0:P], hgn[:, 1, :], ident[:]).then_inc(hgt_psum, 1)
                for j in range(4, 8):
                    relations(k, b, j)

            pe.wait_ge(w_lo, 4)
            pe.wait_ge(dve_chain, MIXW_READY)
            turn(0, 0)
            tile_pe(0, 0, 0, (1, 1))
            tile_pe(1, 0, 1, (2, 0))
            with pe.Fori(1, NP) as i:
                tile_pe(2 * i, i, 0, (2 * i + 1, 1))
                tile_pe(2 * i + 1, i, 1, (2 * i + 2, 0))
            tile_pe(NT - 1, NP, 0, None)

            pe.wait_ge(kmax_up, NT)
            for c in range(CC):
                mm = pe.transpose(bank[0][:, c * P:(c + 1) * P], kmax[:, c * P:(c + 1) * P], ident[:])
            mm.then_inc(setup_pe, 1)
            pe.wait_ge(k_shift_diag, 2)
            pe.matmul(bank[1][:, 0:C], ones[:], dg[:], start=True, stop=True).then_inc(kmb_mm, 1)

            def contexts(i, first, last):
                for s in range(SLOTS):
                    pe.wait_ge(k_exp, SLOTS * i + s + 1)
                    rows = TAIL if last and s == SLOTS - 1 else P
                    for c in range(CC):
                        mm = pe.matmul(bank[2 + c][:, 0:VW], slot[0:rows, s, c * P:(c + 1) * P],
                                       slot[0:rows, s, C + c * VW:C + (c + 1) * VW],
                                       start=(first and s == 0), stop=(last and s == SLOTS - 1))
                    mm.then_inc(ctx_mm, 1)

            contexts(0, True, False)
            with pe.Fori(1, NT // SLOTS - 1) as i:
                contexts(i, False, False)
            contexts(NT // SLOTS - 1, False, True)
            pe.wait_ge(ctx_done, CC * NB)
            for d in range(CC):
                for c in range(CC):
                    mm = pe.matmul(bank[4][:, d * C + c * P:d * C + (c + 1) * P], wqt[:, c, d * P:(d + 1) * P],
                                   ctxbd[:, c, :], start=True, stop=True)
            mm.then_inc(setup_pe, 1)

            def edges(i, s, first):
                S = 8 * i + s
                if s >= 2 or not first:
                    pe.wait_ge(edge_add, adds_before(i, s - 1) if s >= 1 else adds_before(i - 1, 7))
                pe.wait_ge(sel_done, SUP * S + SUP)
                for j in range(SUP):
                    m = (s % 2) * SUP + j
                    pe.wait_ge(msg_lo, SUP * S + j + 1)
                    pe.matmul(bank[s % 2][:, 0:C], sel[:, m, :], mh[:, m, :], start=(j == 0), stop=False)
                    mm = pe.matmul(bank[s % 2][:, 0:C], sel[:, m, :], ml[:, m, :], start=False, stop=(j == SUP - 1))
                mm.then_inc(edge_mm, 1)

            def OUT(p, nt):
                n = nt * P
                pe.wait_ge(xtp_in, 32 * p + 32)
                if not isinstance(p, int) or p > 0:
                    pe.wait_ge(gap_dve, p)
                    pe.wait_ge(tt_lo, p)
                for v in range(CC):
                    mm = three(bank[4][:, v * 256:v * 256 + n], lambda a, c: wqc[:, a, c, v * P:(v + 1) * P],
                               lambda h, c: xtp[:, 0:nt, h * C + c * P:h * C + (c + 1) * P])
                mm.then_inc(out_mm, 1)
                for v in range(CC):
                    mm = pe.matmul(bank[5][:, v * 256:v * 256 + n], wg2[:, v * P:(v + 1) * P],
                                   hgp[:, 0:nt, :].rearrange("p a n -> p (a n)"), start=True, stop=True)
                mm.then_inc(gate_mm, 1)

            def PROJ(p, nt):
                pe.wait_ge(og_lo, p + 1)
                for a in range(nt):
                    mm = three(bank[4][:, a * C:(a + 1) * C], lambda h, c: og[:, h, c, a * P:(a + 1) * P],
                               lambda h, c: wproj[:, h, c, :])
                mm.then_inc(proj_mm, 1)

            def TURN(p, nt):
                pe.wait_ge(tn_dve, 2 * p + nt)
                for a in range(nt):
                    for c in range(CC):
                        mm = pe.transpose(bank[5][:, c * 256 + a * P:c * 256 + (a + 1) * P],
                                          tn[:, a, c * P:(c + 1) * P], ident[:])
                mm.then_inc(tt_mm, 1)

            def LOGIT(p, nt):
                pe.wait_ge(tt_lo, p + 1)
                for a in range(nt):
                    for m in range(2 * CC):
                        h, c = m // CC, m % CC
                        mm = pe.matmul(bank[4][:, a * X:(a + 1) * X], halves(tt[:, h, c, a * P:(a + 1) * P]),
                                       rwt[:, c, :], start=(m == 0), stop=(m == 2 * CC - 1))
                mm.then_inc(logit_mm, 1)

            def COMBT(p, nt):
                pe.wait_ge(comb_dve, p + 1)
                for a in range(nt):
                    mm = pe.transpose(bank[6][0:X, a * P:(a + 1) * P], comb[:, a, :], ident[:])
                mm.then_inc(ct_mm, 1)

            def BIAS2(p, nt):
                pe.wait_ge(ct_act, p + 1)
                for a in range(nt):
                    mm = pe.matmul(bank[7][:, a * C:(a + 1) * C], ct[:, a * P:(a + 1) * P], b2s[:],
                                   start=True, stop=True)
                mm.then_inc(b2_mm, 1)

            def LAYER1(p, nt, e):
                n = nt * P
                if e == 0:
                    pe.wait_ge(y_add, 2 * X * p + AHEAD)
                    pe.wait_ge(tt_lo, p + 1)
                else:
                    if e >= 2:
                        pe.wait_ge(h_act, 2 * (X * p + e) - 2)
                for v in range(CC):
                    mm = three(bank[2 + e % 2][:, v * 256:v * 256 + n],
                               lambda a, c: wreg[:, a, e // WC, c, e % WC, v * P:(v + 1) * P],
                               lambda h, c: tt[:, h, c, 0:n])
                mm.then_inc(h_mm, 1)

            def LAYER2(p, nt, e):
                pe.wait_ge(h_lo, X * p + e + 1)
                if e >= 2:
                    pe.wait_ge(y_add, 2 * X * p + nt * (e - 1) + AHEAD)
                elif e == 1:
                    pe.wait_ge(b2_add, p + 1)
                for a in range(nt):
                    mm = three(bank[6 + e % 2][:, a * C:(a + 1) * C], lambda h, c: ht[e % 2][:, h, c, a * P:(a + 1) * P],
                               lambda h, c: wreg[:, h, 2 + e // WC, c, e % WC, :])
                mm.then_inc(y_mm, 1)

            def slot_of(i, s, groups, p1, n1, p2, n2):
                in_slot(s, p1, n1, p2, n2, OUT=OUT, PROJ=PROJ, TURN=TURN, LOGIT=LOGIT, COMBT=COMBT, BIAS2=BIAS2,
                        LAYER1=LAYER1, LAYER2=LAYER2)
                if s < groups:
                    edges(i, s, isinstance(i, int) and i == 0)

            pe.wait_ge(dve_chain, FLAG_READY)
            far = pe.value_load(flag[0:1, 0:1], min_val=0, max_val=NT * P * R)
            with pe.If(far > 0):
                with pe.Fori(0, ET) as t:
                    pe.wait_ge(far_turn, t + 1)
                    pe.transpose(bank[6][:, 0:P], f_turn, ident[:]).then_inc(far_row, 1)
                    pe.wait_ge(far_msg, t + 1)
                    pe.matmul(bank[7][:, 0:C], f_same, stg[:, 3, :], start=True, stop=True).then_inc(far_mm, 1)

            pe.wait_ge(wqc_done, 1)
            run(pe, slot_of, NP)


EDGE_PREP = 13
WG1_READY = EDGE_PREP + 7
FLAG_READY = WG1_READY + 2
MIXW_READY = FLAG_READY + 3
CHAIN2 = 15


SLOTS_OF_PAIR = (
    ("-COMB", "-LAYER1 0", "-COMBT", "-LOW 0", "-LAYER1 1", "-BIAS2", "-LOW 1"),
    ("-LAYER2 0", "-LAYER1 2", "+OUT", "-ADD 0", "-LOW 2"),
    ("-LAYER2 1", "-LAYER1 3", "+GATE", "-LAYER2 2", "-ADD 1", "+GATE_LOW", "-LOW 3"),
    ("-LAYER1 4", "-LAYER2 3", "-ADD 2", "-LAYER1 5", "+PROJ", "-LOW 4", "-ADD 3", "-LOW 5"),
    ("-LAYER2 4", "-LAYER1 6", "+STATS", "-LAYER2 5", "-ADD 4", "-LOW 6", "-ADD 5"),
    ("-LAYER1 7", "+NORM", "-LAYER2 6", "-LOW 7", "-ADD 6"),
    ("+TURN", "-LAYER2 7", "+TURN_LOW", "-ADD 7"),
    ("+LOGIT",),
)


def in_slot(s, p1, n1, p2, n2, **steps):
    for entry in SLOTS_OF_PAIR[s]:
        name, *expert = entry[1:].split()
        p, nt = (p1, n1) if entry[0] == "+" else (p2, n2)
        if nt and name in steps:
            steps[name](p, nt, *map(int, expert))


def run(eng, slot_of, pairs, before_loop=None, after_loop=None):
    for s in range(8):
        slot_of(0, s, 8, None, 0, None, 0)
    for s in range(8):
        slot_of(1, s, 8, 0, 2, None, 0)
    if before_loop:
        before_loop()
    with eng.Fori(2, pairs) as i:
        for s in range(8):
            slot_of(i, s, 8, i - 1, 2, i - 2, 2)
    if after_loop:
        after_loop()
    for s in range(8):
        slot_of(pairs, s, 4, pairs - 1, 2, pairs - 2, 2)
    for s in range(8):
        slot_of(pairs + 1, s, 0, pairs, 1, pairs - 1, 2)
    for s in range(8):
        slot_of(pairs + 2, s, 0, None, 0, pairs, 1)


_INS = ['x', 'src', 'dst', 'edge_type_16', 'edge_weight1', 'L0_gnn_weight', 'L0_mix_Wqkv', 'L0_mix_Wproj',
        'L0_mix_bproj', 'L0_mix_ln_g', 'L0_mix_ln_b', 'L0_mix_Wg1', 'L0_mix_bg1', 'L0_mix_Wg2', 'L0_mix_bg2',
        'L0_ffn_router_w', 'L0_ffn_w1', 'L0_ffn_b1', 'L0_ffn_w2', 'L0_ffn_b2']


def kernel(**inputs):
    import numpy as _np
    import concourse.bacc as _bacc
    from concourse import mybir as _mybir
    from concourse.bass_utils import run_bass_kernel_spmd as _run

    nc = _bacc.Bacc("TRN2", target_bir_lowering=False, num_devices=1, dynamic_dma_scratch_size=8192)
    arrays, args = {}, []
    for name in _INS:
        a = _np.ascontiguousarray(inputs[name])
        arrays[f"in_{name}"] = a
        args.append(nc.dram_tensor(f"in_{name}", a.shape, _mybir.dt.from_np(a.dtype), kind="ExternalInput").ap())
    args.append(nc.dram_tensor("out_x", inputs["x"].shape, _mybir.dt.float32, kind="ExternalOutput").ap())
    gps_layer(nc, *args)
    r = _run(nc, [arrays], core_ids=[0])
    return r.results[0]["out_x"]
```

```python
from contextlib import ExitStack

import concourse.bass as bass
from concourse import mybir

ALU = mybir.AluOpType
ACT = mybir.ActivationFunctionType
AX = mybir.AxisListType
F32 = mybir.dt.float32
F32R = mybir.dt.float32r
I32 = mybir.dt.int32
U32 = mybir.dt.uint32

P = 128
EPS = 1e-5
HI, LO = 0, 1
PASSES = ((HI, HI), (LO, HI), (HI, LO))


class Tally:

    def __init__(self, sem):
        self.sem, self.n = sem, 0

    def inc(self, instruction):
        instruction.then_inc(self.sem, 1)
        self.n = self.n + 1

    def link(self, eng, instruction):
        self.inc(instruction)
        eng.wait_ge(self.sem, self.n)


def gps_layer(nc, x, src, dst, rel, norm, Wr, Wqkv, Wproj, bproj, ln_g, ln_b, Wg1, bg1, Wg2, bg2,
              router_w, w1, b1, w2, b2, out):
    N, C = x.shape
    E = src.shape[0]
    R = Wr.shape[0]
    X = router_w.shape[0]
    G = Wg1.shape[1]
    NT = -(-N // P)
    TAIL = N - (NT - 1) * P
    NP = NT // 2
    CC = C // P
    HEAD = C // 8
    NB = P // HEAD
    EPT = 16
    SUP = 4
    ROOTS_SLOT = 7
    CUT = 3
    WIN = P
    STEP = 64
    SHIFT = 4
    TAIL_GROUPS = EPT // SUP + 1
    ER = 99
    EB = 8
    ET = ER * EB
    PAD_DST = -100000
    VW = P + 1
    KVW = C + CC * VW
    WC = 4
    AHEAD = 2 * X
    BEGUN = 1
    FAR = 1 << 19
    SLOTS = 7
    RING = 16
    assert N * EPT == E and NT == 2 * NP + 1 and NT % SLOTS == 0 and CC == 2
    assert -(-E // P) + SHIFT <= (8 * NP + TAIL_GROUPS) * SUP <= ET and 4 * EB * P == RING * C

    table = nc.dram_tensor("table", [NT * P * R, C], F32).ap()
    kv_d = nc.dram_tensor("kv_d", [NT, P, KVW], F32).ap()
    xt_d = nc.dram_tensor("xt_d", [NT, P, 2 * C], F32).ap()
    hg_d = nc.dram_tensor("hg_d", [NT, G, P], F32).ap()
    dsl_d = nc.dram_tensor("dsl_d", [P, ET], F32).ap()
    gnn_d = nc.dram_tensor("gnn_d", [NT * P, C], F32).ap()

    ctx = ExitStack()
    with ctx:
        def sb(name, shape, dt, where=ctx):
            return where.enter_context(nc.sbuf_tensor(name, shape, dt))

        def sem(name):
            return ctx.enter_context(nc.semaphore(name))

        xres = sb("xres", [P, NT, C], F32)
        wreg = sb("wreg", [P, 2, 4, CC, WC, C], F32R)
        raw = sb("raw", [P, 2, CC * WC * C], F32)
        stg = sb("stg", [P, RING, C], F32)
        wproj = sb("wproj", [P, 2, CC, C], F32R)
        wqc = sb("wqc", [P, 2, CC, C], F32R)
        gidx = sb("gidx", [P, ET], I32)
        dpr = sb("dpr", [P, ET], F32)
        nrm = sb("nrm", [P, ET], F32)
        ident = sb("ident", [P, P], F32)
        ones = sb("ones", [P, P], F32)
        dbl = sb("dbl", [P, 2 * P], F32)
        kmax = sb("kmax", [P, C], F32)
        kmb = sb("kmb", [P, C], F32)
        wg2 = sb("wg2", [G, C], F32)
        cols = sb("cols", [P, 32], F32)
        rwt = sb("rwt", [P, CC, X], F32)
        rwh = sb("rwh", [P, 2, CC, X], F32R)
        b2s = sb("b2s", [X, C], F32)
        iota8 = sb("iota8", [P, X], F32)
        small = sb("small", [P, 160], F32)
        smallu = sb("smallu", [P, 2, X], U32)
        flag = sb("flag", [1, 1], I32)
        wqt = sb("wqt", [P, CC, C], F32)

        with ExitStack() as one:
            wkv_raw = sb("wkv_raw", [P, CC, 2 * C], F32, one)
            wq_raw = sb("wq_raw", [P, CC, C], F32, one)
            wp_raw = sb("wp_raw", [P, CC, C], F32, one)
            wg1_raw = sb("wg1_raw", [P, CC, G], F32, one)
            wg1_f = sb("wg1_f", [P, CC, G], F32, one)
            wkvg = sb("wkvg", [P, 2, CC, 2 * C + G], F32R, one)
            xt = [sb(f"xt{b}", [P, 2, CC, P], F32R, one) for b in range(2)]
            xn = [sb(f"xn{b}", [P, C], F32, one) for b in range(2)]
            kvs = [sb(f"kvs{b}", [P, KVW], F32, one) for b in range(2)]
            hgn = sb("hgn", [P, 2, G], F32, one)
            hgt = [sb(f"hgt{b}", [G, P], F32, one) for b in range(2)]
            erow = sb("erow", [ER, 2, EB * P], F32, one)
            vrow = sb("vrow", [24, P], F32, one)
            rwr = sb("rwr", [X, C], F32, one)
            bpb = sb("bpb", [P, C], F32, one)
            g1b = sb("g1b", [P, G], F32, one)
            lnbb = sb("lnbb", [P, CC, P], F32, one)
        two = ctx.enter_context(ExitStack())
        ctxbd = sb("ctxbd", [P, CC, P], F32, two)
        dg = sb("dg", [P, C], F32, two)
        mh = sb("mh", [P, 2 * CUT, C], F32R, two)
        ml = sb("ml", [P, 2 * CUT, C], F32R, two)
        sel = sb("sel", [P, 2 * CUT, P], F32R, two)
        sel_norm = sb("sel_norm", [P, 2 * (SUP - CUT), P], F32, two)
        tt = sb("tt", [P, 2, CC, 2 * P], F32R, two)
        xtp = sb("xtp", [P, 2, 2 * C], F32R, two)
        hgp = sb("hgp", [G, 2, P], F32, two)
        ht = [sb(f"ht{b}", [P, 2, CC, 2 * P], F32R, two) for b in range(2)]
        idxcur = sb("idxcur", [P, 2 * EPT], I32, two)

        bank = [ctx.enter_context(nc.psum_tensor(f"bank{b}", [P, 512], F32)) for b in range(8)]

        erow_i = stg[:].rearrange("p a c -> p (a c)")[0:ER, 0:4 * EB * P].rearrange(
            "p (a b) -> p a b", a=4)
        src_r, rel_r, dst_r = (erow_i[:, a, :].bitcast(I32) for a in range(3))
        norm_r = erow_i[:, 3, :]
        lo_i = raw[:, 1, 0:ET].bitcast(I32)
        mask = raw[:, 1, ET:2 * ET]
        dsl = raw[:, 0, 2 * P:2 * P + ET]
        stage = stg[:].rearrange("p (h j) c -> p h (j c)", h=2)
        rel_raw = [xres[:, NT - 8 * (4 - n):NT - 8 * (3 - n), :].rearrange("p a c -> p (a c)") for n in range(4)]
        slot = raw[:].rearrange("p a b -> p (a b)")[:, 0:SLOTS * KVW].rearrange(
            "p (s w) -> p s w", s=SLOTS)
        rs = raw[:].rearrange("p a b -> p (a b)")
        gate = rs[:, 0:512]
        ogf = rs[:, 512:1024]
        tn = rs[:, 1024:1536].rearrange("p (a c) -> p a c", a=2)
        hf = [rs[:, 2048 + 512 * b:2560 + 512 * b] for b in range(2)]
        comb = rs[:, 3072:3072 + 2 * X].rearrange("p (a e) -> p a e", a=2)
        lg = rs[:, 3088:3088 + 2 * X].rearrange("p (a e) -> p a e", a=2)
        top = rs[:, 3104:3104 + 2 * X].rearrange("p (a e) -> p a e", a=2)
        idf = rs[:, 3120:3120 + 2 * X].rearrange("p (a e) -> p a e", a=2)
        cb2 = rs[:, 3136:3136 + 2 * X].rearrange("p (a e) -> p a e", a=2)
        ct = rs[0:X, 3200:3456]
        f_dsl, f_low, f_turn, f_same = rs[:, 0:ET], rs[:, 800:928], rs[:, 928:1056], rs[:, 1056:1184]
        f_dup = rs[:, 1184:1185]
        f_i = rs[:, 1188:1191].bitcast(I32)
        og = xtp[:].rearrange("p a b -> p (a b)").rearrange("p (h c n) -> p h c n", h=2, c=CC)
        b1c = cols[:, 0:2 * X]
        gcol, bcol, bg2c = cols[:, 16:18], cols[:, 18:20], cols[:, 20:22]
        bg2h = small[:, 0:2]
        s2 = small[:, 2:4]
        stats = small[:, 4:16].rearrange("p (a b) -> p a b", a=2)
        mv = small[:, 16:20].rearrange("p (a b) -> p a b", a=2)
        rstd = small[:, 20:22]
        kcol = small[:, 22:24]
        rden = small[:, 24:26]
        cnt = small[:, 26:27]
        dlt = small[:, 28:30]
        th = small[:, 30:32]
        wa = small[:, 32:34]
        wb = small[:, 34:36]
        ve = small[:, 36:38]
        nmr = small[:, 40:42]
        rst1 = small[:, 42:44]
        half = small[:, 38:40]
        bg1r = small[0:1, 64:64 + G]

        eng_names = [nc.vector.engine, nc.tensor.engine, nc.gpsimd.engine]
        waited = [sem(f"waited{n}") for n in range(3)]
        consts = sem("consts")
        cleared = sem("cleared")
        edges_in = sem("edges_in")
        vec_in = sem("vec_in")
        mixw_in = sem("mixw_in")
        rel_in = [sem(f"rel_in{n}") for n in range(4)]
        flag_ready = sem("flag_ready")
        raw_in = [sem(f"raw_in{b}") for b in range(2)]
        x_in = sem("x_in")
        bp_in = sem("bp_in")
        setup_pe = sem("setup_pe")
        setup_act = sem("setup_act")
        dve_chain = sem("dve_chain")
        w_hi = sem("w_hi")
        w_lo = sem("w_lo")
        xn_ready = sem("xn_ready")
        bias_in = sem("bias_in")
        xt_psum = sem("xt_psum")
        xt_hi = sem("xt_hi")
        xt_lo = sem("xt_lo")
        kv_mm = sem("kv_mm")
        kv_cp = sem("kv_cp")
        kmax_up = sem("kmax_up")
        hg_mm = sem("hg_mm")
        var_ready = sem("var_ready")
        rstd_ready = sem("rstd_ready")
        s2_ready = sem("s2_ready")
        pool_chain = sem("pool_chain")
        var2_ready = sem("var2_ready")
        rstd2_ready = sem("rstd2_ready")
        hg_pre = sem("hg_pre")
        hg_act = sem("hg_act")
        hgt_psum = sem("hgt_psum")
        hgt_cp = sem("hgt_cp")
        gnn_mm = sem("gnn_mm")
        tbl_act = sem("tbl_act")
        tbl_dve = sem("tbl_dve")
        tbl_st = [sem(f"tbl_st{h}") for h in range(2)]
        kv_st = [sem(f"kv_st{b}") for b in range(2)]
        xt_st = [sem(f"xt_st{b}") for b in range(2)]
        hg_st = [sem(f"hg_st{b}") for b in range(2)]
        kv_in = [sem(f"kv_in{s}") for s in range(SLOTS)]
        k_shift = sem("k_shift")
        k_exp = sem("k_exp")
        ctx_mm = sem("ctx_mm")
        idx_cur = sem("idx_cur")
        gath = [sem(f"gath{g}") for g in range(4)]
        msg_hi = sem("msg_hi")
        msg_lo = sem("msg_lo")
        sel_done = sem("sel_done")
        edge_mm = sem("edge_mm")
        edge_add = sem("edge_add")
        xtp_in = sem("xtp_in")
        out_mm, gate_mm, gate_act, og_dve, og_hi, og_lo, proj_mm, tn_act, tt_mm, tt_hi, tt_lo, logit_mm, gap_dve, \
            gap_act, comb_dve, acc_act, ct_mm, ct_act, b2_mm, b2_add = (sem(n) for n in (
                "out_mm", "gate_mm", "gate_act", "og_dve", "og_hi", "og_lo", "proj_mm", "tn_act", "tt_mm", "tt_hi",
                "tt_lo", "logit_mm", "gap_dve", "gap_act", "comb_dve", "acc_act", "ct_mm", "ct_act", "b2_mm",
                "b2_add"))
        shift_dve = sem("shift_dve")
        table_kept = sem("table_kept")
        h_mm = sem("h_mm")
        h_act = sem("h_act")
        h_hi = sem("h_hi")
        h_lo = sem("h_lo")
        y_mm = sem("y_mm")
        y_add = sem("y_add")
        out_st = sem("out_st")
        dsl_st = sem("dsl_st")
        far_idx, far_dst, far_turn, far_row, far_uniq, far_in, far_msg, far_mm, far_sum, far_st, far_ld, far_x, \
            far_init = (sem("far_" + n) for n in ("idx", "dst", "turn", "row", "uniq", "in", "msg", "mm", "sum", "st",
                                                  "ld", "x", "init"))
        k_shift_diag = sem("k_shift_diag")
        kmb_mm = sem("kmb_mm")
        ctx_done = sem("ctx_done")
        wqc_done = sem("wqc_done")

        block = ctx.enter_context(nc.Block())

        def halves(t):
            return t.bitcast(F32)

        def edge_window(q):
            first = (STEP * q - WIN // 2) % P
            return dbl[:, (P - first) % P:(P - first) % P + P]

        def window_parts(q):
            return [(0, 128, 0)] if q else [(64, 128, -1), (0, 64, 0)]

        def apart(eng):
            eng.sem_inc(waited[eng_names.index(eng.engine)], 1)

        def first_phase_over(eng):
            eng.wait_ge(gnn_mm, 8 * NT)
            eng.wait_ge(bias_in, NT)
            eng.wait_ge(kmax_up, NT)
            eng.wait_ge(hgt_cp, NT)
            eng.wait_ge(kv_cp, 2 * NT)
            for b, n in ((0, NP + 1), (1, NP)):
                eng.wait_ge(xt_st[b], 16 * n)
                eng.wait_ge(kv_st[b], 16 * n)
                eng.wait_ge(hg_st[b], 16 * n)

        ALL_ADDS = 3 * NT

        def adds_before(i, u):
            return 6 * i + 3 * (u // 2) + 2 * (u % 2) - 1

        @block.sync
        def _(sp):
            sp.wait_ge(cleared, 1)
            for a, v in ((src_r, src), (rel_r, rel), (dst_r, dst), (norm_r, norm.rearrange("e a -> (e a)"))):
                a3 = a.rearrange("p (b e) -> p b e", b=EB)
                first = (ER - SHIFT) * P
                sp.dma_start(a3[SHIFT:ER, 0, :], v[0:first].rearrange("(p e) -> p e", e=P)).then_inc(edges_in, 16)
                mid = first + (EB - 2) * ER * P
                sp.dma_start(a3[:, 1:EB - 1, :], v[first:mid].rearrange("(b p e) -> p b e", p=ER, e=P)).then_inc(edges_in, 16)
                full = (E - mid) // P
                sp.dma_start(a3[0:full, EB - 1, :], v[mid:mid + full * P].rearrange("(p e) -> p e", e=P)).then_inc(edges_in, 16)
                sp.dma_start(a3[full:full + 1, EB - 1, 0:E - mid - full * P],
                             v[mid + full * P:E].rearrange("(a e) -> a e", a=1)).then_inc(edges_in, 16)
            sp.wait_ge(cleared, 2)
            for k, (v, n) in enumerate(((ln_g, CC), (ln_b, CC), (bg2, CC))):
                sp.dma_start(vrow[16 + 2 * k:18 + 2 * k, :], v.rearrange("(a e) -> a e", a=CC)).then_inc(vec_in, 16)
            sp.dma_start(vrow[0:2 * X, :], b1.rearrange("x (a e) -> (x a) e", a=CC)).then_inc(vec_in, 16)
            sp.dma_start(bg1r, bg1.rearrange("(a e) -> a e", a=1)).then_inc(vec_in, 16)
            sp.dma_start(rwr[:], router_w).then_inc(vec_in, 16)
            sp.dma_start(b2s[:], b2).then_inc(vec_in, 16)
            sp.dma_start(wg2[:], Wg2).then_inc(vec_in, 16)
            wqkv_r = Wqkv.rearrange("(c p) n -> p c n", p=P)
            sp.dma_start(wkv_raw[:], wqkv_r[:, :, C:3 * C]).then_inc(mixw_in, 16)
            sp.dma_start(wg1_raw[:], Wg1.rearrange("(c p) n -> p c n", p=P)).then_inc(mixw_in, 16)
            sp.dma_start(wq_raw[:], wqkv_r[:, :, 0:C]).then_inc(mixw_in, 16)
            sp.dma_start(wp_raw[:], Wproj.rearrange("(c p) n -> p c n", p=P)).then_inc(mixw_in, 16)

            def stores(k, i, b):
                sp.wait_ge(xt_lo, k + 1)
                sp.dma_start(xt_d[bass.ds(k, 1)].rearrange("a p f -> (a p) f"),
                             halves(xt[b][:].rearrange("p h c n -> p (h c n)"))).then_inc(xt_st[b], 16)
                sp.wait_ge(kv_cp, 2 * k + 2)
                sp.dma_start(kv_d[bass.ds(k, 1)].rearrange("a p f -> (a p) f"), kvs[b][:]).then_inc(kv_st[b], 16)
                for h in range(2):
                    sp.wait_ge(tbl_act, 4 * k + 2 * h + 2)
                    sp.wait_ge(tbl_dve, 4 * k + 2 * h + 2)
                    sp.dma_start(table_rows[:, bass.ds(k, 1), h * R // 2 * C:(h + 1) * R // 2 * C].rearrange(
                        "p a f -> p (a f)"), stage[:, h, :]).then_inc(tbl_st[h], 16)
                    if h == 0:
                        sp.wait_ge(hgt_cp, k + 1)
                        sp.dma_start(hg_d[bass.ds(k, 1)].rearrange("a p f -> (a p) f"), hgt[b][:]).then_inc(hg_st[b], 16)

            table_rows = table.rearrange("(k p r) c -> p k (r c)", p=P, r=R)
            with sp.Fori(0, NP) as i:
                stores(2 * i, i, 0)
                stores(2 * i + 1, i, 1)
            stores(NT - 1, NP, 0)

            sp.wait_ge(kv_st[0], 16 * (NP + 1))
            sp.wait_ge(kv_st[1], 16 * NP)
            sp.wait_ge(w_lo, 8)

            def load_slots(i):
                for s in range(SLOTS):
                    if not isinstance(i, int) or i > 0:
                        sp.wait_ge(ctx_mm, SLOTS * (i - 1) + s + 1)
                    sp.dma_start(slot[:, s, :], kv_d[bass.ds(SLOTS * i + s, 1)].rearrange("a p f -> (a p) f")
                                 ).then_inc(kv_in[s], 16)

            load_slots(0)
            with sp.Fori(1, NT // SLOTS) as i:
                load_slots(i)

            first_phase_over(sp)

            def load_pair(p, nt):
                if not isinstance(p, int) or p > 0:
                    sp.wait_ge(proj_mm, p)
                sp.dma_start(halves(xtp[:, 0:nt, :]), xt_d[bass.ds(2 * p, nt)].rearrange("a p f -> p a f")).then_inc(xtp_in, 16)
                sp.dma_start(hgp[:, 0:nt, :], hg_d[bass.ds(2 * p, nt)].rearrange("a p f -> p a f")).then_inc(xtp_in, 16)

            def store_pair(p, nt):
                sp.wait_ge(y_add, 2 * X * p + X * nt + AHEAD)
                if nt == 2:
                    sp.dma_start(out[0:NP * 2 * P].rearrange("(a p) c -> p a c", p=P)[:, bass.ds(2 * p, 2), :],
                                 xres[:, bass.ds(2 * p, 2), :]).then_inc(out_st, 16)
                else:
                    sp.dma_start(out[(NT - 1) * P:N, :], xres[0:TAIL, NT - 1, :]).then_inc(out_st, 16)

            load_pair(0, 2)
            load_pair(1, 2)
            with sp.Fori(2, NP) as p:
                load_pair(p, 2)
                store_pair(p - 2, 2)
            load_pair(NP, 1)
            store_pair(NP - 2, 2)
            store_pair(NP - 1, 2)
            store_pair(NP, 1)
            sp.wait_ge(out_st, 16 * (NP + 1))

        @block.gpsimd
        def _(pool):
            pool.memset(ident[:], 0.0).then_inc(consts, 1)
            pool.memset(ones[:], 1.0).then_inc(consts, 1)
            pool.wait_ge(consts, 2)
            pool.affine_select(out=ident[:], in_=ident[:], compare_op=ALU.not_equal, fill=1.0, base=0,
                               pattern=[[-1, P]], channel_multiplier=1).then_inc(consts, 1)
            pool.iota(smallu[:, 0, :].bitcast(I32), pattern=[[1, X]], base=0, channel_multiplier=0).then_inc(consts, 1)
            pool.iota(raw[:, 0, 0:2 * P].bitcast(I32), pattern=[[0, 2], [1, P]], base=0,
                      channel_multiplier=0).then_inc(consts, 1)
            pool.iota(lo_i, pattern=[[STEP, ET // (2 * SUP)], [0, 2 * SUP]], base=-WIN // 2,
                      channel_multiplier=0).then_inc(consts, 1)
            pool.wait_ge(consts, 6)
            pool.tensor_copy(iota8[:], smallu[:, 0, :].bitcast(I32)).then_inc(consts, 1)
            pool.tensor_copy(dbl[:], raw[:, 0, 0:2 * P].bitcast(I32)).then_inc(consts, 1)
            pool.dma_start(bpb[:], bproj.rearrange("(a c) -> a c", a=1).to_broadcast([P, C])).then_inc(bp_in, 16)
            pool.memset(half, -0.5).then_inc(consts, 1)
            pool.wait_ge(consts, 9)
            pool.wait_ge(cleared, 2)
            pool.wait_ge(bp_in, 16)
            pc = Tally(pool_chain)

            def load_x(i):
                pool.dma_start(xres[:, bass.ds(2 * i, 2), :],
                               x[0:NP * 2 * P].rearrange("(a p) c -> p a c", p=P)[:, bass.ds(2 * i, 2), :]
                               ).then_inc(x_in, 16)

            def load_tail():
                pool.dma_start(xres[0:TAIL, NT - 1, :], x[(NT - 1) * P:N, :]).then_inc(x_in, 16)

            def roots(k, i, b):
                pool.wait_ge(var_ready, k + 1)
                if not isinstance(i, int) or i > 0:
                    pool.wait_ge(hg_pre, k - 1)
                apart(pool)
                pc.link(pool, pool.tensor_scalar(ve[:, 0:1], mv[:, b, 1:2], EPS, None, ALU.add))
                pool.tensor_tensor(rstd[:, b:b + 1], ve[:, 0:1], half[:, 0:1], ALU.pow).then_inc(rstd_ready, 1)
                pool.wait_ge(rstd_ready, k + 1)
                apart(pool)
                pc.link(pool, pool.tensor_scalar(ve[:, 1:2], mv[:, b, 1:2], rstd[:, b:b + 1], rstd[:, b:b + 1],
                                                 ALU.mult, ALU.mult))
                apart(pool)
                pc.link(pool, pool.tensor_scalar(ve[:, 1:2], ve[:, 1:2], EPS, None, ALU.add))
                pool.tensor_tensor(s2[:, b:b + 1], ve[:, 1:2], half[:, 0:1], ALU.pow).then_inc(s2_ready, 1)
                pool.wait_ge(xn_ready, k + 1)
                pool.tensor_tensor(xres[:, bass.ds(k, 1), :].rearrange("p a c -> p (a c)"),
                                   xres[:, bass.ds(k, 1), :].rearrange("p a c -> p (a c)"), bpb[:],
                                   ALU.add).then_inc(bias_in, 1)

            load_x(0)
            pool.wait_ge(x_in, 16)
            load_x(1)
            pool.wait_ge(x_in, 32)
            load_x(2)
            roots(0, 0, 0)
            roots(1, 0, 1)
            pool.wait_ge(cleared, 3)
            with pool.Fori(1, NP - 2) as i:
                pc.n = 6 * i
                pool.wait_ge(x_in, 16 * i + 32)
                load_x(i + 2)
                roots(2 * i, i, 0)
                roots(2 * i + 1, i, 1)
            for i in range(NP - 2, NP):
                pc.n = 6 * i
                if i == NP - 2:
                    pool.wait_ge(x_in, 16 * i + 32)
                    load_tail()
                roots(2 * i, i, 0)
                roots(2 * i + 1, i, 1)
            roots(NT - 1, NP, 0)
            first_phase_over(pool)
            pool.wait_ge(tbl_st[0], 16 * NT)
            pool.wait_ge(tbl_st[1], 16 * NT)
            pool.wait_ge(flag_ready, 1)
            far = pool.value_load(flag[0:1, 0:1], min_val=0, max_val=NT * P * R)
            with pool.If(far > 0):
                pool.wait_ge(wqc_done, 1)
                pool.memset(stg[:, 0:3, :], 0.0).then_inc(far_init, 1)
                pool.memset(f_low, 1.0).then_inc(far_init, 1)
                pool.wait_ge(far_init, 2)
                pool.affine_select(out=f_low, in_=f_low, compare_op=ALU.is_gt, fill=0.0, base=0,
                                   pattern=[[-1, P]], channel_multiplier=1).then_inc(far_init, 1)
                pool.dma_start(f_dsl, dsl_d).then_inc(far_ld, 16)
                with pool.Fori(0, NT) as k:
                    pool.dma_start(gnn_d.rearrange("(k p) c -> p k c", p=P)[:, bass.ds(k, 1), :],
                                   stg[:, 0:1, :]).then_inc(far_ld, 16)
                pool.wait_ge(far_ld, 16 * (NT + 1))
                with pool.Fori(0, ET) as t:
                    pool.tensor_copy(f_i[:, 0:1], gidx[:, bass.ds(t, 1)]).then_inc(far_idx, 1)
                    pool.wait_ge(far_idx, t + 1)
                    apart(pool)
                    pool.indirect_dma_start(stg[:, 0, :], None, table,
                                            bass.IndirectOffsetOnAxis(ap=f_i[:, 0:1], axis=0),
                                            bounds_check=NT * P * R - 1, oob_is_err=False).then_inc(far_in, 16)
                    pool.wait_ge(far_dst, t + 1)
                    apart(pool)
                    pool.indirect_dma_start(stg[:, 1, :], None, gnn_d,
                                            bass.IndirectOffsetOnAxis(ap=f_i[:, 1:2], axis=0),
                                            bounds_check=NT * P - 1, oob_is_err=False).then_inc(far_in, 16)
                    pool.wait_ge(far_sum, t + 1)
                    apart(pool)
                    pool.indirect_dma_start(gnn_d, bass.IndirectOffsetOnAxis(ap=f_i[:, 2:3], axis=0),
                                            stg[:, 2, :], None,
                                            bounds_check=NT * P - 1, oob_is_err=False).then_inc(far_st, 16)
                    pool.wait_ge(far_st, 16 * t + 16)
                with pool.Fori(0, NT) as k:
                    pool.dma_start(stg[:, 3:4, :], gnn_d.rearrange("(k p) c -> p k c", p=P)[:, bass.ds(k, 1), :]
                                   ).then_inc(far_ld, 16)
                    pool.wait_ge(far_x, k + 1)

            def gathers(i, groups):
                for s in range(groups):
                    if s % 4 == 0:
                        for g in range(4):
                            if not isinstance(i, int) or i > 0:
                                pool.wait_ge(gath[g], 64 * (2 * i - 1 + s // 4))
                        n = min(4, groups - s) * SUP
                        pool.tensor_copy(idxcur[:, s * SUP:s * SUP + n],
                                         gidx[:, bass.ds((8 * i + s) * SUP, n)]).then_inc(idx_cur, 1)
                        pool.wait_ge(idx_cur, 2 * i + s // 4 + 1)
                    if s >= 4 or not isinstance(i, int) or i > 0:
                        pool.wait_ge(edge_mm, 8 * i + s - 3)
                        apart(pool)
                    for j in range(SUP):
                        if s == ROOTS_SLOT and j == 2 and not (isinstance(i, int) and i < 1):
                            roots2(i - 1, 2)
                        pool.indirect_dma_start(
                            stg[:, (s % 4) * SUP + j, :], None, table,
                            bass.IndirectOffsetOnAxis(ap=idxcur[:, s * SUP + j:s * SUP + j + 1], axis=0),
                            bounds_check=NT * P * R - 1, oob_is_err=False).then_inc(gath[s % 4], 16)

            def roots2(p, nt):
                pool.wait_ge(var2_ready, 2 * p + nt)
                apart(pool)
                pc.link(pool, pool.tensor_scalar(ve[:, 0:nt], mv[:, 0:nt, 1], EPS, None, ALU.add))
                pool.tensor_tensor(rstd[:, 0:nt], ve[:, 0:nt], half[:, 0:nt], ALU.pow).then_inc(rstd2_ready, 1)

            gathers(0, 8)
            gathers(1, 8)
            base = pc.n
            with pool.Fori(2, NP) as i:
                pc.n = base + i - 2
                gathers(i, 8)
            pc.n = base + NP - 2
            gathers(NP, TAIL_GROUPS)
            roots2(NP - 1, 2)
            roots2(NP, 1)

        @block.scalar
        def _(act):
            chunks = [Wr[WC * n:WC * n + WC] for n in range(4)] + \
                     [w[WC * n:WC * n + WC] for w in (w1, w2) for n in range(2)]

            def load_chunk(n):
                place, done = (rel_raw[n], rel_in[n]) if n < 4 else (raw[:, n % 2, :], raw_in[n % 2])
                for c in range(CC):
                    act.dma_start(place.rearrange("p (c r o) -> p c r o", c=CC, r=WC)[:, c],
                                  chunks[n].rearrange("r (c p) o -> p c r o", p=P)[:, c]).then_inc(done, 16)

            def split_hi(n):
                if n < 4:
                    act.wait_ge(rel_in[n], 32)
                else:
                    act.wait_ge(raw_in[n % 2], 32 * (n // 2 - 1))
                act.copy(wreg[:, HI, n % 4].rearrange("p c r o -> p (c r o)"),
                         rel_raw[n] if n < 4 else raw[:, n % 2, :]).then_inc(w_hi, 1)

            for n in range(4):
                load_chunk(n)
            act.wait_ge(setup_pe, 3)
            act.copy(nrm[:, 0:4 * ER], bank[4][:, 0:4 * ER]).then_inc(setup_act, 1)
            act.copy(nrm[:, 4 * ER:ET], bank[5][:, 0:ET - 4 * ER]).then_inc(setup_act, 1)
            act.wait_ge(dve_chain, VECTORS_IN)
            act.copy(rwh[:, HI], rwt[:]).then_inc(setup_act, 1)
            act.wait_ge(mixw_in, 64)
            act.copy(wkvg[:, HI, :, 0:2 * C], wkv_raw[:]).then_inc(setup_act, 1)
            act.copy(wproj[:, HI], wp_raw[:]).then_inc(setup_act, 1)
            act.wait_ge(dve_chain, WG1_READY)
            act.copy(wkvg[:, HI, :, 2 * C:2 * C + G], wg1_f[:]).then_inc(setup_act, 1)
            act.wait_ge(setup_pe, 4)
            act.copy(wqt[:].rearrange("p c n -> p (c n)"), bank[6][:]).then_inc(setup_act, 1)
            for n in range(4):
                split_hi(n)

            def table_out(k, j):
                if j % 4 == 0:
                    if not isinstance(k, int) or k > 0:
                        act.wait_ge(tbl_st[j // 4], 16 * k)
                act.wait_ge(gnn_mm, 8 * k + j + 1)
                act.copy(stage[:, j // 4, (j % 4) * 512:(j % 4 + 1) * 512], bank[3 + j % 4][:]).then_inc(tbl_act, 1)

            def xt_high(k, i, b):
                act.wait_ge(xt_psum, k + 1)
                if not isinstance(i, int) or i > 0:
                    act.wait_ge(gnn_mm, 8 * k - 8)
                    act.wait_ge(xt_st[b], 16 * i)
                act.copy(xt[b][:, HI].rearrange("p c n -> p (c n)"), bank[0][:, 0:C]).then_inc(xt_hi, 1)

            def tile_act(k, i, b, more, nxt):
                act.wait_ge(kv_mm, k + 1)
                if not isinstance(i, int) or i > 0:
                    act.wait_ge(kv_st[b], 16 * i)
                    act.wait_ge(kmax_up, k - 1)
                act.copy(kvs[b][:, 0:C], bank[1][:, 0:C]).then_inc(kv_cp, 1)
                act.copy(kvs[b][:, C:].rearrange("p (c w) -> p c w", c=CC)[:, :, 0:P],
                         bank[1][:, C:2 * C].rearrange("p (c w) -> p c w", c=CC)).then_inc(kv_cp, 1)
                act.wait_ge(hg_pre, k + 1)
                act.activation(hgn[:, 1, :], hgn[:, 0, :], ACT.Gelu).then_inc(hg_act, 1)
                table_out(k, 0)
                table_out(k, 2)
                if more:
                    xt_high(*nxt)
                act.wait_ge(hgt_psum, k + 1)
                if not isinstance(i, int) or i > 0:
                    act.wait_ge(hg_st[b], 16 * i)
                act.copy(hgt[b][:], bank[7][0:G, 0:P]).then_inc(hgt_cp, 1)
                table_out(k, 4)
                table_out(k, 6)

            xt_high(0, 0, 0)
            tile_act(0, 0, 0, True, (1, 0, 1))
            tile_act(1, 0, 1, True, (2, 1, 0))
            act.wait_ge(dve_chain, FAR_READY)
            act.dma_start(dsl_d, dsl).then_inc(dsl_st, 16)
            act.wait_ge(dsl_st, 16)
            load_chunk(4)
            load_chunk(5)
            with act.Fori(1, NP) as i:
                tile_act(2 * i, i, 0, True, (2 * i + 1, i, 1))
                tile_act(2 * i + 1, i, 1, True, (2 * i + 2, i + 1, 0))
            tile_act(NT - 1, NP, 0, False, None)

            for n in range(4, 8):
                if n == 4:
                    act.wait_ge(gnn_mm, 8 * NT)
                split_hi(n)
                if n < 6:
                    act.wait_ge(w_lo, n + 1)
                    load_chunk(n + 2)

            def exps(i):
                for s in range(SLOTS):
                    act.wait_ge(k_shift, SLOTS * i + s + 1)
                    act.activation(slot[:, s, 0:C], slot[:, s, 0:C], ACT.Exp).then_inc(k_exp, 1)

            with act.Fori(0, NT // SLOTS) as i:
                exps(i)
            act.wait_ge(setup_pe, 8)
            act.mul(wqc[:, HI].rearrange("p c n -> p (c n)"), bank[4][:], 0.5).then_inc(setup_act, 1)

            first_phase_over(act)

            def MSGS(i, s, groups):
                if s >= groups:
                    return
                S = 8 * i + s
                act.wait_ge(gath[s % 4], 64 * (2 * i + s // 4 + 1))
                if s >= 2 or not isinstance(i, int) or i > 0:
                    act.wait_ge(edge_mm, S - 1)
                for j in range(CUT):
                    act.activation(mh[:, (s % 2) * CUT + j, :], stg[:, (s % 4) * SUP + j, :], ACT.Copy,
                                   scale=nrm[:, bass.ds(SUP * S + j, 1)]).then_inc(msg_hi, 1)

            def cols2(t, n):
                return t.rearrange("p (c n) -> p c n", c=CC)[:, :, 0:n]

            def GATE_ACT(p, nt):
                act.wait_ge(gate_mm, p + 1)
                for c in range(CC):
                    act.activation(gate[:, c * 256:c * 256 + nt * P], bank[5][:, c * 256:c * 256 + nt * P], ACT.Tanh,
                                   bias=bg2h[:, c:c + 1], scale=0.5).then_inc(gate_act, 1)

            def GATE_HI(p, nt):
                act.wait_ge(og_dve, p + 1)
                act.copy(og[:, HI, :, 0:nt * P], cols2(ogf, nt * P)).then_inc(og_hi, 1)

            def NORM(p, nt):
                act.wait_ge(shift_dve, 2 * p + 2)
                for a in range(nt):
                    xk = xres[:, bass.ds(2 * p + a, 1), :].rearrange("p a c -> p (a c)")
                    act.activation(tn[:, a, :], xk, ACT.Identity, bias=nmr[:, a:a + 1],
                                   scale=rstd[:, a:a + 1]).then_inc(tn_act, 1)
                for a in range(nt):
                    xk = xres[:, bass.ds(2 * p + a, 1), :].rearrange("p a c -> p (a c)")
                    act.activation(xk, xk, ACT.Identity, bias=nmr[:, a:a + 1],
                                   scale=rst1[:, a:a + 1]).then_inc(acc_act, 1)

            def TURN_HI(p, nt):
                act.wait_ge(tt_mm, p + 1)
                act.copy(tt[:, HI, :, 0:nt * P], cols2(bank[5][:], nt * P)).then_inc(tt_hi, 1)

            def WEIGHT(p, nt):
                act.wait_ge(gap_dve, p + 1)
                act.activation(th[:, 0:nt], dlt[:, 0:nt], ACT.Tanh, scale=0.5).then_inc(gap_act, 1)

            def COMBT_ACT(p, nt):
                act.wait_ge(ct_mm, p + 1)
                act.copy(ct[:, 0:nt * P], bank[5][0:X, 0:nt * P]).then_inc(ct_act, 1)

            def LAYER1(p, nt, e):
                T = X * p + e
                act.wait_ge(h_mm, T + 1)
                if e >= 2 or not isinstance(p, int) or p > 0:
                    act.wait_ge(h_lo, T - 1 + BEGUN)
                for c in range(CC):
                    act.activation(hf[e % 2][:, c * 256:c * 256 + nt * P], bank[2 + e % 2][:, c * 256:c * 256 + nt * P],
                                   ACT.Gelu, bias=b1c[:, 2 * e + c:2 * e + c + 1]).then_inc(h_act, 1)
                act.wait_ge(h_act, 2 * T + 2 + 2 * BEGUN)
                if e >= 2 or not isinstance(p, int) or p > 0:
                    act.wait_ge(y_mm, T - 1 + BEGUN)
                act.copy(ht[e % 2][:, HI, :, 0:nt * P], cols2(hf[e % 2], nt * P)).then_inc(h_hi, 1)

            def slot_of(i, s, groups, p1, n1, p2, n2):
                if s == 0 and not isinstance(i, int):
                    act.activation(small[0:1, 120:121], small[0:1, 121:122], ACT.Gelu).then_inc(table_kept, 1)
                in_slot(i, s, groups, p1, n1, p2, n2, MSGS=MSGS, GATE_ACT=GATE_ACT, GATE_HI=GATE_HI, NORM=NORM,
                        TURN_HI=TURN_HI, WEIGHT=WEIGHT, COMBT_ACT=COMBT_ACT, LAYER1=LAYER1)

            run(act, slot_of, NP, TAIL_GROUPS)

        @block.vector
        def _(dve):
            ch = Tally(dve_chain)
            dve.sem_inc(y_add, AHEAD)
            dve.sem_inc(h_lo, BEGUN)
            dve.sem_inc(h_act, 2 * BEGUN)
            dve.sem_inc(y_mm, BEGUN)
            dve.memset(src_r, 0)
            dve.memset(rel_r, 0)
            dve.memset(dst_r, PAD_DST)
            dve.memset(norm_r, 0.0).then_inc(cleared, 1)
            dve.memset(vrow[:], 0.0)
            dve.memset(small[0:1, 120:122], 0.0)
            for b in range(2):
                for c in range(CC):
                    dve.memset(kvs[b][:, C + c * VW + P:C + c * VW + VW], 1.0)
            dve.memset(kmax[:], -3.0e38).then_inc(cleared, 1)
            dve.wait_ge(cleared, 2)

            dve.wait_ge(edges_in, 16 * 16)
            ch.inc(dve.scalar_tensor_tensor(out=erow[:, 0, :], in0=src_r, scalar=float(R), in1=rel_r,
                                            op0=ALU.mult, op1=ALU.add))
            ch.inc(dve.tensor_copy(erow[:, 1, :], dst_r))
            dve.wait_ge(setup_pe, 1)
            ch.inc(dve.tensor_copy(gidx[:, 0:4 * ER], bank[0][:, 0:4 * ER]))
            ch.inc(dve.tensor_copy(gidx[:, 4 * ER:ET], bank[1][:, 0:ET - 4 * ER]))
            dve.wait_ge(consts, 8)
            dve.wait_ge(setup_pe, 2)
            ch.inc(dve.tensor_tensor(dpr[:, 0:4 * ER], bank[2][:, 0:4 * ER], lo_i[:, 0:4 * ER], ALU.subtract))
            ch.link(dve, dve.tensor_tensor(dpr[:, 4 * ER:ET], bank[3][:, 0:ET - 4 * ER], lo_i[:, 4 * ER:ET], ALU.subtract))
            assert ch.n == EDGES_IN
            dve.wait_ge(setup_pe, 5)
            ch.inc(dve.tensor_copy(cols[:, 0:22], bank[7][:, 0:22]))
            ch.link(dve, dve.tensor_copy(rwt[:].rearrange("p c x -> p (c x)"), bank[7][:, 32:32 + CC * X]))
            dve.wait_ge(mixw_in, 64)
            dve.wait_ge(vec_in, 8 * 16)
            ch.inc(dve.tensor_scalar(bg2h, bg2c, 0.5, None, ALU.mult))
            for c in range(CC):
                ch.inc(dve.tensor_scalar(wg1_f[:, c, :], wg1_raw[:, c, :], gcol[:, c:c + 1], None, ALU.mult))
                ch.inc(dve.tensor_scalar(lnbb[:, c, :], ones[:], bcol[:, c:c + 1], None, ALU.mult))
            dve.wait_ge(dve_chain, ch.n)
            assert ch.n == WG1_READY
            dve.wait_ge(setup_pe, 6)
            ch.inc(dve.tensor_copy(g1b[:], bank[5][:, 0:G]))
            dve.wait_ge(setup_act, 3)
            ch.inc(dve.tensor_tensor(rwh[:, LO], rwt[:], halves(rwh[:, HI]), ALU.subtract))
            dve.wait_ge(setup_act, 6)
            ch.inc(dve.tensor_tensor(wkvg[:, LO, :, 0:2 * C], wkv_raw[:], halves(wkvg[:, HI, :, 0:2 * C]), ALU.subtract))
            ch.inc(dve.tensor_tensor(wkvg[:, LO, :, 2 * C:2 * C + G], wg1_f[:],
                                     halves(wkvg[:, HI, :, 2 * C:2 * C + G]), ALU.subtract))
            ch.inc(dve.tensor_tensor(wproj[:, LO], wp_raw[:], halves(wproj[:, HI]), ALU.subtract))
            assert ch.n == MIXW_READY

            def split_lo(n):
                dve.wait_ge(w_hi, n + 1)
                dve.tensor_tensor(wreg[:, LO, n % 4].rearrange("p c r o -> p (c r o)"),
                                  rel_raw[n] if n < 4 else raw[:, n % 2, :],
                                  halves(wreg[:, HI, n % 4].rearrange("p c r o -> p (c r o)")),
                                  ALU.subtract).then_inc(w_lo, 1)

            def layer_norm(k, i, b):
                dve.wait_ge(x_in, 16 * i + 16)
                if not isinstance(i, int) or i > 0:
                    dve.wait_ge(xt_psum, k - 1)
                xk = xres[:, bass.ds(k, 1), :].rearrange("p a c -> p (a c)")
                apart(dve)
                ch.link(dve, dve.bn_stats(stats[:, b, :], xk))
                if not isinstance(i, int) or i > 0:
                    dve.wait_ge(s2_ready, k - 1)
                apart(dve)
                dve.bn_aggr(mv[:, b, :], stats[:, b, :]).then_inc(var_ready, 1)
                dve.wait_ge(rstd_ready, k + 1)
                dve.tensor_scalar(xn[b][:], xk, mv[:, b, 0:1], rstd[:, b:b + 1], ALU.subtract,
                                  ALU.mult).then_inc(xn_ready, 1)

            def table_out(k, j):
                if j % 4 == 1:
                    if not isinstance(k, int) or k > 0:
                        dve.wait_ge(tbl_st[j // 4], 16 * k)
                dve.wait_ge(gnn_mm, 8 * k + j + 1)
                dve.tensor_copy(stage[:, j // 4, (j % 4) * 512:(j % 4 + 1) * 512], bank[3 + j % 4][:]).then_inc(tbl_dve, 1)

            def xt_low(k, b):
                dve.wait_ge(xt_hi, k + 1)
                dve.tensor_tensor(xt[b][:, LO].rearrange("p c n -> p (c n)"), bank[0][:, 0:C],
                                  halves(xt[b][:, HI].rearrange("p c n -> p (c n)")), ALU.subtract).then_inc(xt_lo, 1)

            def tile_dve(k, i, b, rows, nxt):
                dve.wait_ge(hg_mm, k + 1)
                dve.wait_ge(s2_ready, k + 1)
                if not isinstance(k, int) or k > 0:
                    dve.wait_ge(hg_act, k)
                dve.scalar_tensor_tensor(out=hgn[:, 0, :], in0=bank[2][:, 0:G], scalar=s2[:, b:b + 1], in1=g1b[:],
                                         op0=ALU.mult, op1=ALU.add).then_inc(hg_pre, 1)
                if nxt:
                    layer_norm(*nxt)
                table_out(k, 1)
                table_out(k, 3)
                if nxt:
                    xt_low(nxt[0], nxt[2])
                dve.wait_ge(kv_cp, 2 * k + 2)
                if not isinstance(k, int) or k > 0:
                    dve.wait_ge(kmax_up, k)
                dve.tensor_tensor(kmax[0:rows], kmax[0:rows], kvs[b][0:rows, 0:C], ALU.max).then_inc(kmax_up, 1)
                table_out(k, 5)
                table_out(k, 7)

            layer_norm(0, 0, 0)
            split_lo(0)
            xt_low(0, 0)
            for n in range(1, 4):
                split_lo(n)
            dve.wait_ge(w_lo, 4)
            dve.memset(xres[96:P, NT - 1, :], 0.0).then_inc(cleared, 1)
            tile_dve(0, 0, 0, P, (1, 0, 1))
            tile_dve(1, 0, 1, P, (2, 1, 0))
            ch.link(dve, dve.tensor_scalar(mask, dpr[:], 0.0, None, ALU.is_lt))
            ch.link(dve, dve.scalar_tensor_tensor(out=mask, in0=dpr[:], scalar=PAD_DST / 2.0, in1=mask,
                                                  op0=ALU.is_gt, op1=ALU.mult))
            ch.link(dve, dve.scalar_tensor_tensor(out=mask, in0=dpr[:], scalar=WIN - 1.0, in1=mask,
                                                  op0=ALU.is_gt, op1=ALU.add))
            ch.link(dve, dve.tensor_reduce(cnt, mask, AX.X, ALU.add))
            ch.link(dve, dve.tensor_tensor(dsl, dpr[:], lo_i, ALU.add))
            ch.link(dve, dve.scalar_tensor_tensor(out=dsl, in0=dsl, scalar=-float(FAR), in1=mask, op0=ALU.add,
                                                  op1=ALU.mult))
            ch.link(dve, dve.tensor_scalar(dsl, dsl, float(FAR), None, ALU.add))
            assert ch.n == FAR_READY
            base = ch.n
            with dve.Fori(1, NP) as i:
                ch.n = base + 2 * (i - 1)
                tile_dve(2 * i, i, 0, P, (2 * i + 1, i, 1))
                tile_dve(2 * i + 1, i, 1, P, (2 * i + 2, i + 1, 0))
            ch.n = base + 2 * (NP - 1)
            tile_dve(NT - 1, NP, 0, TAIL, None)

            first_phase_over(dve)
            dve.wait_ge(setup_pe, 7)
            dve.tensor_copy(flag[:], bank[0][0:1, C:C + 1]).then_inc(flag_ready, 1)
            ch.link(dve, dve.tensor_reduce(kcol, bank[0][:, 0:C].rearrange("p (c n) -> p c n", c=CC), AX.X, ALU.max))
            for c in range(CC):
                ins = dve.tensor_scalar(dg[:, c * P:(c + 1) * P], ident[:], kcol[:, c:c + 1], None, ALU.mult)
                ins.then_inc(k_shift_diag, 1)
            dve.wait_ge(kmb_mm, 1)
            ch.link(dve, dve.tensor_copy(kmb[:], bank[1][:, 0:C]))
            for n in range(4, 8):
                split_lo(n)

            def shifts(i):
                for s in range(SLOTS):
                    dve.wait_ge(kv_in[s], 16 * i + 16)
                    dve.tensor_tensor(slot[:, s, 0:C], slot[:, s, 0:C], kmb[:], ALU.subtract).then_inc(k_shift, 1)

            with dve.Fori(0, NT // SLOTS) as i:
                shifts(i)

            ch.link(dve, dve.memset(ctxbd[:], 0.0))
            dve.wait_ge(ctx_mm, NT)
            for c in range(CC):
                ch.inc(dve.reciprocal(rden[:, c:c + 1], bank[2 + c][:, P:P + 1]))
            dve.wait_ge(dve_chain, ch.n)
            for c in range(CC):
                for h in range(NB):
                    d = slice(h * HEAD, (h + 1) * HEAD)
                    dve.tensor_scalar(ctxbd[d, c, d], bank[2 + c][d, d], rden[d, c:c + 1], None,
                                      ALU.mult).then_inc(ctx_done, 1)
            dve.wait_ge(setup_act, 8)
            dve.scalar_tensor_tensor(out=wqc[:, LO].rearrange("p c n -> p (c n)"), in0=bank[4][:], scalar=0.5,
                                     in1=halves(wqc[:, HI].rearrange("p c n -> p (c n)")), op0=ALU.mult,
                                     op1=ALU.subtract).then_inc(wqc_done, 1)
            dve.wait_ge(flag_ready, 1)
            far = dve.value_load(flag[0:1, 0:1], min_val=0, max_val=NT * P * R)
            with dve.If(far > 0):
                dve.wait_ge(far_init, 3)
                dve.wait_ge(far_ld, 16 * (NT + 1))
                fch = Tally(dve_chain)
                with dve.Fori(0, ET) as t:
                    fch.n = ch.n + 3 * t
                    dcol = f_dsl[:, bass.ds(t, 1)]
                    dve.wait_ge(far_idx, t + 1)
                    dve.tensor_copy(f_i[:, 1:2], dcol).then_inc(far_dst, 1)
                    dve.tensor_scalar(f_turn, ones[:], dcol, None, ALU.mult).then_inc(far_turn, 1)
                    dve.wait_ge(far_row, t + 1)
                    fch.link(dve, dve.tensor_scalar(f_same, bank[6][:, 0:P], dcol, None, ALU.is_equal))
                    fch.link(dve, dve.tensor_tensor(f_turn, f_same, f_low, ALU.mult))
                    fch.link(dve, dve.tensor_reduce(f_dup, f_turn, AX.X, ALU.add))
                    dve.scalar_tensor_tensor(out=f_i[:, 2:3], in0=f_dup, scalar=float(FAR), in1=dcol,
                                             op0=ALU.mult, op1=ALU.add).then_inc(far_uniq, 1)
                    dve.wait_ge(far_in, 32 * t + 32)
                    dve.tensor_scalar(stg[:, 3, :], stg[:, 0, :], nrm[:, bass.ds(t, 1)], None,
                                      ALU.mult).then_inc(far_msg, 1)
                    dve.wait_ge(far_mm, t + 1)
                    dve.wait_ge(far_uniq, t + 1)
                    dve.tensor_tensor(stg[:, 2, :], bank[7][:, 0:C], stg[:, 1, :], ALU.add).then_inc(far_sum, 1)
                with dve.Fori(0, NT) as k:
                    dve.wait_ge(far_ld, 16 * k + 16 * (NT + 2))
                    xk = xres[:, bass.ds(k, 1), :]
                    dve.tensor_tensor(xk, xk, stg[:, 3:4, :], ALU.add).then_inc(far_x, 1)
            with dve.Else():
                dve.sem_inc(dve_chain, 3 * ET)
            ch.n = ch.n + 3 * ET

            def SELECT(i, s, groups):
                if s >= groups:
                    return
                S = 8 * i + s
                if s >= 2 or not isinstance(i, int) or i > 0:
                    dve.wait_ge(edge_mm, S - 1)
                dve.tensor_tensor(sel[:, (s % 2) * CUT:(s % 2 + 1) * CUT, :],
                                  edge_window(s // 2 % 2).unsqueeze(1).to_broadcast([P, CUT, P]),
                                  dpr[:, bass.ds(SUP * S, CUT)].unsqueeze(2).to_broadcast([P, CUT, P]),
                                  ALU.is_equal).then_inc(sel_done, 1)
                for j in range(CUT, SUP):
                    dve.tensor_scalar(sel_norm[:, (s % 2) * (SUP - CUT) + j - CUT, :], edge_window(s // 2 % 2),
                                      dpr[:, bass.ds(SUP * S + j, 1)], nrm[:, bass.ds(SUP * S + j, 1)],
                                      ALU.is_equal, ALU.mult).then_inc(sel_done, 1)

            def MSGS(i, s, groups):
                if s >= groups:
                    return
                S = 8 * i + s
                for j in range(CUT):
                    m = (s % 2) * CUT + j
                    dve.wait_ge(msg_hi, CUT * S + j + 1)
                    dve.scalar_tensor_tensor(out=ml[:, m, :], in0=stg[:, (s % 4) * SUP + j, :],
                                             scalar=nrm[:, bass.ds(SUP * S + j, 1)], in1=halves(mh[:, m, :]),
                                             op0=ALU.mult, op1=ALU.subtract).then_inc(msg_lo, 1)

            def adds(i, u):
                dve.wait_ge(edge_mm, 8 * i + min(2 * u + 2, TAIL_GROUPS if isinstance(i, int) and i == NP else 8))
                if not (isinstance(i, int) and i == 0 and u == 0):
                    dve.wait_ge(edge_add, adds_before(i, u))
                for a, b, t in window_parts(u % 2):
                    if isinstance(i, int) and not 0 <= 2 * i + u // 2 + t < NT:
                        continue
                    xk = xres[a:b, bass.ds(2 * i + u // 2 + t, 1), :].rearrange("p a c -> p (a c)")
                    dve.tensor_tensor(xk, bank[u % 2][a:b, 0:C], xk, ALU.add).then_inc(edge_add, 1)

            def WINDOW(i, s, groups):
                if s == 0 and not (isinstance(i, int) and i == 0):
                    adds(i - 1, 3)
                elif 0 < s <= groups:
                    adds(i, (s - 1) // 2)

            def LAST_WINDOW(i, s, groups):
                if groups == s:
                    WINDOW(i, s, groups)

            def cols2(t, n):
                return t.rearrange("p (c n) -> p c n", c=CC)[:, :, 0:n]

            def GATE(p, nt):
                n = nt * P
                dve.wait_ge(gate_act, 2 * p + 2)
                dve.wait_ge(out_mm, p + 1)
                dve.scalar_tensor_tensor(out=cols2(ogf, n), in0=cols2(gate, n), scalar=1.0,
                                         in1=cols2(bank[4][:], n), op0=ALU.add, op1=ALU.mult).then_inc(og_dve, 1)

            def GATE_LOW(p, nt):
                dve.wait_ge(og_hi, p + 1)
                dve.tensor_tensor(og[:, LO, :, 0:nt * P], cols2(ogf, nt * P),
                                  halves(og[:, HI, :, 0:nt * P]), ALU.subtract).then_inc(og_lo, 1)

            def STATS(p, nt):
                xp = xres[:, bass.ds(2 * p, nt), :]
                dve.wait_ge(proj_mm, p + 1)
                dve.wait_ge(edge_add, ALL_ADDS if isinstance(p, int) and p == NP else adds_before(p + 1, 1))
                ch.link(dve, dve.tensor_tensor(xp, bank[4][:].rearrange("p (a c) -> p a c", a=2)[:, 0:nt], xp, ALU.add))
                apart(dve)
                for a in range(nt):
                    ch.inc(dve.bn_stats(stats[:, a, :], xres[:, bass.ds(2 * p + a, 1), :].rearrange("p a c -> p (a c)")))
                dve.wait_ge(dve_chain, ch.n)
                apart(dve)
                for a in range(nt):
                    dve.bn_aggr(mv[:, a, :], stats[:, a, :]).then_inc(var2_ready, 1)

            def SHIFT(p, nt):
                dve.wait_ge(rstd2_ready, p + 1)
                dve.scalar_tensor_tensor(out=nmr[:, 0:nt], in0=mv[:, 0:nt, 0], scalar=-1.0, in1=rstd[:, 0:nt],
                                         op0=ALU.mult, op1=ALU.mult).then_inc(shift_dve, 1)
                dve.tensor_scalar(rst1[:, 0:nt], rstd[:, 0:nt], 1.0, None, ALU.add).then_inc(shift_dve, 1)

            def TURN_LOW(p, nt):
                dve.wait_ge(tt_hi, p + 1)
                dve.tensor_tensor(tt[:, LO, :, 0:nt * P], cols2(bank[5][:], nt * P),
                                  halves(tt[:, HI, :, 0:nt * P]), ALU.subtract).then_inc(tt_lo, 1)

            def TOP(p, nt):
                dve.wait_ge(logit_mm, p + 1)
                ch.link(dve, dve.tensor_copy(lg[:, 0:nt], bank[5][:, 0:nt * X].rearrange("p (a e) -> p a e", a=nt)))
                apart(dve)
                for a in range(nt):
                    ch.inc(dve.max(top[:, a, :], lg[:, a, :]))
                dve.wait_ge(dve_chain, ch.n)
                apart(dve)
                dve.tensor_tensor(dlt[:, 0:nt], top[:, 0:nt, 0], top[:, 0:nt, 1], ALU.subtract).then_inc(gap_dve, 1)
                for a in range(nt):
                    ch.inc(dve.max_index(smallu[:, a, :], top[:, a, :], lg[:, a, :]))

            def COMB(p, nt):
                dve.wait_ge(dve_chain, ch.n)
                ch.inc(dve.tensor_copy(idf[:, 0:nt], smallu[:, 0:nt]))
                dve.wait_ge(gap_act, p + 1)
                ch.inc(dve.tensor_scalar(wa[:, 0:nt], th[:, 0:nt], 0.5, 0.5, ALU.mult, ALU.add))
                ch.inc(dve.tensor_scalar(wb[:, 0:nt], th[:, 0:nt], -0.5, 0.5, ALU.mult, ALU.add))
                dve.wait_ge(dve_chain, ch.n)
                for a in range(nt):
                    ch.inc(dve.tensor_scalar(cb2[:, a, :], iota8[:], idf[:, a, 0:1], wa[:, a:a + 1], ALU.is_equal, ALU.mult))
                    ch.inc(dve.tensor_scalar(lg[:, a, :], iota8[:], idf[:, a, 1:2], wb[:, a:a + 1], ALU.is_equal, ALU.mult))
                dve.wait_ge(dve_chain, ch.n)
                dve.wait_ge(y_add, 2 * X * p + AHEAD)
                dve.tensor_tensor(comb[:, 0:nt], cb2[:, 0:nt], lg[:, 0:nt], ALU.add).then_inc(comb_dve, 1)

            def BIAS2_ADD(p, nt):
                dve.wait_ge(b2_mm, p + 1)
                dve.wait_ge(y_add, 2 * X * p + nt * 6 + AHEAD)
                xp = xres[:, bass.ds(2 * p, nt), :]
                dve.tensor_tensor(xp, bank[4][:].rearrange("p (a c) -> p a c", a=2)[:, 0:nt], xp,
                                  ALU.add).then_inc(b2_add, 1)

            def LOW(p, nt, e):
                n = nt * P
                dve.wait_ge(h_hi, X * p + e + 1)
                dve.tensor_tensor(ht[e % 2][:, LO, :, 0:n], cols2(hf[e % 2], n),
                                  halves(ht[e % 2][:, HI, :, 0:n]), ALU.subtract).then_inc(h_lo, 1)

            def ADD(p, nt, e):
                dve.wait_ge(y_mm, X * p + e + 1 + BEGUN)
                if e == 0:
                    dve.wait_ge(acc_act, 2 * p + nt)
                    dve.wait_ge(comb_dve, p + 1)
                elif e == 6:
                    dve.wait_ge(b2_add, p + 1)
                else:
                    dve.wait_ge(y_add, 2 * X * p + nt * e + AHEAD)
                for a in range(nt):
                    xk = xres[:, bass.ds(2 * p + a, 1), :].rearrange("p a c -> p (a c)")
                    dve.scalar_tensor_tensor(out=xk, in0=bank[6 + e % 2][:, a * C:(a + 1) * C],
                                             scalar=comb[:, a, e:e + 1], in1=xk, op0=ALU.mult,
                                             op1=ALU.add).then_inc(y_add, 1)

            def slot_of(i, s, groups, p1, n1, p2, n2):
                if not isinstance(i, int) and s == 0:
                    ch.n = ch.base + CHAIN2 * (i - 2)
                in_slot(i, s, groups, p1, n1, p2, n2, SELECT=SELECT, MSGS=MSGS, WINDOW=WINDOW, LAST_WINDOW=LAST_WINDOW, GATE=GATE,
                        GATE_LOW=GATE_LOW, STATS=STATS, SHIFT=SHIFT, TURN_LOW=TURN_LOW, TOP=TOP, COMB=COMB,
                        BIAS2_ADD=BIAS2_ADD, LOW=LOW, ADD=ADD)

            def before_loop():
                ch.base = ch.n

            def after_loop():
                ch.n = ch.base + CHAIN2 * (NP - 2)

            run(dve, slot_of, NP, TAIL_GROUPS, before_loop, after_loop)

        @block.tensor
        def _(pe):
            pe.wait_ge(consts, 8)
            for a, (rows, at, need) in enumerate(((erow[:, 0, :], 0, 1), (erow[:, 1, :], 2, 2), (norm_r, 4, 2))):
                pe.wait_ge(dve_chain, need)
                for j in range(EB):
                    mm = pe.transpose(bank[at + j // 4][:, (j % 4) * ER:(j % 4 + 1) * ER],
                                      rows[:, j * P:(j + 1) * P], ident[0:ER, 0:ER])
                mm.then_inc(setup_pe, 1)
            pe.wait_ge(mixw_in, 64)
            for c in range(CC):
                for d in range(CC):
                    mm = pe.transpose(bank[6][:, c * C + d * P:c * C + (d + 1) * P],
                                      wq_raw[:, d, c * P:(c + 1) * P], ident[:])
            mm.then_inc(setup_pe, 1)
            pe.wait_ge(vec_in, 8 * 16)
            pe.transpose(bank[7][:, 0:22], vrow[0:22, :], ident[0:22, 0:22])
            for c in range(CC):
                mm = pe.transpose(bank[7][:, 32 + c * X:32 + (c + 1) * X], rwr[:, c * P:(c + 1) * P], ident[0:X, 0:X])
            mm.then_inc(setup_pe, 1)
            pe.wait_ge(dve_chain, WG1_READY)
            pe.wait_ge(setup_act, 2)
            for c in range(CC):
                pe.matmul(bank[5][:, 0:G], lnbb[:, c, :], wg1_raw[:, c, :], start=(c == 0), stop=False)
            pe.matmul(bank[5][:, 0:G], ones[0:1, :], bg1r, start=False, stop=True).then_inc(setup_pe, 1)

            def three(dst, stat, mov, k0=0, chunks=CC):
                n = 0
                for c in range(chunks):
                    for a, b in PASSES:
                        mm = pe.matmul(dst, stat(a, c), mov(b, c), start=(n == 0), stop=(n == 3 * chunks - 1))
                        n += 1
                return mm

            def turn(k, b):
                pe.wait_ge(xn_ready, k + 1)
                if not isinstance(k, int) or k > 0:
                    pe.wait_ge(xt_lo, k)
                for c in range(CC):
                    mm = pe.transpose(bank[0][:, c * P:(c + 1) * P], xn[b][:, c * P:(c + 1) * P], ident[:])
                mm.then_inc(xt_psum, 1)

            def relations(k, b, j):
                if j % 2 == 0:
                    if j >= 4 or not isinstance(k, int) or k > 0:
                        pe.wait_ge(tbl_act, 4 * k + j // 2 - 1)
                else:
                    if j >= 4 or not isinstance(k, int) or k > 0:
                        pe.wait_ge(tbl_dve, 4 * k + (j - 3) // 2)
                if isinstance(k, int) and k == 0:
                    pe.wait_ge(w_lo, j // 2 + 1)
                w = 2 * (j % 2)
                three(bank[3 + j % 4][:], lambda a, c: xt[b][:, a, c, :],
                      lambda h, c: wreg[:, h, j // 2, c, w:w + 2, :].rearrange("p r o -> p (r o)")).then_inc(gnn_mm, 1)

            def tile_pe(k, i, b, nxt):
                pe.wait_ge(xt_lo, k + 1)
                if not isinstance(k, int) or k > 0:
                    pe.wait_ge(kv_cp, 2 * k)
                three(bank[1][:], lambda a, c: xt[b][:, a, c, :], lambda h, c: wkvg[:, h, c, 0:2 * C]).then_inc(kv_mm, 1)
                if not isinstance(k, int) or k > 0:
                    pe.wait_ge(hg_pre, k)
                three(bank[2][:, 0:G], lambda a, c: xt[b][:, a, c, :],
                      lambda h, c: wkvg[:, h, c, 2 * C:2 * C + G]).then_inc(hg_mm, 1)
                for j in range(4):
                    relations(k, b, j)
                if nxt:
                    turn(*nxt)
                pe.wait_ge(hg_act, k + 1)
                if not isinstance(k, int) or k > 0:
                    pe.wait_ge(hgt_cp, k)
                apart(pe)
                pe.transpose(bank[7][0:G, 0:P], hgn[:, 1, :], ident[:]).then_inc(hgt_psum, 1)
                for j in range(4, 8):
                    relations(k, b, j)

            turn(0, 0)
            pe.wait_ge(dve_chain, MIXW_READY)
            tile_pe(0, 0, 0, (1, 1))
            tile_pe(1, 0, 1, (2, 0))
            with pe.Fori(1, NP) as i:
                tile_pe(2 * i, i, 0, (2 * i + 1, 1))
                tile_pe(2 * i + 1, i, 1, (2 * i + 2, 0))
            tile_pe(NT - 1, NP, 0, None)

            pe.wait_ge(kmax_up, NT)
            pe.matmul(bank[0][0:1, C:C + 1], cnt, ones[:, 0:1], start=True, stop=True)
            for c in range(CC):
                mm = pe.transpose(bank[0][:, c * P:(c + 1) * P], kmax[:, c * P:(c + 1) * P], ident[:])
            mm.then_inc(setup_pe, 1)
            pe.wait_ge(k_shift_diag, 2)
            pe.matmul(bank[1][:, 0:C], ones[:], dg[:], start=True, stop=True).then_inc(kmb_mm, 1)

            def contexts(i, first, last):
                for s in range(SLOTS):
                    pe.wait_ge(k_exp, SLOTS * i + s + 1)
                    rows = TAIL if last and s == SLOTS - 1 else P
                    for c in range(CC):
                        mm = pe.matmul(bank[2 + c][:, 0:VW], slot[0:rows, s, c * P:(c + 1) * P],
                                       slot[0:rows, s, C + c * VW:C + (c + 1) * VW],
                                       start=(first and s == 0), stop=(last and s == SLOTS - 1))
                    mm.then_inc(ctx_mm, 1)

            contexts(0, True, False)
            with pe.Fori(1, NT // SLOTS - 1) as i:
                contexts(i, False, False)
            contexts(NT // SLOTS - 1, False, True)
            pe.wait_ge(ctx_done, CC * NB)
            for d in range(CC):
                for c in range(CC):
                    mm = pe.matmul(bank[4][:, d * C + c * P:d * C + (c + 1) * P], wqt[:, c, d * P:(d + 1) * P],
                                   ctxbd[:, c, :], start=True, stop=True)
            mm.then_inc(setup_pe, 1)

            def SUMS(i, s, groups):
                if s >= groups:
                    return
                S = 8 * i + s
                u = s // 2
                if s % 2 == 0 and (u >= 2 or not isinstance(i, int) or i > 0):
                    pe.wait_ge(edge_add, adds_before(i, u - 1) if u else adds_before(i - 1, 3))
                pe.wait_ge(sel_done, (SUP - CUT + 1) * (S + 1))
                pe.wait_ge(gath[s % 4], 64 * (2 * i + s // 4 + 1))
                for j in range(CUT, SUP):
                    pe.matmul(bank[u % 2][:, 0:C], sel_norm[:, (s % 2) * (SUP - CUT) + j - CUT, :],
                              stg[:, (s % 4) * SUP + j, :], start=(s % 2 == 0 and j == CUT), stop=False)
                for j in range(CUT):
                    m = (s % 2) * CUT + j
                    pe.wait_ge(msg_lo, CUT * S + j + 1)
                    pe.matmul(bank[u % 2][:, 0:C], sel[:, m, :], mh[:, m, :], start=False, stop=False)
                    mm = pe.matmul(bank[u % 2][:, 0:C], sel[:, m, :], ml[:, m, :], start=False,
                                   stop=(j == CUT - 1 and (s % 2 == 1 or s == groups - 1)))
                mm.then_inc(edge_mm, 1)

            def OUT(p, nt):
                n = nt * P
                pe.wait_ge(xtp_in, 32 * p + 32)
                for v in range(CC):
                    mm = three(bank[4][:, v * 256:v * 256 + n], lambda a, c: wqc[:, a, c, v * P:(v + 1) * P],
                               lambda h, c: xtp[:, 0:nt, h * C + c * P:h * C + (c + 1) * P])
                mm.then_inc(out_mm, 1)

            def GATES(p, nt):
                n = nt * P
                if not isinstance(p, int) or p > 0:
                    pe.wait_ge(gap_dve, p)
                for v in range(CC):
                    mm = pe.matmul(bank[5][:, v * 256:v * 256 + n], wg2[:, v * P:(v + 1) * P],
                                   hgp[:, 0:nt, :].rearrange("p a n -> p (a n)"), start=True, stop=True)
                mm.then_inc(gate_mm, 1)

            def PROJ(p, nt):
                pe.wait_ge(og_lo, p + 1)
                for a in range(nt):
                    mm = three(bank[4][:, a * C:(a + 1) * C], lambda h, c: og[:, h, c, a * P:(a + 1) * P],
                               lambda h, c: wproj[:, h, c, :])
                mm.then_inc(proj_mm, 1)

            def TURN(p, nt):
                pe.wait_ge(tn_act, 2 * p + nt)
                for a in range(nt):
                    for c in range(CC):
                        mm = pe.transpose(bank[5][:, c * 256 + a * P:c * 256 + (a + 1) * P],
                                          tn[:, a, c * P:(c + 1) * P], ident[:])
                mm.then_inc(tt_mm, 1)

            def LOGIT(p, nt):
                pe.wait_ge(tt_lo, p + 1)
                for a in range(nt):
                    mm = three(bank[5][:, a * X:(a + 1) * X], lambda h, c: tt[:, h, c, a * P:(a + 1) * P],
                               lambda h, c: rwh[:, h, c, :])
                mm.then_inc(logit_mm, 1)

            def COMBT(p, nt):
                pe.wait_ge(comb_dve, p + 1)
                if not isinstance(p, int) or p < NP:
                    pe.wait_ge(gate_act, 2 * p + 4)
                for a in range(nt):
                    mm = pe.transpose(bank[5][0:X, a * P:(a + 1) * P], comb[:, a, :], ident[:])
                mm.then_inc(ct_mm, 1)

            def BIAS2(p, nt):
                pe.wait_ge(ct_act, p + 1)
                if not isinstance(p, int) or p < NP:
                    pe.wait_ge(var2_ready, 2 * (p + 1) + (1 if isinstance(p, int) and p == NP - 1 else 2))
                for a in range(nt):
                    mm = pe.matmul(bank[4][:, a * C:(a + 1) * C], ct[:, a * P:(a + 1) * P], b2s[:],
                                   start=True, stop=True)
                mm.then_inc(b2_mm, 1)

            def LAYER1(p, nt, e):
                n = nt * P
                if e == 0:
                    pe.wait_ge(tt_lo, p + 1)
                if e >= 2 or not isinstance(p, int) or p > 0:
                    pe.wait_ge(h_act, 2 * (X * p + e) - 2 + 2 * BEGUN)
                for v in range(CC):
                    mm = three(bank[2 + e % 2][:, v * 256:v * 256 + n],
                               lambda a, c: wreg[:, a, e // WC, c, e % WC, v * P:(v + 1) * P],
                               lambda h, c: tt[:, h, c, 0:n])
                mm.then_inc(h_mm, 1)

            def LAYER2(p, nt, e):
                pe.wait_ge(h_lo, X * p + e + 1 + BEGUN)
                pe.wait_ge(y_add, 2 * X * p + (nt * (e - 1) if e else -2) + AHEAD)
                for a in range(nt):
                    mm = three(bank[6 + e % 2][:, a * C:(a + 1) * C], lambda h, c: ht[e % 2][:, h, c, a * P:(a + 1) * P],
                               lambda h, c: wreg[:, h, 2 + e // WC, c, e % WC, :])
                mm.then_inc(y_mm, 1)

            def slot_of(i, s, groups, p1, n1, p2, n2):
                in_slot(i, s, groups, p1, n1, p2, n2, SUMS=SUMS, OUT=OUT, GATES=GATES, PROJ=PROJ, TURN=TURN,
                        LOGIT=LOGIT, COMBT=COMBT, BIAS2=BIAS2, LAYER1=LAYER1, LAYER2=LAYER2)

            pe.wait_ge(flag_ready, 1)
            far = pe.value_load(flag[0:1, 0:1], min_val=0, max_val=NT * P * R)
            with pe.If(far > 0):
                with pe.Fori(0, ET) as t:
                    pe.wait_ge(far_turn, t + 1)
                    pe.transpose(bank[6][:, 0:P], f_turn, ident[:]).then_inc(far_row, 1)
                    pe.wait_ge(far_msg, t + 1)
                    pe.matmul(bank[7][:, 0:C], f_same, stg[:, 3, :], start=True, stop=True).then_inc(far_mm, 1)

            pe.wait_ge(wqc_done, 1)
            run(pe, slot_of, NP, TAIL_GROUPS)


EDGES_IN = 6
VECTORS_IN = EDGES_IN + 2
WG1_READY = VECTORS_IN + 5
MIXW_READY = WG1_READY + 5
FAR_READY = MIXW_READY + 3 + 7
CHAIN2 = 15


SLOTS_OF_PAIR = (
    ("-WEIGHT", "*SELECT", "-LOW 1", "*MSGS", "*WINDOW", "-COMB", "-LAYER1 2", "-LAYER2 0", "+OUT", "+GATES",
     "*SUMS"),
    ("*SELECT", "-ADD 0", "-LOW 2", "+GATE_ACT", "*MSGS", "+GATE", "-LAYER1 3", "-LAYER2 1", "+GATE_HI", "*SUMS"),
    ("-ADD 1", "*SELECT", "-LOW 3", "*MSGS", "+GATE_LOW", "*WINDOW", "-LAYER1 4", "-LAYER2 2", "-COMBT",
     "*SUMS"),
    ("-ADD 2", "*SELECT", "-LOW 4", "-COMBT_ACT", "*MSGS", "+PROJ", "+STATS", "-LAYER1 5", "-LAYER2 3", "*SUMS"),
    ("-ADD 3", "*SELECT", "-LOW 5", "*MSGS", "+SHIFT", "*WINDOW", "-LAYER1 6", "+NORM", "-LAYER2 4",
     "*SUMS"),
    ("-ADD 4", "*SELECT", "-LOW 6", "*MSGS", "*LAST_WINDOW", "-LAYER1 7", "+TURN",  "+TURN_HI", "-LAYER2 5", "-BIAS2",
     "*SUMS"),
    ("+TURN_LOW", "-ADD 5", "*SELECT", "-LOW 7", "*MSGS", "-BIAS2_ADD", "*WINDOW", "-LAYER2 6", "+LAYER1 0", "+LOGIT", "*SUMS"),
    ("-ADD 6", "*SELECT", "+LOW 0", "*MSGS", "+TOP", "-LAYER2 7", "+LAYER1 1", "-ADD 7", "*SUMS"),
)


def in_slot(i, s, groups, p1, n1, p2, n2, **steps):
    for entry in SLOTS_OF_PAIR[s]:
        name, *expert = entry[1:].split()
        if name not in steps:
            continue
        if entry[0] == "*":
            if groups:
                steps[name](i, s, groups)
        else:
            p, nt = (p1, n1) if entry[0] == "+" else (p2, n2)
            if nt:
                steps[name](p, nt, *map(int, expert))


def run(eng, slot_of, pairs, tail_groups, before_loop=None, after_loop=None):
    for s in range(8):
        slot_of(0, s, 8, None, 0, None, 0)
    for s in range(8):
        slot_of(1, s, 8, 0, 2, None, 0)
    if before_loop:
        before_loop()
    with eng.Fori(2, pairs) as i:
        for s in range(8):
            slot_of(i, s, 8, i - 1, 2, i - 2, 2)
    if after_loop:
        after_loop()
    for s in range(8):
        slot_of(pairs, s, tail_groups, pairs - 1, 2, pairs - 2, 2)
    for s in range(8):
        slot_of(pairs + 1, s, 0, pairs, 1, pairs - 1, 2)
    for s in range(8):
        slot_of(pairs + 2, s, 0, None, 0, pairs, 1)


_INS = ['x', 'src', 'dst', 'edge_type_16', 'edge_weight1', 'L0_gnn_weight', 'L0_mix_Wqkv', 'L0_mix_Wproj',
        'L0_mix_bproj', 'L0_mix_ln_g', 'L0_mix_ln_b', 'L0_mix_Wg1', 'L0_mix_bg1', 'L0_mix_Wg2', 'L0_mix_bg2',
        'L0_ffn_router_w', 'L0_ffn_w1', 'L0_ffn_b1', 'L0_ffn_w2', 'L0_ffn_b2']


def kernel(**inputs):
    import numpy as _np
    import concourse.bacc as _bacc
    from concourse import mybir as _mybir
    from concourse.bass_utils import run_bass_kernel_spmd as _run

    nc = _bacc.Bacc("TRN2", target_bir_lowering=False, num_devices=1, dynamic_dma_scratch_size=8192)
    arrays, args = {}, []
    for name in _INS:
        a = _np.ascontiguousarray(inputs[name])
        arrays[f"in_{name}"] = a
        args.append(nc.dram_tensor(f"in_{name}", a.shape, _mybir.dt.from_np(a.dtype), kind="ExternalInput").ap())
    args.append(nc.dram_tensor("out_x", inputs["x"].shape, _mybir.dt.float32, kind="ExternalOutput").ap())
    gps_layer(nc, *args)
    r = _run(nc, [arrays], core_ids=[0])
    return r.results[0]["out_x"]
```
